# Optimizing a Trainium2 kernel written in Bass

```python
import numpy as np
import jax
import jax.numpy as jnp

def _softmax(x, axis=-1):
    return jax.nn.softmax(x, axis=axis)

def _gelu(x):
    return jax.nn.gelu(x, approximate=True)

def _silu(x):
    return jax.nn.silu(x)

def _sigmoid(x):
    return jax.nn.sigmoid(x)

def _layernorm(x, axis=-1, eps=1e-05):
    m = jnp.mean(x, axis=axis, keepdims=True)
    v = jnp.var(x, axis=axis, keepdims=True)
    return (x - m) / jnp.sqrt(v + eps)

def _scatter_add(tgt, idx, src, axis=0):
    return tgt.at[idx].add(src)

def _segment_sum(src, seg, n):
    return jax.ops.segment_sum(src, seg, n)
kernel_name = 'mk_vit_tower_d1_tok_img1024_r4_4554fd'

def setup_inputs(seed: int=0):
    np.random.seed(seed)
    _w = jnp.asarray

    def _rec_inputs():
        import jax
        import jax.numpy as jnp
        _rk = jax.random.key(seed)
        x = -0.00011082 + 0.999858 * jax.random.normal(jax.random.fold_in(_rk, 1), (16, 5, 128, 128), jnp.float32)
        return x
    x = _rec_inputs()

    def _L0_tok_setup():
        import jax, jax.numpy as jnp
        import numpy as np
        PATCH = 8
        EPS = 1e-05

        def _patchify(x):
            B, C, H, Wd = x.shape
            p = PATCH
            x = x.reshape(B, C, H // p, p, Wd // p, p)
            x = x.transpose(0, 2, 4, 1, 3, 5)
            return x.reshape(B, H // p * (Wd // p), C * p * p)
        key = jax.random.key(seed)
        k1, k2 = jax.random.split(key)
        B, C, H, W_ = (32, 5, 128, 128)
        in_feat, embed_dim = (C * PATCH * PATCH, 256)
        x = jax.random.normal(k1, (B, C, H, W_), dtype=jnp.float32)
        W = jax.random.normal(k2, (in_feat, embed_dim), dtype=jnp.float32) * (1.0 / np.sqrt(in_feat))
        gamma = jnp.ones((embed_dim,), dtype=jnp.float32)
        return {'x': x, 'W': W, 'gamma': gamma}
    _L0_tok_all = _L0_tok_setup()
    _L0_tok_in = {k: v for k, v in _L0_tok_all.items() if k in ('W', 'gamma')}
    del _L0_tok_all

    def _L0_attn_setup():
        import jax, jax.numpy as jnp
        import numpy as np
        B, S, D_MODEL = (2, 512, 256)
        H, D = (16, 64)
        D_INNER = H * D
        EPS = 1e-05
        key = jax.random.key(seed)
        ks = jax.random.split(key, 10)
        sc = 0.02
        return {'x': jax.random.normal(ks[0], (B, S, D_MODEL), dtype=jnp.float32), 'Wq': jax.random.normal(ks[1], (D_MODEL, D_INNER), dtype=jnp.float32) * sc, 'Wk': jax.random.normal(ks[2], (D_MODEL, D_INNER), dtype=jnp.float32) * sc, 'Wv': jax.random.normal(ks[3], (D_MODEL, D_INNER), dtype=jnp.float32) * sc, 'Wg': jax.random.normal(ks[4], (D_MODEL, D_INNER), dtype=jnp.float32) * sc, 'Wa': jax.random.normal(ks[5], (D_MODEL, H), dtype=jnp.float32) * sc, 'ba': jax.random.normal(ks[6], (H,), dtype=jnp.float32) * sc, 'Wo': jax.random.normal(ks[7], (D_INNER, D_MODEL), dtype=jnp.float32) * sc, 'gn_w': jnp.ones((D_INNER,), dtype=jnp.float32), 'gn_b': jnp.zeros((D_INNER,), dtype=jnp.float32)}
    _L0_attn_all = _L0_attn_setup()
    _L0_attn_in = {k: v for k, v in _L0_attn_all.items() if k in ('Wq', 'Wk', 'Wv', 'Wg', 'Wa', 'ba', 'Wo', 'gn_w', 'gn_b')}
    del _L0_attn_all

    def _L0_ffn_setup():
        import jax, jax.numpy as jnp
        import numpy as np
        EMBED_DIM = 256
        HIDDEN_DIM = 1024
        NUM_EXPERTS = 8
        TOP_K = 2
        key = jax.random.key(seed)
        ks = jax.random.split(key, 4)
        std1 = float(np.sqrt(2.0 / EMBED_DIM))
        std2 = float(np.sqrt(2.0 / HIDDEN_DIM))
        x = jax.random.normal(ks[0], (1, 512, EMBED_DIM), dtype=jnp.float32)
        w_router = jax.random.normal(ks[1], (EMBED_DIM, NUM_EXPERTS), dtype=jnp.float32) * 0.02
        w1 = jax.random.normal(ks[2], (NUM_EXPERTS, EMBED_DIM, HIDDEN_DIM), dtype=jnp.float32) * std1
        b1 = jnp.zeros((NUM_EXPERTS, HIDDEN_DIM), dtype=jnp.float32)
        w2 = jax.random.normal(ks[3], (NUM_EXPERTS, HIDDEN_DIM, EMBED_DIM), dtype=jnp.float32) * std2
        b2 = jnp.zeros((NUM_EXPERTS, EMBED_DIM), dtype=jnp.float32)
        return {'x': x, 'w_router': w_router, 'w1': w1, 'b1': b1, 'w2': w2, 'b2': b2}
    _L0_ffn_all = _L0_ffn_setup()
    _L0_ffn_in = {k: v for k, v in _L0_ffn_all.items() if k in ('w_router', 'w1', 'b1', 'w2', 'b2')}
    del _L0_ffn_all
    return {'x': x, 'L0_tok_W': _L0_tok_in['W'], 'L0_tok_gamma': _L0_tok_in['gamma'], 'L0_attn_Wq': _L0_attn_in['Wq'], 'L0_attn_Wk': _L0_attn_in['Wk'], 'L0_attn_Wv': _L0_attn_in['Wv'], 'L0_attn_Wg': _L0_attn_in['Wg'], 'L0_attn_Wa': _L0_attn_in['Wa'], 'L0_attn_ba': _L0_attn_in['ba'], 'L0_attn_Wo': _L0_attn_in['Wo'], 'L0_attn_gn_w': _L0_attn_in['gn_w'], 'L0_attn_gn_b': _L0_attn_in['gn_b'], 'L0_ffn_w_router': _L0_ffn_in['w_router'], 'L0_ffn_w1': _L0_ffn_in['w1'], 'L0_ffn_b1': _L0_ffn_in['b1'], 'L0_ffn_w2': _L0_ffn_in['w2'], 'L0_ffn_b2': _L0_ffn_in['b2']}

def reference(x, L0_tok_W, L0_tok_gamma, L0_attn_Wq, L0_attn_Wk, L0_attn_Wv, L0_attn_Wg, L0_attn_Wa, L0_attn_ba, L0_attn_Wo, L0_attn_gn_w, L0_attn_gn_b, L0_ffn_w_router, L0_ffn_w1, L0_ffn_b1, L0_ffn_w2, L0_ffn_b2):
    import jax
    import jax.numpy as jnp

    def _L0_tok_ref(x, W, gamma):
        import jax, jax.numpy as jnp
        import numpy as np
        PATCH = 8
        EPS = 1e-05

        def _patchify(x):
            B, C, H, Wd = x.shape
            p = PATCH
            x = x.reshape(B, C, H // p, p, Wd // p, p)
            x = x.transpose(0, 2, 4, 1, 3, 5)
            return x.reshape(B, H // p * (Wd // p), C * p * p)
        tokens = _patchify(x)
        h = jnp.einsum('bnf,fd->bnd', tokens, W)
        mu = jnp.mean(h, axis=-1, keepdims=True)
        var = jnp.mean(jnp.square(h - mu), axis=-1, keepdims=True)
        out = (h - mu) * jax.lax.rsqrt(var + EPS) * gamma
        return out

    def _L0_attn_ref(x, Wq, Wk, Wv, Wg, Wa, ba, Wo, gn_w, gn_b):
        import jax, jax.numpy as jnp
        import numpy as np
        B, S, D_MODEL = (2, 512, 256)
        H, D = (16, 64)
        D_INNER = H * D
        EPS = 1e-05
        b, s, _ = x.shape
        q = jax.nn.silu(jnp.einsum('bsm,md->bsd', x, Wq).reshape(b, s, H, D).transpose(0, 2, 1, 3))
        k = jax.nn.silu(jnp.einsum('bsm,md->bsd', x, Wk).reshape(b, s, H, D).transpose(0, 2, 1, 3))
        v = jnp.einsum('bsm,md->bsd', x, Wv).reshape(b, s, H, D).transpose(0, 2, 1, 3)
        log_alpha = -jax.nn.softplus(jnp.einsum('bsm,mh->bsh', x, Wa) + ba)
        cum = jnp.cumsum(log_alpha, axis=1).transpose(0, 2, 1)
        diff = cum[:, :, :, None] - cum[:, :, None, :]
        causal = jnp.tril(jnp.ones((s, s), dtype=bool))
        decay = jnp.exp(jnp.where(causal, diff, -jnp.inf))
        attn = jnp.einsum('bhid,bhjd->bhij', q, k) * decay
        o = jnp.einsum('bhij,bhjd->bhid', attn, v)
        o = o.transpose(0, 2, 1, 3)
        mean = jnp.mean(o, axis=(1, 3), keepdims=True)
        var = jnp.var(o, axis=(1, 3), keepdims=True)
        o = (o - mean) / jnp.sqrt(var + EPS)
        o = o * gn_w.reshape(H, D) + gn_b.reshape(H, D)
        o = o.reshape(b, s, H * D)
        gate = jax.nn.sigmoid(jnp.einsum('bsm,md->bsd', x, Wg))
        return jnp.einsum('bsd,dm->bsm', o * gate, Wo)

    def _L0_ffn_ref(x, w_router, w1, b1, w2, b2):
        import jax, jax.numpy as jnp
        import numpy as np
        EMBED_DIM = 256
        HIDDEN_DIM = 1024
        NUM_EXPERTS = 8
        TOP_K = 2
        orig_shape = x.shape
        xf = x.reshape(-1, EMBED_DIM)
        logits = xf @ w_router
        probs = jax.nn.softmax(logits, axis=-1)
        topk_w, topk_idx = jax.lax.top_k(probs, TOP_K)
        mask = jax.nn.one_hot(topk_idx, NUM_EXPERTS, dtype=xf.dtype)
        weights = jnp.sum(topk_w[..., None] * mask, axis=1)
        h = jnp.einsum('te,ieh->tih', xf, w1) + b1
        h = jax.nn.gelu(h)
        out = jnp.einsum('tih,ihe->tie', h, w2) + b2
        out = jnp.sum(out * weights[..., None], axis=1)
        return out.reshape(orig_shape)
    h = _L0_tok_ref(x, L0_tok_W, L0_tok_gamma)
    h = h + _L0_attn_ref(_layernorm(h, axis=-1), L0_attn_Wq, L0_attn_Wk, L0_attn_Wv, L0_attn_Wg, L0_attn_Wa, L0_attn_ba, L0_attn_Wo, L0_attn_gn_w, L0_attn_gn_b)
    h = h + _L0_ffn_ref(_layernorm(h, axis=-1), L0_ffn_w_router, L0_ffn_w1, L0_ffn_b1, L0_ffn_w2, L0_ffn_b2)
    return h

_drawn_inputs = setup_inputs


def setup_inputs(seed=0):
    import zlib

    import numpy as np

    out = dict(_drawn_inputs(seed))
    spreads = {'L0_tok_gamma': (1.0, 0.2),
     'L0_attn_gn_w': (1.0, 0.2),
     'L0_attn_gn_b': (0.0, 0.1),
     'L0_ffn_b1': (0.0, 0.355),
     'L0_ffn_b2': (0.0, 0.363)}
    factors = {'L0_attn_ba': 4.91}
    for name, (base, spread) in spreads.items():
        noise = np.random.default_rng([zlib.crc32(name.encode()), seed]).standard_normal(out[name].shape)
        drawn = base * np.exp(spread * noise) if base else spread * noise
        out[name] = jnp.asarray(drawn.astype(out[name].dtype))
    for name, factor in factors.items():
        out[name] = (out[name] * factor).astype(out[name].dtype)
    return out
```

```python
from contextlib import ExitStack

import numpy as np
import concourse.bass as bass
from concourse import mybir

F32 = mybir.dt.float32
F32R = mybir.dt.float32r
BF16 = mybir.dt.bfloat16
I32 = mybir.dt.int32
U32 = mybir.dt.uint32
ALU = mybir.AluOpType
ACT = mybir.ActivationFunctionType
AX = mybir.AxisListType

P = 128
B = 16
S = 256
NS = S // P
C, PATCH, SIDE = 5, 8, 128
FEAT = C * PATCH * PATCH
KT = FEAT // P
KREM = FEAT - KT * P
E = 256
EC = E // P
H, D = 16, 64
DI = H * D
NP = DI // P
PQ = NP // 2
X = 8
HID = 1024
HC = HID // P
TOPK = 2
T = B * S
EPS = 1e-5
BLK = 512
BS = BLK // P
CAP = T + BLK
NBLK = T // BLK
NT = (T * TOPK + X * (BLK - 1)) // BLK
LW = S + P


def vit_layer(nc, xT, w_tok, gamma, wq, wk, wv, wg, wa, ba, wo, gn_w, gn_b,
              w_router, w1, b1, w2, b2,
              ident_d, upper_d, ones_d, strict_d, half_d, sel_d, mask_d, iota_d, blk_d, tri8_d, til_d, out):
    with ExitStack() as ctx:
        def sb(name, shape, dt=F32):
            return ctx.enter_context(nc.sbuf_tensor(name, shape, dt))

        def sem(name):
            return ctx.enter_context(nc.semaphore(name))

        xnT_d = nc.dram_tensor("xnT_scratch", (B, P, EC * S), F32).ap()
        h_d = nc.dram_tensor("h_scratch", (B, P, NS * E), F32).ap()
        h2_d = nc.dram_tensor("h2_scratch", (B, P, NS * E), F32).ap()
        lists_d = nc.dram_tensor("expert_rows", (X * CAP, E), F32).ap()
        y_d = nc.dram_tensor("expert_out", (NT * BLK, E), F32).ap()

        ident = sb("ident", [P, P])
        upper = sb("upper", [P, P])
        ones = sb("ones", [P, P])
        strict = sb("strict", [P, P])
        half = sb("half", [P, P])
        sel_r = sb("sel_r", [2 * H, H * P], F32R)
        identb = sb("identb", [P, P], BF16)
        maskb = sb("maskb", [P, 2 * P], BF16)
        iota8 = sb("iota8", [P, X])
        gammaB = sb("gammaB", [P, E])
        baB = sb("baB", [P, H])
        wa_sb = sb("wa_sb", [P, EC, H])
        wr_sb = sb("wr_sb", [P, EC, X])
        gnw = sb("gnw", [P, NP])
        gnb = sb("gnb", [P, NP])
        gnwh = sb("gnwh", [P, NP])
        gnbh = sb("gnbh", [P, NP])

        big_r = sb("big_r", [P, 20480], F32R)
        wsp = [[big_r[:, (2 * i + j) * 2048:(2 * i + j + 1) * 2048].rearrange("p (k n) -> p k n", k=EC)
                for j in range(2)] for i in range(4)]
        wo_sp = [big_r[:, 16384 + j * 2048:16384 + (j + 1) * 2048].rearrange("p (k n) -> p k n", k=NP)
                 for j in range(2)]
        w1_sp = [big_r[:, j * 2048:(j + 1) * 2048].rearrange("p (k n) -> p k n", k=EC) for j in range(2)]
        w2_sp = [big_r[:, (2 + j) * 2048:(3 + j) * 2048].rearrange("p (k n) -> p k n", k=HC) for j in range(2)]
        g_sp = [big_r[:, 8192 + j * 4096:8192 + (j + 1) * 4096].rearrange("p (k n) -> p k n", k=HC) for j in range(2)]
        xe_sp = [big_r[:, 16384 + j * 1024:16384 + (j + 1) * 1024].rearrange("p (k n) -> p k n", k=EC) for j in range(2)]

        small_r = sb("small_r", [P, 5120], F32R)
        xt_sp = [[small_r[:, (2 * i + j) * 768:(2 * i + j + 1) * 768].rearrange("p (k n) -> p k n", k=KT + 1)
                  for j in range(2)] for i in range(2)]
        wt_sp = [small_r[:, 3072 + j * 768:3072 + (j + 1) * 768].rearrange("p (k n) -> p k n", k=KT + 1)
                 for j in range(2)]
        y_sp = [small_r[:, j * 2048:(j + 1) * 2048].rearrange("p (k n) -> p k n", k=NP) for j in range(2)]
        xn_sp = [small_r[:, 4096 + j * 512:4096 + (j + 1) * 512].rearrange("p (k n) -> p k n", k=EC)
                 for j in range(2)]

        big_f = sb("big_f", [P, 8192])
        stage_w = [big_f[:, i * 2048:(i + 1) * 2048] for i in range(2)]
        xt_f = [big_f[:, 4096 + i * 768:4096 + (i + 1) * 768].rearrange("p (k n) -> p k n", k=KT + 1) for i in range(2)]
        wt_f = big_f[:, 5632:6400].rearrange("p (k n) -> p k n", k=KT + 1)
        sel_f = stage_w[1][0:2 * H, :]
        tg = [big_f[:, i * 2048:(i + 1) * 2048].rearrange("p (k n) -> p k n", k=NP) for i in range(2)]
        osb = [big_f[:, 4096 + i * 2048:4096 + (i + 1) * 2048].rearrange("p (k n) -> p k n", k=NP) for i in range(2)]
        w1_f = [big_f[:, i * 2048:(i + 1) * 2048] for i in range(2)]
        w2_f = [big_f[:, 4096 + i * 2048:4096 + (i + 1) * 2048] for i in range(2)]

        mid_f = sb("mid_f", [P, 6144])
        hn1 = [mid_f[:, i * 512:(i + 1) * 512].rearrange("p (s n) -> p s n", s=NS) for i in range(2)]
        h1 = [mid_f[:, 1024 + i * 512:1024 + (i + 1) * 512].rearrange("p (s n) -> p s n", s=NS) for i in range(2)]
        xn1 = [mid_f[:, 2048 + i * 512:2048 + (i + 1) * 512].rearrange("p (s n) -> p s n", s=NS) for i in range(2)]
        xnT1 = [mid_f[:, 3072 + i * 512:3072 + (i + 1) * 512].rearrange("p (k n) -> p k n", k=EC) for i in range(2)]
        v_sb = mid_f[:, 0:2048].rearrange("p (s n) -> p s n", s=NS)
        yn = mid_f[:, 2048:4096].rearrange("p (k n) -> p k n", k=NP)
        yf = mid_f[:, 4096:6144].rearrange("p (k n) -> p k n", k=NP)
        rows_f = [mid_f[:, i * 1024:(i + 1) * 1024].rearrange("p (s n) -> p s n", s=BS) for i in range(2)]
        gel = [mid_f[:, 2048 + i * 512:2048 + (i + 1) * 512] for i in range(2)]
        yo = [mid_f[:, 3072 + i * 1024:3072 + (i + 1) * 1024].rearrange("p (s n) -> p s n", s=BS) for i in range(2)]

        qk_s = [sb(f"qk_s{i}", [P, 2 * S]) for i in range(2)]
        tq = sb("tq", [P, 2 * S])
        dec = [sb(f"dec{i}", [P, LW]) for i in range(2)]
        att = [sb(f"att{i}", [P, LW]) for i in range(2)]
        xs = sb("xs", [P, EC * S])
        hb = sb("hb", [P, NS * E])
        h2 = sb("h2", [P, NS, E])
        xn2 = sb("xn2", [P, NS, E])
        xn2T = sb("xn2T", [P, EC, S])
        cumR = sb("cumR", [2 * H, LW], F32R)
        ccs = sb("ccs", [P, NS, 2 * H])
        ncum = sb("ncum", [P, NS, H])
        z_all = sb("z_all", [P, B * NS, H])
        la_all = sb("la_all", [P, B * NS, H])
        za, zl = qk_s
        st = sb("st", [P, NS, 6])
        mv = sb("mv", [P, NS, 2])
        rs = sb("rs", [P, NS, 1])
        mhalf = sb("mhalf", [P, NP])
        st1 = [sb(f"st1_{i}", [P, NS, 6]) for i in range(2)]
        mv1 = [sb(f"mv1_{i}", [P, NS, 2]) for i in range(2)]
        rs1 = [sb(f"rs1_{i}", [P, NS, 1]) for i in range(2)]
        gst = sb("gst", [P, 6])
        gmv = sb("gmv", [P, NP, 2])
        gm = sb("gm", [P, NP])
        gd = sb("gd", [P, NP])
        gt = sb("gt", [P, NP])
        gr = sb("gr", [P, NP])
        gsc = sb("gsc", [P, NP])
        gbi = sb("gbi", [P, NP])
        lg = sb("lg", [P, NS, X])
        top = sb("top", [P, NS, X])
        topi = sb("topi", [P, NS, X], U32)
        tope = sb("tope", [P, NS, X])
        ntop = sb("ntop", [P, NS, 1])
        tsum = sb("tsum", [P, NS, 1])
        trec = sb("trec", [P, NS, 1])
        idxf = sb("idxf", [P, NS, TOPK])
        pick = sb("pick", [P, NS, TOPK, X])
        both = sb("both", [P, NS, X])
        rank = sb("rank", [P, NS, X])
        rsel = sb("rsel", [P, NS * TOPK])
        junk = sb("junk", [P, X])
        taken = sb("taken", [P, X])
        slot = sb("slot", [P, NS * TOPK], U32)
        slots_all = sb("slots_all", [P, B, NS * TOPK], U32)
        w_all = sb("w_all", [P, B, NS * TOPK])
        iob = sb("iob", [P, X * NBLK])
        tri8 = sb("tri8", [P, X * X])
        til = sb("til", [P, NT * X])
        tmp64 = sb("tmp64", [P, X, X])
        nb = sb("nb", [P, X])
        cb = sb("cb", [P, X])
        cmp = sb("cmp", [P, NT, X])
        cmn = sb("cmn", [P, NT, X])
        te = sb("te", [P, NT])
        tst = sb("tst", [P, NT])
        tva = sb("tva", [P, NT])
        tr0 = sb("tr0", [P, NT])
        dlt = sb("dlt", [P, X])
        idx_all = sb("idx_all", [P, B, NS * TOPK])
        onx = hb[:, :].rearrange("p (n a) -> p n a", a=X)
        dsel = sb("dsel", [P, B * NS * TOPK])
        yrow = sb("yrow", [P, B * NS * TOPK], U32)
        tab = sb("tab", [P, 2 * NT], I32)
        padf = sb("padf", [P, X])
        padi = sb("padi", [P, X], I32)
        zeros = sb("zeros", [P, E])
        b1_sb = [sb(f"b1_{i}", [P, HC]) for i in range(2)]
        b2_sb = [tq[:, i * E:(i + 1) * E] for i in range(2)]
        NG = 3
        ga = [mid_f[:, (2 * i) * 256:(2 * i + 1) * 256] for i in range(NG)]
        gb = [mid_f[:, (2 * i + 1) * 256:(2 * i + 2) * 256] for i in range(NG)]
        hf = [mid_f[:, 2048 + i * 256:2304 + i * 256] for i in range(NG)]
        f1 = [mid_f[:, 3072 + i * 256:3328 + i * 256] for i in range(NG)]
        f2 = [mid_f[:, 4096 + i * 256:4352 + i * 256] for i in range(NG)]
        slc = [sb(f"slc{i}", [P, 1], U32) for i in range(2 * NG)]

        bank = [ctx.enter_context(nc.psum_tensor(f"bank{i}", [P, 512], F32)) for i in range(8)]

        names = """
        passed mh_done c_in c_sel c_selr c_maskb ws_in0 ws_in1 ws_hi ws_lo wt_in wt_hi wt_lo g_in
        xt_in0 xt_in1 xt_hi xt_lo0 xt_lo1 tok_ps0 tok_ps1 s1_st s1_mv s1_ve s1_ve2 s1_rs s1_hn0 s1_hn1 s1_h s1_st2 s1_mv2 s1_rs2 s1_xn s1_tps0 s1_tps1 s1_xnT0 s1_xnT1 s1_aps0 s1_aps1 s1_z0 s1_z1 b_ve gv_done
        h_out0 h_out1 xnT_out0 xnT_out1
        sp_abs sp_e sp_l sp_m sp_la gnh
        xs_in xh_done xl_done cum_ps cc_hi cc_lo ncum_done ct_ps ct_copied v_ps v_act v_dve
        qk_ps g_ps tq_done tg_done silu_done d_ps exp_done s_ps mult_done o_ps o_done gst_done gmv_done
        gn1_ps gn_step gt2_done gn2_ps gr_done yn_done yf_done yh_done yl_done
        wo_ps hb_in h2_done h2_out b_st b_mv b_rs b_xn x2_ps x2_done lg_ps lg_done top_done topi_done ntop_done
        tope_done trec_done wall_done idxf_done pick_done both_done rk_ps rank_done taken_done rsel_done
        slot_done slotc_done scat
        tb zero_done pad_out
        row_in0 row_in1 w1_in0 w1_in1 w2_in0 w2_in1 b_in0 b_in1 xe_ps xe_hi xe_lo w1_hi w1_lo w2_hi w2_lo
        hid_ps gel_done gh_done gl_done y_ps y_done y_out0 y_out1
        slc_done ga_in0 ga_in1 ga_in2 hf_in0 hf_in1 hf_in2 f1_done f2_done o_out0 o_out1 o_out2
        """.split()
        M = {n: sem(n) for n in names}

        block = ctx.enter_context(nc.Block())

        def three(part_w, part_x):
            return [(part_w[0], part_x[0]), (part_w[0], part_x[1]), (part_w[1], part_x[0])]

        def f32(ap):
            return ap.bitcast(F32)

        def plain(eng):
            eng.sem_inc(M["passed"])

        W_ATT = [wq, wk, wv, wg]
        w_parts = wsp + [wo_sp]

        @block.sync
        def _(sp):
            for dst, src in ((ident[:, :], ident_d), (gammaB[:, :], gamma.rearrange("(a n) -> a n", a=1).broadcast_to([P, E])),
                             (baB[:, :], ba.rearrange("(a n) -> a n", a=1).broadcast_to([P, H])),
                             (wa_sb[:, :, :], wa.rearrange("(k p) n -> p k n", p=P))):
                sp.dma_start(dst, src).then_inc(M["c_in"], 16)
            sp.dma_start(wt_f[:, 0:KT, :], w_tok[0:KT * P, :].rearrange("(k p) n -> p k n", p=P)).then_inc(M["wt_in"], 16)
            sp.dma_start(wt_f[0:KREM, KT, :], w_tok[KT * P:FEAT, :]).then_inc(M["wt_in"], 16)

            def load_patches(p, par):
                b = 2 * p + par
                sp.wait_ge(M[f"xt_lo{par}"], 2 * p)
                src = xT[:, bass.ds(b * S, S)]
                sp.dma_start(xt_f[par][:, 0:KT, :], src[0:KT * P, :].rearrange("(k p) n -> p k n", p=P)).then_inc(M[f"xt_in{par}"], 16)
                sp.dma_start(xt_f[par][0:KREM, KT, :], src[KT * P:FEAT, :]).then_inc(M[f"xt_in{par}"], 16)

            def store_stage1(p, par):
                b = 2 * p + par
                sp.wait_ge(M["s1_h"], NS * (b + 1))
                sp.dma_start(h_d[bass.ds(b, 1), :, :].rearrange("a p n -> (a p) n"),
                             h1[par].rearrange("p s n -> p (s n)")).then_inc(M[f"h_out{par}"], 16)
                sp.wait_ge(M[f"s1_xnT{par}"], p + 1)
                sp.dma_start(xnT_d[bass.ds(b, 1), :, :].rearrange("a p n -> (a p) n"),
                             xnT1[par].rearrange("p k n -> p (k n)")).then_inc(M[f"xnT_out{par}"], 16)

            for par in range(2):
                load_patches(0, par)
            def two_images(p):
                for par in range(2):
                    store_stage1(p, par)
                    load_patches(p + 1, par)

            two_images(0)
            with sp.Fori(1, B // 2 - 1) as p:
                two_images(p)
            for par in range(2):
                store_stage1(B // 2 - 1, par)

            for i, w in enumerate(W_ATT + [wo]):
                if i == 1:
                    sp.wait_ge(M["c_selr"], 1)
                if i >= 2:
                    sp.wait_ge(M["ws_lo"], i - 1)
                sp.dma_start(stage_w[i % 2].rearrange("p (k n) -> p k n", k=EC if i < 4 else NP),
                             w.rearrange("(k p) n -> p k n", p=P)).then_inc(M[f"ws_in{i % 2}"], 16)

            for par in range(2):
                sp.wait_ge(M[f"h_out{par}"], 16 * (B // 2))
                sp.wait_ge(M[f"xnT_out{par}"], 16 * (B // 2))

            def load_image(b):
                sp.wait_ge(M["xl_done"], b)
                sp.dma_start(xs[:, :], xnT_d[bass.ds(b, 1), :, :].rearrange("a p n -> (a p) n")).then_inc(M["xs_in"], 16)

            def load_h(b):
                sp.wait_ge(M["h2_done"], b)
                sp.dma_start(hb[:, :], h_d[bass.ds(b, 1), :, :].rearrange("a p n -> (a p) n")).then_inc(M["hb_in"], 16)

            def store_h2(b):
                sp.wait_ge(M["h2_done"], b + 1)
                sp.dma_start(h2_d[bass.ds(b, 1), :, :].rearrange("a p n -> (a p) n"),
                             h2[:, :, :].rearrange("p s n -> p (s n)")).then_inc(M["h2_out"], 16)

            load_image(0)
            load_h(0)
            load_image(1)
            with sp.Fori(2, B) as b:
                store_h2(b - 2)
                load_h(b - 1)
                load_image(b)
            store_h2(B - 2)
            load_h(B - 1)
            store_h2(B - 1)

            sp.wait_ge(M["tb"], 19)
            sp.wait_ge(M["zero_done"], 1)
            for e in range(X):
                first = sp.value_load(padi[0:1, e:e + 1], min_val=e * CAP, max_val=e * CAP + T)
                sp.dma_start(lists_d[bass.ds(first, BLK), :].rearrange("(s p) n -> p s n", p=P),
                             zeros[:, :].rearrange("p (a n) -> p a n", a=1).broadcast_to([P, BS, E])).then_inc(M["pad_out"], 16)
            sp.wait_ge(M["pad_out"], 16 * X)
            sp.wait_ge(M["scat"], 16 * NS * TOPK * B)

            def load_weights(i, par, n):
                e = sp.value_load(tab[0:1, bass.ds(i, 1)], min_val=0, max_val=X - 1)
                r = sp.value_load(tab[0:1, bass.ds(i + NT, 1)], min_val=0, max_val=X * CAP - BLK)
                sp.wait_ge(M["xe_ps"], EC * 2 * n)
                sp.dma_start(rows_f[par], lists_d[bass.ds(r, BLK), :].rearrange("(s p) n -> p s n", p=P)).then_inc(M[f"row_in{par}"], 16)
                sp.wait_ge(M["w1_lo"], 2 * n)
                sp.dma_start(w1_f[par].rearrange("p (k n) -> p k n", k=EC),
                             w1[bass.ds(e, 1), :, :].rearrange("a (k p) n -> (a p) k n", p=P)).then_inc(M[f"w1_in{par}"], 16)
                sp.wait_ge(M["gh_done"], HC * 2 * n)
                sp.dma_start(b1_sb[par][:, :], b1[bass.ds(e, 1), :, :].rearrange("a p k -> (a p) k")).then_inc(M[f"b_in{par}"], 16)
                sp.wait_ge(M["w2_lo"], 2 * n)
                sp.dma_start(w2_f[par].rearrange("p (k n) -> p k n", k=HC),
                             w2[bass.ds(e, 1), :, :].rearrange("a (k p) n -> (a p) k n", p=P)).then_inc(M[f"w2_in{par}"], 16)
                sp.wait_ge(M["y_done"], 2 * 2 * n)
                sp.dma_start(b2_sb[par][:, :], b2[bass.ds(e, 1), :].broadcast_to([P, E])).then_inc(M[f"b_in{par}"], 16)

            def store_rows(i, par):
                sp.wait_ge(M["y_done"], 2 * (i + 1))
                sp.dma_start(y_d[bass.ds(i * BLK, BLK), :].rearrange("(s p) n -> p s n", p=P), yo[par]).then_inc(M[f"y_out{par}"], 16)

            load_weights(0, 0, 0)
            def two_blocks(q):
                load_weights(2 * q + 1, 1, q)
                store_rows(2 * q, 0)
                load_weights(2 * q + 2, 0, q + 1)
                store_rows(2 * q + 1, 1)

            two_blocks(0)
            with sp.Fori(1, (NT - 1) // 2) as q:
                two_blocks(q)
            store_rows(NT - 1, 0)

            sp.wait_ge(M["h2_out"], 16 * B)

            def load_h2(t, r, n):
                sp.wait_ge(M["f1_done"], t - NG + 1) if t >= NG else None
                sp.dma_start(hf[r], h2_d[t // NS, :, (t % NS) * E:(t % NS + 1) * E]).then_inc(M[f"hf_in{r}"], 16)

            def store_out(t, r):
                sp.wait_ge(M["f2_done"], t + 1)
                sp.dma_start(out[t // NS, (t % NS) * P:(t % NS + 1) * P, :], f2[r]).then_inc(M[f"o_out{r}"], 16)

            sp.wait_ge(M["y_out0"], 16 * ((NT + 1) // 2))
            sp.wait_ge(M["y_out1"], 16 * (NT // 2))
            for t in range(T // P):
                load_h2(t, t % NG, t // NG)
                if t >= 2:
                    store_out(t - 2, (t - 2) % NG)
            store_out(T // P - 2, (T // P - 2) % NG)
            store_out(T // P - 1, (T // P - 1) % NG)
            for r in range(NG):
                sp.wait_ge(M[f"o_out{r}"], 16 * len(range(r, T // P, NG)))

        @block.gpsimd
        def _(pool):
            for n, dst in enumerate((upper, ones, strict, half)):
                pool.dma_start(dst[:, :], (upper_d, ones_d, strict_d, half_d)[n]).then_inc(M["g_in"], 16)
            pool.dma_start(sel_f, sel_d).then_inc(M["c_sel"], 16)
            pool.dma_start(iota8[:, :], iota_d).then_inc(M["g_in"], 16)
            pool.dma_start(wr_sb[:, :, :], w_router.rearrange("(k p) n -> p k n", p=P)).then_inc(M["g_in"], 16)
            pool.dma_start(gnw[:, :], gn_w).then_inc(M["g_in"], 16)
            pool.dma_start(gnb[:, :], gn_b).then_inc(M["g_in"], 16)
            pool.dma_start(iob[:, :], blk_d.broadcast_to(iob.shape)).then_inc(M["g_in"], 16)
            pool.dma_start(tri8[:, :], tri8_d.broadcast_to(tri8.shape)).then_inc(M["g_in"], 16)
            pool.dma_start(til[:, :], til_d.broadcast_to(til.shape)).then_inc(M["g_in"], 16)
            pool.memset(zeros[:, :], 0.0).then_inc(M["zero_done"], 1)
            pool.wait_ge(M["c_sel"], 16)
            pool.tensor_copy(sel_r[:, :], sel_f).then_inc(M["c_selr"], 1)
            pool.dma_start(dec[0][:, 0:2 * P], mask_d).then_inc(M["c_maskb"], 16)
            pool.wait_ge(M["c_maskb"], 16)
            pool.tensor_copy(maskb[:, :], dec[0][:, 0:2 * P]).then_inc(M["c_selr"], 1)
            pool.wait_ge(M["c_in"], 64)
            pool.tensor_copy(identb[:, :], ident[:, :]).then_inc(M["c_selr"], 1)
            pool.memset(mhalf[:, :], -0.5).then_inc(M["mh_done"], 1)
            pool.wait_ge(M["mh_done"], 1)

            def rsqrt(v, given, made, n):
                pool.wait_ge(M[given], n)
                pool.tensor_tensor(v, v, mhalf[:, 0:v.shape[1]], ALU.pow).then_inc(M[made], 1)

            with pool.Fori(0, B // 2) as p:
                for par in range(2):
                    rsqrt(rs1[par][:, :, 0], "s1_ve", "s1_rs", 2 * p + par + 1)
                    rsqrt(rs1[par][:, :, 0], "s1_ve2", "s1_rs2", 2 * p + par + 1)

            def scatter(b):
                for j in range(NS * TOPK):
                    if j == 0:
                        pool.wait_ge(M["slot_done"], b + 1)
                        plain(pool)
                    pool.indirect_dma_start(out=lists_d[:, :], out_offset=bass.IndirectOffsetOnAxis(ap=slot[:, j:j + 1], axis=0),
                                            in_=xn2[:, j // TOPK, :], in_offset=None).then_inc(M["scat"], 16)

            with pool.Fori(0, B) as b:
                rsqrt(gr[:, :], "gv_done", "gr_done", b + 1)
                rsqrt(rs[:, :, 0], "b_ve", "b_rs", b + 1)
                scatter(b)

            pool.wait_ge(M["y_out0"], 16 * ((NT + 1) // 2))
            pool.wait_ge(M["y_out1"], 16 * (NT // 2))
            for t in range(T // P):
                r = t % NG
                pool.wait_ge(M["slc_done"], 2 * (t + 1))
                if t >= NG:
                    pool.wait_ge(M["f2_done"], t - NG + 1)
                pool.indirect_dma_start(out=ga[r], out_offset=None, in_=y_d[:, :],
                                        in_offset=bass.IndirectOffsetOnAxis(ap=slc[2 * r][:, 0:1], axis=0)).then_inc(M[f"ga_in{r}"], 16)
                pool.indirect_dma_start(out=gb[r], out_offset=None, in_=y_d[:, :],
                                        in_offset=bass.IndirectOffsetOnAxis(ap=slc[2 * r + 1][:, 0:1], axis=0)).then_inc(M[f"ga_in{r}"], 16)

        @block.scalar
        def _(act):
            act.wait_ge(M["wt_in"], 32)
            act.activation(wt_sp[0][:, 0:KT, :], wt_f[:, 0:KT, :], ACT.Copy).then_inc(M["wt_hi"], 1)
            act.activation(wt_sp[0][0:KREM, KT, :], wt_f[0:KREM, KT, :], ACT.Copy).then_inc(M["wt_hi"], 1)

            def split_hi(p, par):
                act.wait_ge(M[f"xt_in{par}"], 32 * (p + 1))
                act.wait_ge(M[f"tok_ps{par}"], NS * p)
                act.activation(xt_sp[par][0][:, 0:KT, :], xt_f[par][:, 0:KT, :], ACT.Copy).then_inc(M["xt_hi"], 1)
                act.activation(xt_sp[par][0][0:KREM, KT, :], xt_f[par][0:KREM, KT, :], ACT.Copy).then_inc(M["xt_hi"], 1)

            def keep_xnT(p, par):
                b = 2 * p + par
                act.wait_ge(M[f"s1_tps{par}"], p + 1)
                act.wait_ge(M[f"xnT_out{par}"], 16 * p)
                act.wait_ge(M[f"s1_aps{par}"], p)
                act.activation(xnT1[par].rearrange("p k n -> p (k n)"), bank[4 + par][:, :], ACT.Copy).then_inc(M[f"s1_xnT{par}"], 1)

            for par in range(2):
                split_hi(0, par)
            def two_images(p):
                for par in range(2):
                    keep_xnT(p, par)
                    split_hi(p + 1, par)

            two_images(0)
            with act.Fori(1, B // 2 - 1) as p:
                two_images(p)
            for par in range(2):
                keep_xnT(B // 2 - 1, par)

            for i in range(5):
                act.wait_ge(M[f"ws_in{i % 2}"], 16 * (i // 2 + 1))
                act.activation(w_parts[i][0].rearrange("p k n -> p (k n)"), stage_w[i % 2], ACT.Copy).then_inc(M["ws_hi"], 1)

            for par in range(2):
                act.wait_ge(M[f"s1_z{par}"], B // 2)
            act.activation(za[:, :], z_all[:, :, :].rearrange("p t n -> p (t n)"), ACT.Abs).then_inc(M["sp_abs"], 1)
            act.wait_ge(M["sp_abs"], 1)
            act.activation(zl[:, :], za[:, :], ACT.Exp, scale=-1.0).then_inc(M["sp_e"], 1)
            act.wait_ge(M["sp_e"], 1)
            act.activation(za[:, :], zl[:, :], ACT.Ln, bias=1.0).then_inc(M["sp_l"], 1)

            def tanh_qk(b, c):
                act.wait_ge(M["qk_ps"], NP * b + c + 1)
                act.wait_ge(M["silu_done"], NP * b + c)
                act.activation(tq[:, :], bank[0][:, :], ACT.Tanh, scale=0.5).then_inc(M["tq_done"], 1)

            def tanh_g(b, c, par):
                act.wait_ge(M["g_ps"], NP * b + c + 1)
                act.activation(tg[par][:, c, :], bank[1][:, 0:S], ACT.Tanh, scale=0.5).then_inc(M["tg_done"], 1)

            def decay(b, h):
                act.wait_ge(M["d_ps"], H * b + h + 1)
                act.wait_ge(M["mult_done"], H * b + max(h - 1, 0))
                act.activation(dec[h % 2][:, 0:S], bank[2 + h % 2][:, 0:S], ACT.Exp, bias=ncum[:, 0, h:h + 1])
                act.activation(dec[h % 2][:, S:LW], bank[2 + h % 2][:, S:LW], ACT.Exp, bias=ncum[:, 1, h:h + 1]).then_inc(M["exp_done"], 1)

            def keep_o(b, c, par):
                act.wait_ge(M["o_ps"], NP * b + c + 1)
                act.activation(osb[par][:, c, :], bank[6][:, 0:S], ACT.Copy).then_inc(M["o_done"], 1)

            def y_hi(pb, j):
                act.wait_ge(M["yf_done"], 2 * pb + j + 1)
                act.wait_ge(M["wo_ps"], pb)
                act.activation(y_sp[0][:, PQ * j:PQ * j + PQ, :], yf[:, PQ * j:PQ * j + PQ, :], ACT.Copy).then_inc(M["yh_done"], 1)

            def keep_x2(pb):
                act.wait_ge(M["x2_ps"], pb + 1)
                act.wait_ge(M["lg_ps"], pb)
                act.activation(xn2T[:, :, :].rearrange("p k n -> p (k n)"), bank[7][:, :], ACT.Copy).then_inc(M["x2_done"], 1)

            def top_exp(pb):
                act.wait_ge(M["ntop_done"], pb + 1)
                act.wait_ge(M["wall_done"], pb)
                for s in range(NS):
                    act.activation(tope[:, s, :], top[:, s, :], ACT.Exp, bias=ntop[:, s, :],
                                   accum_out=tsum[:, s, :]).then_inc(M["tope_done"], 1)

            def image(b, par, post):
                act.wait_ge(M["xs_in"], 16 * (b + 1))
                act.wait_ge(M["g_ps"], NP * b)
                act.activation(xn_sp[0].rearrange("p k n -> p (k n)"), xs[:, :], ACT.Copy).then_inc(M["xh_done"], 1)
                for i in range(2):
                    act.wait_ge(M["v_ps"], 4 * b + i + 1)
                    if i == 0:
                        act.wait_ge(M["o_ps"], NP * b)
                    act.activation(v_sb[:, 0, i * 512:(i + 1) * 512], bank[2 + i][:, :], ACT.Copy).then_inc(M["v_act"], 1)
                act.wait_ge(M["ct_ps"], b + 1)
                act.activation(cumR[:, 0:S], bank[7][0:2 * H, 0:S], ACT.Copy)
                act.activation(cumR[:, S:LW], bank[7][0:2 * H, P:S], ACT.Copy).then_inc(M["ct_copied"], 1)
                tanh_qk(b, 0)
                tanh_g(b, 0, par)
                for c in range(NP):
                    decay(b, 2 * c)
                    decay(b, 2 * c + 1)
                    if c + 1 < NP:
                        tanh_qk(b, c + 1)
                        tanh_g(b, c + 1, par)
                    if post and c in (1, 2):
                        y_hi(b - 1, c - 1)
                    if post and c == 5:
                        keep_x2(b - 1)
                    if post and c == 6:
                        top_exp(b - 1)
                    keep_o(b, c, par)

            act.wait_ge(M["ncum_done"], 0)
            image(0, 0, False)
            image(1, 1, True)
            with act.Fori(1, B // 2) as p:
                image(2 * p, 0, True)
                image(2 * p + 1, 1, True)
            y_hi(B - 1, 0)
            y_hi(B - 1, 1)
            keep_x2(B - 1)
            top_exp(B - 1)

            def w_hi(name, parts, staged, par, n, i, used, count):
                act.wait_ge(M[f"{name}_in{par}"], 16 * (n + 1))
                act.wait_ge(M[used], count)
                act.activation(parts[0].rearrange("p k n -> p (k n)"), staged[par], ACT.Copy).then_inc(M[f"{name}_hi"], 1)

            def x_hi(i):
                for k in range(EC):
                    act.wait_ge(M["xe_ps"], EC * i + k + 1)
                    act.wait_ge(M["hid_ps"], HC * i)
                    act.activation(xe_sp[0][:, k, :], bank[k][:, :], ACT.Copy).then_inc(M["xe_hi"], 1)

            def hidden(i, par, n, c):
                act.wait_ge(M["hid_ps"], HC * i + c + 1)
                if c == 0:
                    act.wait_ge(M[f"b_in{par}"], 32 * (n + 1))
                act.wait_ge(M["gl_done"], HC * i + max(c - 1, 0))
                act.activation(gel[c % 2], bank[2 + c % 2][:, :], ACT.Gelu_apprx_tanh, bias=b1_sb[par][:, c:c + 1]).then_inc(M["gel_done"], 1)
                act.wait_ge(M["gel_done"], HC * i + c + 1)
                act.wait_ge(M["y_ps"], i)
                act.activation(g_sp[0][:, c, :], gel[c % 2], ACT.Copy).then_inc(M["gh_done"], 1)

            def blockrow(i, par, n, last):
                for c in range(HC):
                    hidden(i, par, n, c)
                    if c == 1:
                        w_hi("w2", w2_sp, w2_f, par, n, i, "y_ps", i)
                if not last:
                    nn = n + (1 if par else 0)
                    x_hi(i + 1)
                    w_hi("w1", w1_sp, w1_f, 1 - par, nn, i + 1, "hid_ps", HC * (i + 1))

            act.wait_ge(M["rank_done"], 0)
            x_hi(0)
            w_hi("w1", w1_sp, w1_f, 0, 0, 0, "wo_ps", B)
            def two_blocks(q):
                blockrow(2 * q, 0, q, False)
                blockrow(2 * q + 1, 1, q, False)

            two_blocks(0)
            with act.Fori(1, (NT - 1) // 2) as q:
                two_blocks(q)
            blockrow(NT - 1, 0, (NT - 1) // 2, True)

        @block.tensor
        def _(pe):
            pe.wait_ge(M["wt_lo"], 2)
            pe.wait_ge(M["c_in"], 64)

            def tokens(p, par):
                b = 2 * p + par
                pe.wait_ge(M[f"xt_lo{par}"], 2 * (p + 1))
                for s in range(NS):
                    pe.wait_ge(M[f"s1_hn{par}"], NS * p)
                    for k in range(KT + 1):
                        rows = P if k < KT else KREM
                        for j, (wp, xp) in enumerate(three(wt_sp, xt_sp[par])):
                            mm = pe.matmul(bank[2 * par + s][:, 0:E], xp[0:rows, k, s * P:(s + 1) * P], wp[0:rows, k, :],
                                           start=(k == 0 and j == 0), stop=(k == KT and j == 2))
                    mm.then_inc(M[f"tok_ps{par}"], 1)

            def turn(p, par):
                b = 2 * p + par
                pe.wait_ge(M["s1_xn"], NS * (b + 1))
                pe.wait_ge(M[f"s1_xnT{par}"], p)
                for k in range(EC):
                    for s in range(NS):
                        mm = pe.transpose(bank[4 + par][:, k * S + s * P:k * S + (s + 1) * P],
                                          xn1[par][:, s, k * P:(k + 1) * P], ident[:, :])
                mm.then_inc(M[f"s1_tps{par}"], 1)

            def logits(p, par):
                b = 2 * p + par
                pe.wait_ge(M[f"s1_xnT{par}"], p + 1)
                pe.wait_ge(M[f"s1_z{par}"], p)
                for s in range(NS):
                    for k in range(EC):
                        mm = pe.matmul(bank[6 + par][:, s * H:(s + 1) * H], xnT1[par][:, k, s * P:(s + 1) * P], wa_sb[:, k, :],
                                       start=(k == 0), stop=(k == EC - 1))
                mm.then_inc(M[f"s1_aps{par}"], 1)

            tokens(0, 0)
            tokens(0, 1)
            def two_images(p):
                for par in range(2):
                    turn(p, par)
                    logits(p, par)
                    tokens(p + 1, par)

            two_images(0)
            with pe.Fori(1, B // 2 - 1) as p:
                two_images(p)
            for par in range(2):
                turn(B // 2 - 1, par)
                logits(B // 2 - 1, par)

            def cum(b):
                pe.wait_ge(M["taken_done"], b - 1) if not isinstance(b, int) or b > 1 else None
                pe.wait_ge(M["sp_la"], 1)
                la = [la_all[:, bass.ds(2 * b + s, 1), :].rearrange("p a n -> p (a n)") for s in range(NS)]
                pe.matmul(bank[7][:, 0:H], upper[:, :], la[0], start=True, stop=True)
                pe.matmul(bank[7][:, H:2 * H], ones[:, :], la[0], start=True, stop=False)
                pe.matmul(bank[7][:, H:2 * H], upper[:, :], la[1], start=False, stop=True).then_inc(M["cum_ps"], 1)

            def cum_rows(b):
                pe.wait_ge(M["ncum_done"], b + 1)
                for s in range(NS):
                    mm = pe.transpose(bank[7][0:2 * H, s * P:(s + 1) * P], ccs[:, s, :], ident[:, :])
                mm.then_inc(M["ct_ps"], 1)

            def values(b):
                pe.wait_ge(M["xl_done"], b + 1)
                for s in range(NS):
                    for n in range(2):
                        i = 2 * s + n
                        pe.wait_ge(M["exp_done"] if s == 0 else M["mult_done"], H * b)
                        for k in range(EC):
                            for j, (wp, xp) in enumerate(three(wsp[2], xn_sp)):
                                mm = pe.matmul(bank[2 + i][:, :], xp[:, k, s * P:(s + 1) * P], wp[:, k, n * 512:(n + 1) * 512],
                                               start=(k == 0 and j == 0), stop=(k == EC - 1 and j == 2))
                        mm.then_inc(M["v_ps"], 1)

            def project(dst, w, c, m):
                for k in range(EC):
                    for j, (wp, xp) in enumerate(three(wsp[w], xn_sp)):
                        mm = pe.matmul(dst, wp[:, k, c * P:(c + 1) * P], xp[:, k, :],
                                       start=(k == 0 and j == 0), stop=(k == EC - 1 and j == 2))
                if m is not None:
                    mm.then_inc(M[m], 1)

            def qkg(b, c):
                pe.wait_ge(M["silu_done"], NP * b + c)
                project(bank[0][:, 0:S], 0, c, None)
                project(bank[0][:, S:2 * S], 1, c, "qk_ps")
                pe.wait_ge(M["tg_done"], NP * b + c)
                project(bank[1][:, 0:S], 3, c, "g_ps")

            def decays(b, h):
                if h < 2:
                    pe.wait_ge(M["v_act"], 2 * b + h + 1)
                pe.wait_ge(M["exp_done"], H * b + max(h - 1, 0))
                if h == 0:
                    pe.wait_ge(M["ct_copied"], b + 1)
                dst = bank[2 + h % 2]
                pe.matmul(dst[:, 0:LW], sel_r[:, h * P:(h + 1) * P], cumR[:, :], start=True, stop=False)
                pe.matmul(dst[:, :].rearrange("p (a n) -> p a n", n=P)[:, 0:3:2, :], identb[:, :],
                          maskb[:, :].rearrange("p (a n) -> p a n", n=P), start=False, stop=True).then_inc(M["d_ps"], 1)

            def scores(b, c, h):
                if c == 0:
                    pe.wait_ge(M["v_dve"], 2 * b + h % 2 + 1)
                pe.wait_ge(M["mult_done"], H * b + max(h - 1, 0))
                pe.wait_ge(M["silu_done"], NP * b + c + 1)
                r = slice(D * (h % 2), D * (h % 2) + D)
                q, k = qk_s[c % 2][r, 0:S], qk_s[c % 2][r, S:2 * S]
                dst = bank[4 + h % 2]
                pe.matmul(dst[:, 0:S], k[:, 0:P], q, start=True, stop=True)
                pe.matmul(dst[:, S:LW], k[:, P:S], q[:, P:S], start=True, stop=True).then_inc(M["s_ps"], 1)

            def weighted(b, c):
                pe.wait_ge(M["o_done"], NP * b + c)
                for hh in range(2):
                    h = 2 * c + hh
                    pe.wait_ge(M["mult_done"], H * b + h + 1)
                    dst = bank[6][D * hh:D * hh + D, :]
                    pe.matmul(dst[:, 0:S], v_sb[:, 0, h * D:(h + 1) * D], att[hh][:, 0:S], start=True, stop=False)
                    mm = pe.matmul(dst[:, P:S], v_sb[:, 1, h * D:(h + 1) * D], att[hh][:, S:LW], start=False, stop=True)
                mm.then_inc(M["o_ps"], 1)

            def gn_mean(pb):
                pe.wait_ge(M["gmv_done"], NP * (pb + 1))
                if True:
                    pe.matmul(bank[7][:, 0:NP], half[:, :], gmv[:, :, 0], start=True, stop=True).then_inc(M["gn1_ps"], 1)

            def gn_var(pb):
                pe.wait_ge(M["gt2_done"], pb + 1)
                pe.matmul(bank[7][:, 0:NP], half[:, :], gt[:, :], start=True, stop=True).then_inc(M["gn2_ps"], 1)

            def out_proj(pb, j):
                pe.wait_ge(M["yl_done"], 2 * pb + j + 1)
                for c in range(PQ * j, PQ * j + PQ):
                    for s in range(NS):
                        for q, (wp, yp) in enumerate(three(wo_sp, y_sp)):
                            mm = pe.matmul(bank[7][:, s * E:(s + 1) * E], yp[:, c, s * P:(s + 1) * P], wp[:, c, :],
                                           start=(c == 0 and s == 0 and q == 0), stop=(c == NP - 1 and q == 2),
                                           skip_group_check=True)
                if j == 1:
                    mm.then_inc(M["wo_ps"], 1)

            def turn2(pb):
                pe.wait_ge(M["b_xn"], NS * (pb + 1))
                for k in range(EC):
                    for s in range(NS):
                        mm = pe.transpose(bank[7][:, k * S + s * P:k * S + (s + 1) * P], xn2[:, s, k * P:(k + 1) * P], ident[:, :])
                mm.then_inc(M["x2_ps"], 1)

            def route(pb):
                pe.wait_ge(M["x2_done"], pb + 1)
                for s in range(NS):
                    for k in range(EC):
                        mm = pe.matmul(bank[7][:, s * X:(s + 1) * X], xn2T[:, k, s * P:(s + 1) * P], wr_sb[:, k, :],
                                       start=(k == 0), stop=(k == EC - 1))
                mm.then_inc(M["lg_ps"], 1)

            def ranks(pb):
                pe.wait_ge(M["both_done"], pb + 1)
                pe.matmul(bank[7][:, 0:X], strict[:, :], both[:, 0, :], start=True, stop=True)
                pe.matmul(bank[7][:, X:2 * X], ones[:, :], both[:, 0, :], start=True, stop=False)
                pe.matmul(bank[7][:, X:2 * X], strict[:, :], both[:, 1, :], start=False, stop=True)
                pe.matmul(bank[7][:, 2 * X:3 * X], ones[:, :], both[:, 0, :], start=True, stop=False)
                pe.matmul(bank[7][:, 2 * X:3 * X], ones[:, :], both[:, 1, :], start=False, stop=True).then_inc(M["rk_ps"], 1)

            pe.wait_ge(M["g_in"], 16 * 11)
            pe.wait_ge(M["ws_lo"], 5)
            pe.wait_ge(M["c_selr"], 3)
            for par in range(2):
                pe.wait_ge(M[f"s1_z{par}"], B // 2)

            def image(b, post):
                cum(b)
                values(b)
                cum_rows(b)
                qkg(b, 0)
                for c in range(NP):
                    decays(b, 2 * c)
                    decays(b, 2 * c + 1)
                    if post and c == 0:
                        pe.wait_ge(M["ct_copied"], b + 1)
                        gn_mean(b - 1)
                    scores(b, c, 2 * c)
                    scores(b, c, 2 * c + 1)
                    if post and c == 0:
                        gn_var(b - 1)
                    if c + 1 < NP:
                        qkg(b, c + 1)
                    if post and c in (2, 3):
                        out_proj(b - 1, c - 2)
                    if post and c == 5:
                        turn2(b - 1)
                    if post and c == 6:
                        route(b - 1)
                    if post and c == 7:
                        ranks(b - 1)
                    weighted(b, c)

            image(0, False)
            image(1, True)
            with pe.Fori(1, B // 2) as p:
                image(2 * p, True)
                image(2 * p + 1, True)
            gn_mean(B - 1)
            gn_var(B - 1)
            out_proj(B - 1, 0)
            out_proj(B - 1, 1)
            turn2(B - 1)
            route(B - 1)
            ranks(B - 1)

            def turn_rows(i, par, n):
                pe.wait_ge(M[f"row_in{par}"], 16 * (n + 1))
                pe.wait_ge(M["xe_lo"], EC * i)
                for k in range(EC):
                    for s in range(BS):
                        mm = pe.transpose(bank[k][:, s * P:(s + 1) * P], rows_f[par][:, s, k * P:(k + 1) * P], ident[:, :])
                    mm.then_inc(M["xe_ps"], 1)

            def layer1(i):
                pe.wait_ge(M["xe_lo"], EC * (i + 1))
                pe.wait_ge(M["w1_lo"], i + 1)
                for c in range(HC):
                    pe.wait_ge(M["gel_done"], HC * i + max(c - 1, 0))
                    for k in range(EC):
                        for j, (wp, xp) in enumerate(three(w1_sp, xe_sp)):
                            mm = pe.matmul(bank[2 + c % 2][:, :], wp[:, k, c * P:(c + 1) * P], xp[:, k, :],
                                           start=(k == 0 and j == 0), stop=(k == EC - 1 and j == 2))
                    mm.then_inc(M["hid_ps"], 1)

            def layer2(i):
                pe.wait_ge(M["w2_lo"], i + 1)
                pe.wait_ge(M["y_done"], 2 * i)
                for c in range(HC):
                    pe.wait_ge(M["gl_done"], HC * i + c + 1)
                    for s in range(BS):
                        for j, (wp, gp) in enumerate(three(w2_sp, g_sp)):
                            mm = pe.matmul(bank[6 + s // 2][:, (s % 2) * E:(s % 2 + 1) * E], gp[:, c, s * P:(s + 1) * P], wp[:, c, :],
                                           start=(c == 0 and s % 2 == 0 and j == 0), stop=(c == HC - 1 and j == 2),
                                           skip_group_check=True)
                mm.then_inc(M["y_ps"], 1)

            turn_rows(0, 0, 0)
            def two_blocks(q):
                for par in range(2):
                    layer1(2 * q + par)
                    turn_rows(2 * q + par + 1, 1 - par, q + par)
                    layer2(2 * q + par)

            two_blocks(0)
            with pe.Fori(1, (NT - 1) // 2) as q:
                two_blocks(q)
            layer1(NT - 1)
            layer2(NT - 1)

        @block.vector
        def _(dve):
            dve.wait_ge(M["wt_hi"], 2)
            dve.wait_ge(M["wt_in"], 32)
            dve.tensor_tensor(wt_sp[1][:, 0:KT, :], wt_f[:, 0:KT, :], f32(wt_sp[0][:, 0:KT, :]), ALU.subtract).then_inc(M["wt_lo"], 1)
            dve.tensor_tensor(wt_sp[1][0:KREM, KT, :], wt_f[0:KREM, KT, :], f32(wt_sp[0][0:KREM, KT, :]), ALU.subtract).then_inc(M["wt_lo"], 1)
            dve.wait_ge(M["c_in"], 64)

            def split_lo(p, par):
                b = 2 * p + par
                dve.wait_ge(M["xt_hi"], 2 * (b + 1))
                dve.wait_ge(M[f"xt_in{par}"], 32 * (p + 1))
                hi, lo = xt_sp[par]
                dve.tensor_tensor(lo[:, 0:KT, :], xt_f[par][:, 0:KT, :], f32(hi[:, 0:KT, :]), ALU.subtract).then_inc(M[f"xt_lo{par}"], 1)
                dve.tensor_tensor(lo[0:KREM, KT, :], xt_f[par][0:KREM, KT, :], f32(hi[0:KREM, KT, :]), ALU.subtract).then_inc(M[f"xt_lo{par}"], 1)

            def norm(src, st_, mv_, rs_, sems, base):
                for s in range(NS):
                    src[2](s)
                    dve.bn_stats(st_[:, s, :], src[0](s)).then_inc(M[sems[0]], 1)
                dve.wait_ge(M[sems[0]], NS * base + NS)
                plain(dve)
                for s in range(NS):
                    dve.bn_aggr(mv_[:, s, :], st_[:, s, :]).then_inc(M[sems[1]], 1)
                dve.wait_ge(M[sems[1]], NS * base + NS)
                dve.tensor_scalar(rs_[:, :, 0], mv_[:, :, 1], EPS, None, ALU.add).then_inc(M[sems[2]], 1)
                dve.wait_ge(M[sems[3]], base + 1)

            def embed(p, par):
                b = 2 * p + par
                norm((lambda s: bank[2 * par + s][:, 0:E], None, lambda s: dve.wait_ge(M[f"tok_ps{par}"], NS * p + s + 1)),
                     st1[par], mv1[par], rs1[par], ("s1_st", "s1_mv", "s1_ve", "s1_rs"), b)
                for s in range(NS):
                    dve.tensor_scalar(hn1[par][:, s, :], bank[2 * par + s][:, 0:E], mv1[par][:, s, 0:1], rs1[par][:, s, :],
                                      ALU.subtract, ALU.mult).then_inc(M[f"s1_hn{par}"], 1)
                dve.wait_ge(M[f"h_out{par}"], 16 * p)
                for s in range(NS):
                    dve.wait_ge(M[f"s1_hn{par}"], NS * p + s + 1)
                    dve.tensor_tensor(h1[par][:, s, :], hn1[par][:, s, :], gammaB[:, :], ALU.mult).then_inc(M["s1_h"], 1)
                norm((lambda s: h1[par][:, s, :], None, lambda s: dve.wait_ge(M["s1_h"], NS * b + s + 1)),
                     st1[par], mv1[par], rs1[par], ("s1_st2", "s1_mv2", "s1_ve2", "s1_rs2"), b)
                dve.wait_ge(M[f"s1_tps{par}"], p)
                for s in range(NS):
                    dve.tensor_scalar(xn1[par][:, s, :], h1[par][:, s, :], mv1[par][:, s, 0:1], rs1[par][:, s, :],
                                      ALU.subtract, ALU.mult).then_inc(M["s1_xn"], 1)

            def decay_logits(p, par):
                b = 2 * p + par
                dve.wait_ge(M[f"s1_aps{par}"], p + 1)
                dve.tensor_tensor(z_all[:, bass.ds(2 * b, NS), :], bank[6 + par][:, 0:NS * H].rearrange("p (s n) -> p s n", s=NS),
                                  baB[:, :].rearrange("p (a n) -> p a n", a=1).broadcast_to([P, NS, H]), ALU.add).then_inc(M[f"s1_z{par}"], 1)

            for par in range(2):
                split_lo(0, par)
            def two_images(p):
                embed(p, 0)
                embed(p, 1)
                split_lo(p + 1, 0)
                split_lo(p + 1, 1)
                decay_logits(p, 0)
                decay_logits(p, 1)

            two_images(0)
            with dve.Fori(1, B // 2 - 1) as p:
                two_images(p)
            embed(B // 2 - 1, 0)
            embed(B // 2 - 1, 1)
            decay_logits(B // 2 - 1, 0)
            decay_logits(B // 2 - 1, 1)

            for i in range(5):
                dve.wait_ge(M["ws_hi"], i + 1)
                dve.tensor_tensor(w_parts[i][1].rearrange("p k n -> p (k n)"), stage_w[i % 2],
                                  f32(w_parts[i][0].rearrange("p k n -> p (k n)")), ALU.subtract).then_inc(M["ws_lo"], 1)

            zf = z_all[:, :, :].rearrange("p t n -> p (t n)")
            for par in range(2):
                dve.wait_ge(M[f"s1_z{par}"], B // 2)
            dve.wait_ge(M["sp_l"], 1)
            dve.tensor_scalar(zl[:, :], zf, 0.0, None, ALU.max).then_inc(M["sp_m"], 1)
            dve.wait_ge(M["sp_m"], 1)
            dve.scalar_tensor_tensor(out=la_all[:, :, :].rearrange("p t n -> p (t n)"), in0=zl[:, :], scalar=-1.0,
                                     in1=za[:, :], op0=ALU.mult, op1=ALU.subtract).then_inc(M["sp_la"], 1)
            dve.wait_ge(M["g_in"], 16 * 11)
            dve.tensor_scalar(gnwh[:, :], gnw[:, :], 0.5, None, ALU.mult).then_inc(M["gnh"], 1)
            dve.tensor_scalar(gnbh[:, :], gnb[:, :], 0.5, None, ALU.mult).then_inc(M["gnh"], 1)
            dve.memset(taken[:, :], 0.0).then_inc(M["gnh"], 1)
            dve.wait_ge(M["gnh"], 3)

            def silu(b, c):
                dve.wait_ge(M["tq_done"], NP * b + c + 1)
                dve.wait_ge(M["s_ps"], H * b + max(2 * c - 2, 0))
                dve.scalar_tensor_tensor(out=qk_s[c % 2][:, :], in0=tq[:, :], scalar=1.0, in1=bank[0][:, :],
                                         op0=ALU.add, op1=ALU.mult).then_inc(M["silu_done"], 1)

            def decayed(b, c, h):
                dve.wait_ge(M["s_ps"], H * b + h + 1)
                dve.wait_ge(M["exp_done"], H * b + h + 1)
                dve.wait_ge(M["o_ps"], NP * b + c)
                dve.tensor_tensor(att[h % 2][:, :], bank[4 + h % 2][:, 0:LW], dec[h % 2][:, :], ALU.mult).then_inc(M["mult_done"], 1)

            def head_stats(b, c, par):
                dve.wait_ge(M["o_done"], NP * b + c + 1)
                dve.wait_ge(M["gmv_done"], NP * b + c)
                dve.bn_stats(gst[:, :], osb[par][:, c, :]).then_inc(M["gst_done"], 1)
                dve.wait_ge(M["gst_done"], NP * b + c + 1)
                if c == 0 and not (isinstance(b, int) and b == 0):
                    dve.wait_ge(M["gt2_done"], b)
                plain(dve)
                dve.bn_aggr(gmv[:, c, :], gst[:, :]).then_inc(M["gmv_done"], 1)

            def spread(pb):
                dve.wait_ge(M["gn1_ps"], pb + 1)
                dve.tensor_copy(gm[:, :], bank[7][:, 0:NP]).then_inc(M["gn_step"], 1)
                dve.wait_ge(M["gn_step"], 6 * pb + 1)
                dve.wait_ge(M["gmv_done"], NP * (pb + 1))
                dve.tensor_tensor(gd[:, :], gmv[:, :, 0], gm[:, :], ALU.subtract).then_inc(M["gn_step"], 1)
                dve.wait_ge(M["gn_step"], 6 * pb + 2)
                dve.wait_ge(M["gn2_ps"], pb)
                dve.tensor_tensor(gt[:, :], gd[:, :], gd[:, :], ALU.mult).then_inc(M["gn_step"], 1)
                dve.wait_ge(M["gn_step"], 6 * pb + 3)
                dve.tensor_tensor(gt[:, :], gt[:, :], gmv[:, :, 1], ALU.add).then_inc(M["gt2_done"], 1)

            def affine(pb):
                dve.wait_ge(M["gn2_ps"], pb + 1)
                dve.tensor_scalar(gr[:, :], bank[7][:, 0:NP], 16 * EPS, None, ALU.add).then_inc(M["gv_done"], 1)
                dve.wait_ge(M["gr_done"], pb + 1)
                dve.tensor_tensor(gsc[:, :], gr[:, :], gnwh[:, :], ALU.mult).then_inc(M["gn_step"], 1)
                dve.wait_ge(M["gn_step"], 6 * pb + 4)
                dve.tensor_tensor(gd[:, :], gm[:, :], gsc[:, :], ALU.mult).then_inc(M["gn_step"], 1)
                dve.wait_ge(M["gn_step"], 6 * pb + 5)
                dve.tensor_tensor(gbi[:, :], gnbh[:, :], gd[:, :], ALU.subtract).then_inc(M["gn_step"], 1)
                dve.wait_ge(M["gn_step"], 6 * pb + 6)

            def gated(pb, par, j):
                dve.wait_ge(M["o_done"], NP * (pb + 1))
                for c in range(PQ * j, PQ * j + PQ):
                    dve.tensor_scalar(yn[:, c, :], osb[par][:, c, :], gsc[:, c:c + 1], gbi[:, c:c + 1],
                                      ALU.mult, ALU.add).then_inc(M["yn_done"], 1)
                dve.wait_ge(M["yn_done"], NP * pb + PQ * (j + 1))
                dve.wait_ge(M["tg_done"], NP * (pb + 1))
                dve.wait_ge(M["yh_done"], 2 * pb + j)
                cs = slice(PQ * j, PQ * j + PQ)
                dve.scalar_tensor_tensor(out=yf[:, cs, :], in0=tg[par][:, cs, :], scalar=1.0, in1=yn[:, cs, :],
                                         op0=ALU.add, op1=ALU.mult).then_inc(M["yf_done"], 1)

            def y_lo(pb, j):
                cs = slice(PQ * j, PQ * j + PQ)
                dve.wait_ge(M["yh_done"], 2 * pb + j + 1)
                dve.tensor_tensor(y_sp[1][:, cs, :], yf[:, cs, :], f32(y_sp[0][:, cs, :]), ALU.subtract).then_inc(M["yl_done"], 1)

            def residual(pb):
                dve.wait_ge(M["wo_ps"], pb + 1)
                dve.wait_ge(M["hb_in"], 16 * (pb + 1))
                dve.wait_ge(M["h2_out"], 16 * pb)
                dve.tensor_tensor(h2[:, :, :].rearrange("p s n -> p (s n)"), bank[7][:, :], hb[:, :], ALU.add).then_inc(M["h2_done"], 1)
                norm((lambda s: h2[:, s, :], None, lambda s: dve.wait_ge(M["h2_done"], pb + 1)), st, mv, rs, ("b_st", "b_mv", "b_ve", "b_rs"), pb)
                dve.wait_ge(M["scat"], 16 * NS * TOPK * pb)
                for s in range(NS):
                    dve.tensor_scalar(xn2[:, s, :], h2[:, s, :], mv[:, s, 0:1], rs[:, s, :], ALU.subtract, ALU.mult).then_inc(M["b_xn"], 1)

            def choose(pb):
                dve.wait_ge(M["lg_ps"], pb + 1)
                dve.tensor_copy(lg[:, :, :].rearrange("p s n -> p (s n)"), bank[7][:, 0:NS * X]).then_inc(M["lg_done"], 1)
                dve.wait_ge(M["lg_done"], pb + 1)
                plain(dve)
                for s in range(NS):
                    dve.max(top[:, s, :], lg[:, s, :]).then_inc(M["top_done"], 1)
                dve.wait_ge(M["top_done"], NS * (pb + 1))
                dve.tensor_scalar(ntop[:, :, 0], top[:, :, 0], -1.0, None, ALU.mult).then_inc(M["ntop_done"], 1)
                for s in range(NS):
                    dve.max_index(topi[:, s, :], top[:, s, :], lg[:, s, :]).then_inc(M["topi_done"], 1)
                dve.wait_ge(M["topi_done"], NS * (pb + 1))
                dve.tensor_copy(idxf[:, :, :], topi[:, :, 0:TOPK]).then_inc(M["idxf_done"], 1)
                dve.wait_ge(M["idxf_done"], pb + 1)
                for s in range(NS):
                    for k in range(TOPK):
                        dve.tensor_scalar(pick[:, s, k, :], iota8[:, :], idxf[:, s, k:k + 1], None, ALU.is_equal).then_inc(M["pick_done"], 1)
                dve.wait_ge(M["pick_done"], NS * TOPK * (pb + 1))
                dve.tensor_tensor(both[:, :, :], pick[:, :, 0, :], pick[:, :, 1, :], ALU.add).then_inc(M["both_done"], 1)

            def weigh(pb):
                dve.wait_ge(M["tope_done"], NS * (pb + 1))
                dve.reciprocal(trec[:, :, 0], tsum[:, :, 0]).then_inc(M["trec_done"], 1)
                dve.wait_ge(M["trec_done"], pb + 1)
                wrow = w_all[:, bass.ds(pb, 1), :].rearrange("p a (s k) -> p (a s) k", s=NS)
                dve.tensor_tensor(wrow, tope[:, :, 0:TOPK], trec[:, :, :].broadcast_to([P, NS, TOPK]), ALU.mult).then_inc(M["wall_done"], 1)

            def place(pb):
                dve.wait_ge(M["rk_ps"], pb + 1)
                dve.wait_ge(M["taken_done"], pb)
                dve.tensor_tensor(rank[:, :, :], bank[7][:, 0:NS * X].rearrange("p (s n) -> p s n", s=NS),
                                  taken[:, :].rearrange("p (a n) -> p a n", a=1).broadcast_to([P, NS, X]), ALU.add).then_inc(M["rank_done"], 1)
                dve.wait_ge(M["rank_done"], pb + 1)
                dve.tensor_tensor(taken[:, :], bank[7][:, 2 * X:3 * X], taken[:, :], ALU.add).then_inc(M["taken_done"], 1)
                for s in range(NS):
                    for k in range(TOPK):
                        j = TOPK * s + k
                        dve.wait_ge(M["rsel_done"], NS * TOPK * pb + j)
                        dve.tensor_tensor_reduce(junk[:, :], rank[:, s, :], pick[:, s, k, :], 1.0, 0.0, ALU.mult, ALU.add,
                                                 rsel[:, j:j + 1]).then_inc(M["rsel_done"], 1)
                dve.wait_ge(M["rsel_done"], NS * TOPK * (pb + 1))
                dve.wait_ge(M["scat"], 16 * NS * TOPK * pb)
                dve.scalar_tensor_tensor(out=slot[:, :], in0=idxf[:, :, :].rearrange("p s k -> p (s k)"), scalar=float(CAP), in1=rsel[:, :],
                                         op0=ALU.mult, op1=ALU.add).then_inc(M["slot_done"], 1)
                dve.wait_ge(M["slot_done"], pb + 1)
                dve.tensor_copy(slots_all[:, bass.ds(pb, 1), :].rearrange("p a n -> p (a n)"), slot[:, :])
                dve.tensor_copy(idx_all[:, bass.ds(pb, 1), :].rearrange("p a n -> p (a n)"), idxf[:, :, :].rearrange("p s k -> p (s k)")).then_inc(M["slotc_done"], 1)

            def image(b, par, post):
                dve.wait_ge(M["xh_done"], b + 1)
                dve.tensor_tensor(xn_sp[1].rearrange("p k n -> p (k n)"), xs[:, :], f32(xn_sp[0].rearrange("p k n -> p (k n)")),
                                  ALU.subtract).then_inc(M["xl_done"], 1)
                dve.wait_ge(M["cum_ps"], b + 1)
                dve.wait_ge(M["ct_ps"], b)
                cps = bank[7][:, 0:NS * H].rearrange("p (s n) -> p s n", s=NS)
                dve.tensor_copy(ccs[:, :, 0:H].bitcast(F32R), cps).then_inc(M["cc_hi"], 1)
                dve.wait_ge(M["cc_hi"], b + 1)
                dve.tensor_tensor(ccs[:, :, H:2 * H], cps, ccs[:, :, 0:H], ALU.subtract).then_inc(M["cc_lo"], 1)
                dve.wait_ge(M["exp_done"], H * b)
                dve.tensor_scalar(ncum[:, :, :], cps, -1.0, None, ALU.mult).then_inc(M["ncum_done"], 1)
                for i in range(2):
                    dve.wait_ge(M["v_ps"], 4 * b + 3 + i)
                    if i == 0:
                        dve.wait_ge(M["o_ps"], NP * b)
                    dve.tensor_copy(v_sb[:, 1, i * 512:(i + 1) * 512], bank[4 + i][:, :]).then_inc(M["v_dve"], 1)
                silu(b, 0)
                if post:
                    head_stats(b - 1, NP - 1, 1 - par)
                for c in range(NP):
                    if post and c == 0:
                        spread(b - 1)
                    decayed(b, c, 2 * c)
                    decayed(b, c, 2 * c + 1)
                    if post and c == 0:
                        affine(b - 1)
                    if c + 1 < NP:
                        silu(b, c + 1)
                    if c >= 1:
                        head_stats(b, c - 1, par)
                    if post and c == 0:
                        gated(b - 1, 1 - par, 0)
                    if post and c == 1:
                        y_lo(b - 1, 0)
                        gated(b - 1, 1 - par, 1)
                    if post and c == 2:
                        y_lo(b - 1, 1)
                    if post and c == 4:
                        residual(b - 1)
                    if post and c == 6:
                        choose(b - 1)
                    if post and c == 7:
                        weigh(b - 1)
                        place(b - 1)

            image(0, 0, False)
            image(1, 1, True)
            with dve.Fori(1, B // 2) as p:
                image(2 * p, 0, True)
                image(2 * p + 1, 1, True)
            head_stats(B - 1, NP - 1, 1)
            spread(B - 1)
            affine(B - 1)
            for j in range(2):
                gated(B - 1, 1, j)
                y_lo(B - 1, j)
            residual(B - 1)
            choose(B - 1)
            weigh(B - 1)
            place(B - 1)

            tbc = [0]

            def tb(ins):
                tbc[0] += 1
                ins.then_inc(M["tb"], 1)
                dve.wait_ge(M["tb"], tbc[0])

            cnt = taken[:, :]
            dve.wait_ge(M["taken_done"], B)
            tb(dve.tensor_tensor(tmp64[:, :, :], cnt.rearrange("p (n a) -> p n a", a=1).broadcast_to([P, X, NBLK]),
                                 iob[:, :].rearrange("p (n a) -> p n a", a=NBLK), ALU.is_gt))
            tb(dve.tensor_reduce(nb[:, :], tmp64[:, :, :], AX.X, ALU.add))
            tb(dve.tensor_tensor(tmp64[:, :, :], nb[:, :].rearrange("p (a n) -> p a n", a=1).broadcast_to([P, X, X]),
                                 tri8[:, :].rearrange("p (a n) -> p a n", a=X), ALU.mult))
            tb(dve.tensor_reduce(cb[:, :], tmp64[:, :, :], AX.X, ALU.add))
            tb(dve.tensor_tensor(cmp[:, :, :], cb[:, :].rearrange("p (a n) -> p a n", a=1).broadcast_to([P, NT, X]),
                                 til[:, :].rearrange("p (a n) -> p a n", a=NT), ALU.is_le))
            tb(dve.tensor_tensor(cmn[:, :, :], cmp[:, :, :], nb[:, :].rearrange("p (a n) -> p a n", a=1).broadcast_to([P, NT, X]), ALU.mult))
            tb(dve.tensor_reduce(te[:, :], cmp[:, :, :], AX.X, ALU.add))
            tb(dve.tensor_reduce(tst[:, :], cmn[:, :, :], AX.X, ALU.add))
            tiles = til[:, :].rearrange("p (a n) -> p a n", a=NT)[:, :, 0]
            tb(dve.tensor_scalar(tva[:, :], te[:, :], float(X), None, ALU.is_lt))
            tb(dve.tensor_tensor(te[:, :], te[:, :], tva[:, :], ALU.mult))
            tb(dve.tensor_tensor(tr0[:, :], tiles, tst[:, :], ALU.subtract))
            tb(dve.tensor_tensor(tr0[:, :], tr0[:, :], tva[:, :], ALU.mult))
            tb(dve.tensor_scalar(tr0[:, :], tr0[:, :], float(BLK), None, ALU.mult))
            tb(dve.scalar_tensor_tensor(out=tr0[:, :], in0=te[:, :], scalar=float(CAP), in1=tr0[:, :], op0=ALU.mult, op1=ALU.add))
            tb(dve.tensor_tensor(dlt[:, :], cb[:, :], nb[:, :], ALU.subtract))
            tb(dve.tensor_scalar(dlt[:, :], dlt[:, :], float(BLK), None, ALU.mult))
            tb(dve.scalar_tensor_tensor(out=dlt[:, :], in0=iota8[:, :], scalar=-float(CAP), in1=dlt[:, :], op0=ALU.mult, op1=ALU.add))
            dve.tensor_copy(tab[:, 0:NT], te[:, :])
            dve.tensor_copy(tab[:, NT:2 * NT], tr0[:, :])
            tb(dve.scalar_tensor_tensor(out=padf[:, :], in0=iota8[:, :], scalar=float(CAP), in1=cnt, op0=ALU.mult, op1=ALU.add))
            tb(dve.tensor_copy(padi[:, :], padf[:, :]))

            nch = B * NS * TOPK
            dve.wait_ge(M["slotc_done"], B)
            idf = idx_all[:, :, :].rearrange("p b (j a) -> p (b j) a", a=1).broadcast_to([P, nch, X])
            tb(dve.tensor_tensor(onx[:, :, :], idf, iota8[:, :].rearrange("p (a n) -> p a n", a=1).broadcast_to([P, nch, X]), ALU.is_equal))
            tb(dve.tensor_tensor(onx[:, :, :], onx[:, :, :], dlt[:, :].rearrange("p (a n) -> p a n", a=1).broadcast_to([P, nch, X]), ALU.mult))
            tb(dve.tensor_reduce(dsel[:, :], onx[:, :, :], AX.X, ALU.add))
            tb(dve.tensor_tensor(yrow[:, :], slots_all[:, :, :].rearrange("p b j -> p (b j)"), dsel[:, :], ALU.add))

            def w_lo(name, parts, staged, par, i):
                dve.wait_ge(M[f"{name}_hi"], i + 1)
                dve.tensor_tensor(parts[1].rearrange("p k n -> p (k n)"), staged[par], f32(parts[0].rearrange("p k n -> p (k n)")),
                                  ALU.subtract).then_inc(M[f"{name}_lo"], 1)

            def x_lo(i):
                for k in range(EC):
                    dve.wait_ge(M["xe_hi"], EC * i + k + 1)
                    dve.tensor_tensor(xe_sp[1][:, k, :], bank[k][:, :], f32(xe_sp[0][:, k, :]), ALU.subtract).then_inc(M["xe_lo"], 1)

            def hidden_lo(i, c):
                dve.wait_ge(M["gh_done"], HC * i + c + 1)
                dve.tensor_tensor(g_sp[1][:, c, :], gel[c % 2], f32(g_sp[0][:, c, :]), ALU.subtract).then_inc(M["gl_done"], 1)

            def keep_y(i, par, n):
                dve.wait_ge(M["y_ps"], i + 1)
                dve.wait_ge(M[f"y_out{par}"], 16 * n)
                for m in range(2):
                    dve.tensor_tensor(yo[par][:, 2 * m:2 * m + 2, :], bank[6 + m][:, :].rearrange("p (s n) -> p s n", s=2),
                                      b2_sb[par][:, :].rearrange("p (a n) -> p a n", a=1).broadcast_to([P, 2, E]), ALU.add).then_inc(M["y_done"], 1)

            def blockrow(i, par, n, last):
                for c in range(HC):
                    hidden_lo(i, c)
                    if c == 1:
                        w_lo("w2", w2_sp, w2_f, par, i)
                if not last:
                    x_lo(i + 1)
                    w_lo("w1", w1_sp, w1_f, 1 - par, i + 1)
                keep_y(i, par, n)

            x_lo(0)
            w_lo("w1", w1_sp, w1_f, 0, 0)
            def two_blocks(q):
                blockrow(2 * q, 0, q, False)
                blockrow(2 * q + 1, 1, q, False)

            two_blocks(0)
            with dve.Fori(1, (NT - 1) // 2) as q:
                two_blocks(q)
            blockrow(NT - 1, 0, (NT - 1) // 2, True)

            def index(t):
                for k in range(TOPK):
                    if t >= NG and k == 0:
                        dve.wait_ge(M[f"ga_in{t % NG}"], 32 * (t // NG))
                    dve.tensor_copy(slc[2 * (t % NG) + k][:, :], yrow[:, TOPK * t + k:TOPK * t + k + 1])\
                       .then_inc(M["slc_done"], 1)

            dve.wait_ge(M["slotc_done"], B)
            dve.wait_ge(M["wall_done"], B)
            for t in range(NG):
                index(t)
            for t in range(T // P):
                r = t % NG
                w = [w_all[:, t // NS, TOPK * (t % NS) + k:TOPK * (t % NS) + k + 1] for k in range(TOPK)]
                dve.wait_ge(M[f"ga_in{r}"], 32 * (t // NG + 1))
                dve.wait_ge(M[f"hf_in{r}"], 16 * (t // NG + 1))
                dve.scalar_tensor_tensor(out=f1[r], in0=ga[r], scalar=w[0], in1=hf[r], op0=ALU.mult, op1=ALU.add).then_inc(M["f1_done"], 1)
                dve.wait_ge(M["f1_done"], t + 1)
                if t >= NG:
                    dve.wait_ge(M[f"o_out{r}"], 16 * (t // NG))
                dve.scalar_tensor_tensor(out=f2[r], in0=gb[r], scalar=w[1], in1=f1[r], op0=ALU.mult, op1=ALU.add).then_inc(M["f2_done"], 1)
                if t + NG < T // P:
                    index(t + NG)


_INS = ['x', 'L0_tok_W', 'L0_tok_gamma', 'L0_attn_Wq', 'L0_attn_Wk', 'L0_attn_Wv', 'L0_attn_Wg', 'L0_attn_Wa',
        'L0_attn_ba', 'L0_attn_Wo', 'L0_attn_gn_w', 'L0_attn_gn_b', 'L0_ffn_w_router', 'L0_ffn_w1', 'L0_ffn_b1',
        'L0_ffn_w2', 'L0_ffn_b2']


def constants():
    i = np.arange(P)
    sel = np.zeros((2 * H, H, P), np.float32)
    for h in range(H):
        sel[h, h] = sel[H + h, h] = 1
    before = np.where(i[:, None] <= i[None, :], 0.0, -1e30)
    n = np.arange(X)
    return {
        "c_ident": np.eye(P, dtype=np.float32),
        "c_upper": (i[:, None] <= i[None, :]).astype(np.float32),
        "c_ones": np.ones((P, P), np.float32),
        "c_strict": (i[:, None] < i[None, :]).astype(np.float32),
        "c_half": ((i[:, None] // D == i[None, :] // D) / D).astype(np.float32),
        "c_sel": sel.reshape(2 * H, H * P),
        "c_mask": np.tile(before, (1, 2)).astype(np.float32),
        "c_iota": np.tile(n.astype(np.float32), (P, 1)),
        "c_blk": np.tile(np.arange(NBLK, dtype=np.float32) * BLK, (1, X)).reshape(1, X * NBLK),
        "c_tri8": (n[None, :] <= n[:, None]).astype(np.float32).reshape(1, X * X),
        "c_til": np.repeat(np.arange(NT, dtype=np.float32), X).reshape(1, NT * X),
    }


def laid_out(inputs):
    a = {n: np.asarray(inputs[n]) for n in _INS}
    side = SIDE // PATCH
    a['x'] = a['x'].reshape(B, C, side, PATCH, side, PATCH).transpose(1, 3, 5, 0, 2, 4).reshape(FEAT, T)
    a['L0_attn_gn_w'] = a['L0_attn_gn_w'].reshape(NP, P).T
    a['L0_attn_gn_b'] = a['L0_attn_gn_b'].reshape(NP, P).T
    a['L0_ffn_b1'] = a['L0_ffn_b1'].reshape(X, HC, P).transpose(0, 2, 1)
    return {n: np.ascontiguousarray(v) for n, v in a.items()}


def kernel(**inputs):
    import concourse.bacc as _bacc
    from concourse.bass_utils import run_bass_kernel_spmd as _run

    nc = _bacc.Bacc("TRN2", target_bir_lowering=False, num_devices=1)
    arrays, args = {}, []
    for name, a in {**laid_out(inputs), **constants()}.items():
        arrays[f"in_{name}"] = a
        args.append(nc.dram_tensor(f"in_{name}", a.shape, mybir.dt.from_np(a.dtype), kind="ExternalInput").ap())
    out = nc.dram_tensor("out_0", (B, S, E), F32, kind="ExternalOutput").ap()
    vit_layer(nc, *args, out)
    r = _run(nc, [arrays], core_ids=[0])
    return r.results[0]["out_0"]
```

```python
from contextlib import ExitStack

import numpy as np
import concourse.bass as bass
from concourse import mybir

F32 = mybir.dt.float32
F32R = mybir.dt.float32r
BF16 = mybir.dt.bfloat16
I32 = mybir.dt.int32
U32 = mybir.dt.uint32
ALU = mybir.AluOpType
ACT = mybir.ActivationFunctionType
AX = mybir.AxisListType

P = 128
B = 16
S = 256
NS = S // P
C, PATCH, SIDE = 5, 8, 128
FEAT = C * PATCH * PATCH
KT = FEAT // P
KREM = FEAT - KT * P
E = 256
EC = E // P
H, D = 16, 64
DI = H * D
NP = DI // P
PQ = NP // 2
X = 8
HID = 1024
HC = HID // P
TOPK = 2
T = B * S
EPS = 1e-5
BLK = 512
BS = BLK // P
CAP = T + BLK
NBLK = T // BLK
HB = 4
NT = (T * TOPK + X * (BLK - 1)) // BLK
LW = S + P


def vit_layer(nc, xT, w_tok, gamma, wq, wk, wv, wg, wa, ba, wo, gn_w, gn_b,
              w_router, w1, b1, w2, b2,
              ident_d, upper_d, ones_d, strict_d, half_d, sel_d, mask_d, iota_d, blk_d, tri8_d, til_d, out):
    with ExitStack() as ctx:
        def sb(name, shape, dt=F32):
            return ctx.enter_context(nc.sbuf_tensor(name, shape, dt))

        def sem(name):
            return ctx.enter_context(nc.semaphore(name))

        h_d = nc.dram_tensor("h_scratch", (B, P, NS * E), F32).ap()
        h2_d = nc.dram_tensor("h2_scratch", (B, P, NS * E), F32).ap()
        lists_d = nc.dram_tensor("expert_rows", (X * CAP, E), F32).ap()
        y_d = nc.dram_tensor("expert_out", (NT * BLK, E), F32).ap()

        ident = sb("ident", [P, P])
        upper = sb("upper", [P, P])
        ones = sb("ones", [P, P])
        strict = sb("strict", [P, P])
        half = sb("half", [P, P])
        sel_r = sb("sel_r", [2 * H, H], F32R)
        identb = sb("identb", [P, P], BF16)
        maskb = sb("maskb", [P, 2 * P], BF16)
        iota8 = sb("iota8", [P, X])
        gammaB = sb("gammaB", [P, E])
        baB = sb("baB", [P, H])
        wa_sb = sb("wa_sb", [P, EC, H])
        wr_sb = sb("wr_sb", [P, EC, X])
        gnw = sb("gnw", [P, NP])
        gnb = sb("gnb", [P, NP])
        gnwh = sb("gnwh", [P, NP])
        gnbh = sb("gnbh", [P, NP])

        big_r = sb("big_r", [P, 20480], F32R)
        wsp = [[big_r[:, (2 * i + j) * 2048:(2 * i + j + 1) * 2048].rearrange("p (k n) -> p k n", k=EC)
                for j in range(2)] for i in range(4)]
        wo_sp = [big_r[:, 16384 + j * 2048:16384 + (j + 1) * 2048].rearrange("p (k n) -> p k n", k=NP)
                 for j in range(2)]
        w1_sp = [big_r[:, j * 2048:(j + 1) * 2048].rearrange("p (k n) -> p k n", k=EC) for j in range(2)]
        w2_sp = [big_r[:, (2 + j) * 2048:(3 + j) * 2048].rearrange("p (k n) -> p k n", k=HC) for j in range(2)]
        g_sp = [big_r[:, 8192 + j * 4096:8192 + (j + 1) * 4096].rearrange("p (k n) -> p k n", k=HC) for j in range(2)]
        xe_sp = [big_r[:, 16384 + j * 1024:16384 + (j + 1) * 1024].rearrange("p (k n) -> p k n", k=EC) for j in range(2)]

        y_sp = [sb(f"y_sp{j}", [P, NP, S], F32R) for j in range(2)]
        xn_sp = [sb(f"xn_sp{j}", [P, EC, S], F32R) for j in range(2)]
        xt_sp = [sb(f"xt_sp{j}", [P, KT + 1, S], F32R) for j in range(2)]
        wt_sp = [sb(f"wt_sp{j}", [P, KT + 1, E], F32R) for j in range(2)]
        xt_f = sb("xt_f", [P, KT + 1, S])

        big_f = sb("big_f", [P, 8192])
        stage_w = [big_f[:, i * 2048:(i + 1) * 2048] for i in range(2)]
        wt_f = big_f[:, 4096:4864].rearrange("p (k n) -> p k n", k=KT + 1)
        sel_f = big_f[0:2 * H, 4864:4864 + H]
        mask_f = big_f[:, 5120:5120 + 2 * P]
        tg = [big_f[:, i * 2048:(i + 1) * 2048].rearrange("p (k n) -> p k n", k=NP) for i in range(2)]
        osb = [big_f[:, 4096 + i * 2048:4096 + (i + 1) * 2048].rearrange("p (k n) -> p k n", k=NP) for i in range(2)]
        w1_f = [big_f[:, i * 2048:(i + 1) * 2048] for i in range(2)]
        w2_f = [big_f[:, 4096 + i * 2048:4096 + (i + 1) * 2048] for i in range(2)]

        mid_f = sb("mid_f", [P, 5120])
        v_sb = mid_f[:, 0:2048].rearrange("p (s n) -> p s n", s=NS)
        yf = mid_f[:, 2048:4096].rearrange("p (k n) -> p k n", k=NP)
        rows_f = [mid_f[:, i * 1024:(i + 1) * 1024].rearrange("p (s n) -> p s n", s=BS) for i in range(2)]
        gel = [mid_f[:, 2048 + i * 512:2048 + (i + 1) * 512] for i in range(2)]
        yo = [mid_f[:, 3072 + i * 1024:3072 + (i + 1) * 1024].rearrange("p (s n) -> p s n", s=BS) for i in range(2)]

        qk_s = [sb(f"qk_s{i}", [P, 2 * S]) for i in range(2)]
        tq = sb("tq", [P, 2 * S])
        dec = [sb(f"dec{i}", [P, LW]) for i in range(2)]
        att = [sb(f"att{i}", [P, LW]) for i in range(2)]
        h1 = sb("h1", [P, NS, E])
        xn1 = sb("xn1", [P, NS, E])
        xs = sb("xs", [P, EC * S])
        hb = sb("hb", [P, NS * E])
        h2 = sb("h2", [P, NS, E])
        xn2 = sb("xn2", [P, NS, E])
        xn2T = sb("xn2T", [P, EC, S])
        cumR = sb("cumR", [2 * H, LW], F32R)
        ccs = sb("ccs", [P, NS, 2 * H])
        ncum = sb("ncum", [P, NS, H])
        zb = sb("zb", [P, NS * H])
        za = sb("za", [P, NS * H])
        ze = sb("ze", [P, NS * H])
        zl = sb("zl", [P, NS * H])
        zm = sb("zm", [P, NS * H])
        la = sb("la", [P, NS, H])
        st = sb("st", [P, NS, 6])
        mv = sb("mv", [P, NS, 2])
        rs = sb("rs", [P, NS, 1])
        mhalf = sb("mhalf", [P, NP])
        st1 = sb("st1", [P, NS, 6])
        mv1 = sb("mv1", [P, NS, 2])
        st1u = sb("st1u", [P, NS, 6])
        mv1u = sb("mv1u", [P, NS, 2])
        rs1 = sb("rs1", [P, 2, NS])
        gst = sb("gst", [P, 6])
        gmv = sb("gmv", [P, NP, 2])
        gm = sb("gm", [P, NP])
        gd = sb("gd", [P, NP])
        gt = sb("gt", [P, NP])
        gr = sb("gr", [P, NP])
        gsc = sb("gsc", [P, NP])
        gbi = sb("gbi", [P, NP])
        lg = sb("lg", [P, NS, X])
        top = sb("top", [P, NS, X])
        topi = sb("topi", [P, NS, X], U32)
        tope = sb("tope", [P, NS, X])
        ntop = sb("ntop", [P, NS, 1])
        tsum = sb("tsum", [P, NS, 1])
        trec = sb("trec", [P, NS, 1])
        idxf = sb("idxf", [P, NS, TOPK])
        pick = sb("pick", [P, NS, TOPK, X])
        both = sb("both", [P, NS, X])
        rank = sb("rank", [P, NS, X])
        rsel = sb("rsel", [P, NS * TOPK])
        junk = sb("junk", [P, X])
        taken = sb("taken", [P, X])
        slot = sb("slot", [P, NS * TOPK], U32)
        slots_all = sb("slots_all", [P, B, NS * TOPK], U32)
        w_all = sb("w_all", [P, B, NS * TOPK])
        iob = sb("iob", [P, X * NBLK])
        tri8 = sb("tri8", [P, X * X])
        til = sb("til", [P, NT * X])
        tmp64 = sb("tmp64", [P, X, X])
        nb = sb("nb", [P, X])
        cb = sb("cb", [P, X])
        cmp = sb("cmp", [P, NT, X])
        cmn = sb("cmn", [P, NT, X])
        te = sb("te", [P, NT])
        tst = sb("tst", [P, NT])
        tva = sb("tva", [P, NT])
        tr0 = sb("tr0", [P, NT])
        dlt = sb("dlt", [P, X])
        idx_all = sb("idx_all", [P, B, NS * TOPK])
        onx = hb[:, :].rearrange("p (n a) -> p n a", a=X)
        dsel = sb("dsel", [P, B * NS * TOPK])
        yrow = sb("yrow", [P, B * NS * TOPK], U32)
        tab = sb("tab", [P, 2 * NT], I32)
        padf = sb("padf", [P, X])
        padi = sb("padi", [P, X], I32)
        zeros = sb("zeros", [P, E])
        b1_sb = [sb(f"b1_{i}", [P, HC]) for i in range(2)]
        b2_sb = [tq[:, i * E:(i + 1) * E] for i in range(2)]
        NG = 3
        ga, gb, hf, f1, f2 = ([mid_f[:, (5 * i + j) * E:(5 * i + j + 1) * E] for i in range(NG)] for j in range(5))

        bank = [ctx.enter_context(nc.psum_tensor(f"bank{i}", [P, 512], F32)) for i in range(8)]

        names = """
        passed mh_done c_in c_sel c_selr c_maskb ws_in0 ws_in1 ws_hi ws_lo wt_in wt_hi wt_lo g_in
        xt_in xt_hi xt_lo tok_ps s1_st s1_mv s1_u s1_v1 s1_st2 s1_mv2 s1_ve s1_rs s1_h s1_xn
        s1_tps s1_xnT s1_aps s1_z b_ve gv_done h_out
        sp_abs sp_e sp_l sp_m sp_la gnh
        xs_in xh_done xl_done cum_ps cc_hi cc_lo ncum_done ct_ps ct_copied v_ps v_act v_dve
        qk_ps g_ps tq_done tg_done silu_done d_ps exp_done s_ps mult_done o_ps o_done gst_done gmv_done
        gn1_ps gn_step gt2_done gn2_ps gr_done yn_done yf_done yh_done yl_done
        wo_ps hb_in h2_done h2_out b_st b_mv b_rs b_xn x2_ps x2_done lg_ps lg_done top_done topi_done ntop_done
        tope_done trec_done wall_done idxf_done pick_done both_done rk_ps rank_done taken_done rsel_done
        slot_done slotc_done scat
        tb zero_done pad_out
        row_in0 row_in1 w1_in0 w1_in1 w2_in0 w2_in1 b_in0 b_in1 xe_ps xe_hi xe_lo w1_hi w1_lo w2_hi w2_lo
        hid_ps gel_done gh_done gl_done y_ps y_done y_out0 y_out1
        ga_in0 ga_in1 ga_in2 hf_in0 hf_in1 hf_in2 f1_done f2_done o_out0 o_out1 o_out2
        """.split()
        M = {n: sem(n) for n in names}

        block = ctx.enter_context(nc.Block())

        def three(part_w, part_x):
            return [(part_w[0], part_x[0]), (part_w[0], part_x[1]), (part_w[1], part_x[0])]

        def f32(ap):
            return ap.bitcast(F32)

        def plain(eng):
            eng.sem_inc(M["passed"])

        W_ATT = [wq, wk, wv, wg]
        w_parts = wsp + [wo_sp]

        @block.sync
        def _(sp):
            for dst, src in ((ident[:, :], ident_d), (gammaB[:, :], gamma.rearrange("(a n) -> a n", a=1).broadcast_to([P, E])),
                             (baB[:, :], ba.rearrange("(a n) -> a n", a=1).broadcast_to([P, H])),
                             (wa_sb[:, :, :], wa.rearrange("(k p) n -> p k n", p=P))):
                sp.dma_start(dst, src).then_inc(M["c_in"], 16)
            sp.dma_start(wt_f[:, 0:KT, :], w_tok[0:KT * P, :].rearrange("(k p) n -> p k n", p=P)).then_inc(M["wt_in"], 16)
            sp.dma_start(wt_f[0:KREM, KT, :], w_tok[KT * P:FEAT, :]).then_inc(M["wt_in"], 16)

            def load_patches(n):
                sp.wait_ge(M["xt_lo"], 2 * n)
                src = xT[:, bass.ds(n * S, S)]
                sp.dma_start(xt_f[:, 0:KT, :], src[0:KT * P, :].rearrange("(k p) n -> p k n", p=P)).then_inc(M["xt_in"], 16)
                sp.dma_start(xt_f[0:KREM, KT, :], src[KT * P:FEAT, :]).then_inc(M["xt_in"], 16)

            def store_h(n):
                sp.wait_ge(M["s1_h"], NS * (n + 1))
                sp.dma_start(h_d[bass.ds(n, 1), :, :].rearrange("a p n -> (a p) n"),
                             h1[:, :, :].rearrange("p s n -> p (s n)")).then_inc(M["h_out"], 16)

            def load_h(b):
                sp.wait_ge(M["h_out"], 16 * (b + 1))
                sp.wait_ge(M["h2_done"], b)
                sp.dma_start(hb[:, :], h_d[bass.ds(b, 1), :, :].rearrange("a p n -> (a p) n")).then_inc(M["hb_in"], 16)

            def store_h2(b):
                sp.wait_ge(M["h2_done"], b + 1)
                sp.dma_start(h2_d[bass.ds(b, 1), :, :].rearrange("a p n -> (a p) n"),
                             h2[:, :, :].rearrange("p s n -> p (s n)")).then_inc(M["h2_out"], 16)

            load_patches(0)
            for i, w in enumerate(W_ATT + [wo]):
                if i >= 2:
                    sp.wait_ge(M["ws_lo"], i - 1)
                sp.dma_start(stage_w[i % 2].rearrange("p (k n) -> p k n", k=EC if i < 4 else NP),
                             w.rearrange("(k p) n -> p k n", p=P)).then_inc(M[f"ws_in{i % 2}"], 16)
            load_patches(1)
            store_h(0)
            load_patches(2)
            store_h(1)
            load_h(0)
            with sp.Fori(1, B - 2) as b:
                load_patches(b + 2)
                store_h(b + 1)
                store_h2(b - 1)
                load_h(b)
            store_h(B - 1)
            for b in range(B - 2, B):
                store_h2(b - 1)
                load_h(b)
            store_h2(B - 1)

            sp.wait_ge(M["tb"], 19)
            sp.wait_ge(M["zero_done"], 1)
            for e in range(X):
                first = sp.value_load(padi[0:1, e:e + 1], min_val=e * CAP, max_val=e * CAP + T)
                sp.dma_start(lists_d[bass.ds(first, BLK), :].rearrange("(s p) n -> p s n", p=P),
                             zeros[:, :].rearrange("p (a n) -> p a n", a=1).broadcast_to([P, BS, E])).then_inc(M["pad_out"], 16)
            sp.wait_ge(M["pad_out"], 16 * X)
            sp.wait_ge(M["scat"], 16 * NS * TOPK * B)

            def load_weights(i, par, n):
                e = sp.value_load(tab[0:1, bass.ds(i, 1)], min_val=0, max_val=X - 1)
                r = sp.value_load(tab[0:1, bass.ds(i + NT, 1)], min_val=0, max_val=X * CAP - BLK)
                sp.wait_ge(M["xe_ps"], EC * 2 * n)
                sp.dma_start(rows_f[par], lists_d[bass.ds(r, BLK), :].rearrange("(s p) n -> p s n", p=P)).then_inc(M[f"row_in{par}"], 16)
                sp.wait_ge(M["w1_lo"], 2 * n)
                sp.dma_start(w1_f[par].rearrange("p (k n) -> p k n", k=EC),
                             w1[bass.ds(e, 1), :, :].rearrange("a (k p) n -> (a p) k n", p=P)).then_inc(M[f"w1_in{par}"], 16)
                sp.wait_ge(M["gh_done"], HC * 2 * n)
                sp.dma_start(b1_sb[par][:, :], b1[bass.ds(e, 1), :, :].rearrange("a p k -> (a p) k")).then_inc(M[f"b_in{par}"], 16)
                sp.wait_ge(M["w2_lo"], 2 * n)
                sp.dma_start(w2_f[par].rearrange("p (k n) -> p k n", k=HC),
                             w2[bass.ds(e, 1), :, :].rearrange("a (k p) n -> (a p) k n", p=P)).then_inc(M[f"w2_in{par}"], 16)
                sp.wait_ge(M["y_done"], 2 * 2 * n)
                sp.dma_start(b2_sb[par][:, :], b2[bass.ds(e, 1), :].broadcast_to([P, E])).then_inc(M[f"b_in{par}"], 16)

            def store_rows(i, par):
                sp.wait_ge(M["y_done"], 2 * (i + 1))
                sp.dma_start(y_d[bass.ds(i * BLK, BLK), :].rearrange("(s p) n -> p s n", p=P), yo[par]).then_inc(M[f"y_out{par}"], 16)

            load_weights(0, 0, 0)
            def two_blocks(q):
                load_weights(2 * q + 1, 1, q)
                store_rows(2 * q, 0)
                load_weights(2 * q + 2, 0, q + 1)
                store_rows(2 * q + 1, 1)

            two_blocks(0)
            with sp.Fori(1, (NT - 1) // 2) as q:
                two_blocks(q)
            store_rows(NT - 1, 0)

            sp.wait_ge(M["h2_out"], 16 * B)

            def load_h2(t, r, n):
                sp.wait_ge(M["f1_done"], t - NG + 1) if t >= NG else None
                sp.dma_start(hf[r], h2_d[t // NS, :, (t % NS) * E:(t % NS + 1) * E]).then_inc(M[f"hf_in{r}"], 16)

            def store_out(t, r):
                sp.wait_ge(M["f2_done"], t + 1)
                sp.dma_start(out[t // NS, (t % NS) * P:(t % NS + 1) * P, :], f2[r]).then_inc(M[f"o_out{r}"], 16)

            sp.wait_ge(M["y_out0"], 16 * ((NT + 1) // 2))
            sp.wait_ge(M["y_out1"], 16 * (NT // 2))
            for t in range(T // P):
                load_h2(t, t % NG, t // NG)
                if t >= 2:
                    store_out(t - 2, (t - 2) % NG)
            store_out(T // P - 2, (T // P - 2) % NG)
            store_out(T // P - 1, (T // P - 1) % NG)
            for r in range(NG):
                sp.wait_ge(M[f"o_out{r}"], 16 * len(range(r, T // P, NG)))

        @block.gpsimd
        def _(pool):
            for n, dst in enumerate((upper, ones, strict, half)):
                pool.dma_start(dst[:, :], (upper_d, ones_d, strict_d, half_d)[n]).then_inc(M["g_in"], 16)
            pool.dma_start(sel_f, sel_d).then_inc(M["c_sel"], 16)
            pool.dma_start(iota8[:, :], iota_d).then_inc(M["g_in"], 16)
            pool.dma_start(wr_sb[:, :, :], w_router.rearrange("(k p) n -> p k n", p=P)).then_inc(M["g_in"], 16)
            pool.dma_start(gnw[:, :], gn_w).then_inc(M["g_in"], 16)
            pool.dma_start(gnb[:, :], gn_b).then_inc(M["g_in"], 16)
            pool.dma_start(iob[:, :], blk_d.broadcast_to(iob.shape)).then_inc(M["g_in"], 16)
            pool.dma_start(tri8[:, :], tri8_d.broadcast_to(tri8.shape)).then_inc(M["g_in"], 16)
            pool.dma_start(til[:, :], til_d.broadcast_to(til.shape)).then_inc(M["g_in"], 16)
            pool.memset(zeros[:, :], 0.0).then_inc(M["zero_done"], 1)
            pool.wait_ge(M["c_sel"], 16)
            pool.tensor_copy(sel_r[:, :], sel_f).then_inc(M["c_selr"], 1)
            pool.dma_start(mask_f, mask_d).then_inc(M["c_maskb"], 16)
            pool.wait_ge(M["c_maskb"], 16)
            pool.tensor_copy(maskb[:, :], mask_f).then_inc(M["c_selr"], 1)
            pool.wait_ge(M["c_in"], 64)
            pool.tensor_copy(identb[:, :], ident[:, :]).then_inc(M["c_selr"], 1)
            pool.memset(mhalf[:, :], -0.5).then_inc(M["mh_done"], 1)
            pool.wait_ge(M["mh_done"], 1)

            def rsqrt(v, given, made, n):
                pool.wait_ge(M[given], n)
                pool.tensor_tensor(v, v, mhalf[:, 0:v.shape[1]], ALU.pow).then_inc(M[made], 1)

            def scatter(b):
                for j in range(NS * TOPK):
                    if j == 0:
                        pool.wait_ge(M["slot_done"], b + 1)
                        plain(pool)
                    pool.indirect_dma_start(out=lists_d[:, :], out_offset=bass.IndirectOffsetOnAxis(ap=slot[:, j:j + 1], axis=0),
                                            in_=xn2[:, j // TOPK, :], in_offset=None).then_inc(M["scat"], 16)

            def image(b, post, post2, nxt):
                if post:
                    rsqrt(gr[:, :], "gv_done", "gr_done", b)
                if nxt:
                    rsqrt(rs1[:, :, :].rearrange("p j s -> p (j s)"), "s1_ve", "s1_rs", b + 2)
                if post2:
                    scatter(b - 2)
                if post:
                    rsqrt(rs[:, :, 0], "b_ve", "b_rs", b)

            rsqrt(rs1[:, :, :].rearrange("p j s -> p (j s)"), "s1_ve", "s1_rs", 1)
            image(0, False, False, True)
            image(1, True, False, True)
            image(2, True, True, True)
            with pool.Fori(3, B - 1) as b:
                image(b, True, True, True)
            image(B - 1, True, True, False)
            rsqrt(gr[:, :], "gv_done", "gr_done", B)
            scatter(B - 2)
            rsqrt(rs[:, :, 0], "b_ve", "b_rs", B)
            scatter(B - 1)

            pool.wait_ge(M["y_out0"], 16 * ((NT + 1) // 2))
            pool.wait_ge(M["y_out1"], 16 * (NT // 2))
            pool.wait_ge(M["tb"], 23)
            for t in range(T // P):
                r = t % NG
                if t >= NG:
                    pool.wait_ge(M["f2_done"], t - NG + 1)
                pool.indirect_dma_start(out=ga[r], out_offset=None, in_=y_d[:, :],
                                        in_offset=bass.IndirectOffsetOnAxis(ap=yrow[:, TOPK * t:TOPK * t + 1], axis=0)).then_inc(M[f"ga_in{r}"], 16)
                pool.indirect_dma_start(out=gb[r], out_offset=None, in_=y_d[:, :],
                                        in_offset=bass.IndirectOffsetOnAxis(ap=yrow[:, TOPK * t + 1:TOPK * t + 2], axis=0)).then_inc(M[f"ga_in{r}"], 16)

        @block.scalar
        def _(act):
            act.wait_ge(M["wt_in"], 32)
            act.activation(wt_sp[0][:, 0:KT, :], wt_f[:, 0:KT, :], ACT.Copy).then_inc(M["wt_hi"], 1)
            act.activation(wt_sp[0][0:KREM, KT, :], wt_f[0:KREM, KT, :], ACT.Copy).then_inc(M["wt_hi"], 1)

            def patches_hi(n):
                act.wait_ge(M["xt_in"], 32 * (n + 1))
                act.wait_ge(M["tok_ps"], n)
                act.activation(xt_sp[0][:, 0:KT, :], xt_f[:, 0:KT, :], ACT.Copy).then_inc(M["xt_hi"], 1)
                act.activation(xt_sp[0][0:KREM, KT, :], xt_f[0:KREM, KT, :], ACT.Copy).then_inc(M["xt_hi"], 1)

            def keep_xnT(n):
                act.wait_ge(M["s1_tps"], n + 1)
                act.wait_ge(M["xl_done"], n)
                act.activation(xs[:, :], bank[7][:, :], ACT.Copy).then_inc(M["s1_xnT"], 1)

            def softplus(n):
                act.wait_ge(M["s1_z"], n + 1)
                act.activation(za[:, :], zb[:, :], ACT.Abs).then_inc(M["sp_abs"], 1)
                act.wait_ge(M["sp_abs"], n + 1)
                act.activation(ze[:, :], za[:, :], ACT.Exp, scale=-1.0).then_inc(M["sp_e"], 1)
                act.wait_ge(M["sp_e"], n + 1)
                act.wait_ge(M["sp_la"], n)
                act.activation(zl[:, :], ze[:, :], ACT.Ln, bias=1.0).then_inc(M["sp_l"], 1)

            def xn_hi(n):
                act.wait_ge(M["s1_xnT"], n + 1)
                act.wait_ge(M["g_ps"], NP * n)
                act.activation(xn_sp[0][:, :, :].rearrange("p k n -> p (k n)"), xs[:, :], ACT.Copy).then_inc(M["xh_done"], 1)

            def scaled_h(n):
                act.wait_ge(M["s1_rs"], n + 1)
                act.wait_ge(M["s1_xn"], NS * (n + 1))
                for s in range(NS):
                    act.activation(h1[:, s, :], h1[:, s, :], ACT.Copy, scale=rs1[:, 0, s:s + 1]).then_inc(M["s1_h"], 1)

            patches_hi(0)
            scaled_h(0)
            for i in range(5):
                act.wait_ge(M[f"ws_in{i % 2}"], 16 * (i // 2 + 1))
                act.activation(w_parts[i][0].rearrange("p k n -> p (k n)"), stage_w[i % 2], ACT.Copy).then_inc(M["ws_hi"], 1)
                if i == 1:
                    keep_xnT(0)
            softplus(0)
            xn_hi(0)

            def tanh_qk(b, c):
                act.wait_ge(M["qk_ps"], NP * b + c + 1)
                act.wait_ge(M["silu_done"], NP * b + c)
                act.activation(tq[:, :], bank[0][:, :], ACT.Tanh, scale=0.5).then_inc(M["tq_done"], 1)

            def tanh_g(b, c, par):
                act.wait_ge(M["g_ps"], NP * b + c + 1)
                act.activation(tg[par][:, c, :], bank[1][:, 0:S], ACT.Tanh, scale=0.5).then_inc(M["tg_done"], 1)

            def decay(b, h):
                act.wait_ge(M["d_ps"], H * b + h + 1)
                act.wait_ge(M["mult_done"], H * b + max(h - 1, 0))
                act.activation(dec[h % 2][:, 0:S], bank[2 + h % 2][:, 0:S], ACT.Exp, bias=ncum[:, 0, h:h + 1])
                act.activation(dec[h % 2][:, S:LW], bank[2 + h % 2][:, S:LW], ACT.Exp, bias=ncum[:, 1, h:h + 1]).then_inc(M["exp_done"], 1)

            def keep_o(b, c, par):
                act.wait_ge(M["o_ps"], NP * b + c + 1)
                act.activation(osb[par][:, c, :], bank[6][:, 0:S], ACT.Copy).then_inc(M["o_done"], 1)

            def affined(pb, par, j):
                act.wait_ge(M["gn_step"], 6 * pb + 6)
                act.wait_ge(M["yl_done"], 2 * pb - 1 + j) if not isinstance(pb, int) or pb > 0 else None
                for c in range(PQ * j, PQ * j + PQ):
                    act.activation(yf[:, c, :], osb[par][:, c, :], ACT.Identity, scale=gsc[:, c:c + 1], bias=gbi[:, c:c + 1]).then_inc(M["yn_done"], 1)

            def y_hi(pb, j):
                act.wait_ge(M["yf_done"], 2 * pb + j + 1)
                act.wait_ge(M["wo_ps"], pb)
                act.activation(y_sp[0][:, PQ * j:PQ * j + PQ, :], yf[:, PQ * j:PQ * j + PQ, :], ACT.Copy).then_inc(M["yh_done"], 1)

            def keep_x2(pb):
                act.wait_ge(M["x2_ps"], pb + 1)
                act.wait_ge(M["lg_ps"], pb)
                act.activation(xn2T[:, :, :].rearrange("p k n -> p (k n)"), bank[7][:, :], ACT.Copy).then_inc(M["x2_done"], 1)

            def top_exp(pb):
                act.wait_ge(M["ntop_done"], pb + 1)
                act.wait_ge(M["wall_done"], pb)
                for s in range(NS):
                    act.activation(tope[:, s, :], top[:, s, :], ACT.Exp, bias=ntop[:, s, :],
                                   accum_out=tsum[:, s, :]).then_inc(M["tope_done"], 1)

            def image(b, par, post, post2, nxt):
                for i in range(2):
                    act.wait_ge(M["v_ps"], 4 * b + i + 1)
                    if i == 0:
                        act.wait_ge(M["o_ps"], NP * b)
                    act.activation(v_sb[:, 0, i * 512:(i + 1) * 512], bank[2 + i][:, :], ACT.Copy).then_inc(M["v_act"], 1)
                tanh_qk(b, 0)
                tanh_g(b, 0, par)
                act.wait_ge(M["ct_ps"], b + 1)
                act.activation(cumR[:, 0:S], bank[7][0:2 * H, 0:S], ACT.Copy)
                act.activation(cumR[:, S:LW], bank[7][0:2 * H, P:S], ACT.Copy).then_inc(M["ct_copied"], 1)
                for c in range(NP):
                    if nxt and c == 6:
                        keep_xnT(b + 1)
                    decay(b, 2 * c)
                    decay(b, 2 * c + 1)
                    if post2 and c == 0:
                        keep_x2(b - 2)
                    if nxt and c == 0:
                        patches_hi(b + 1)
                    if post and c in (2, 3):
                        affined(b - 1, 1 - par, c - 2)
                    if post and c in (4, 6):
                        y_hi(b - 1, c // 2 - 2)
                    if c == 5:
                        if nxt:
                            scaled_h(b + 1)
                        if post2:
                            top_exp(b - 2)
                    if nxt and c == 7:
                        xn_hi(b + 1)
                        softplus(b + 1)
                    if c + 1 < NP:
                        tanh_qk(b, c + 1)
                        tanh_g(b, c + 1, par)
                    keep_o(b, c, par)

            image(0, 0, False, False, True)
            image(1, 1, True, False, True)
            image(2, 0, True, True, True)
            image(3, 1, True, True, True)
            with act.Fori(2, B // 2 - 1) as p:
                image(2 * p, 0, True, True, True)
                image(2 * p + 1, 1, True, True, True)
            image(B - 2, 0, True, True, True)
            image(B - 1, 1, True, True, False)
            keep_x2(B - 2)
            affined(B - 1, 1, 0)
            affined(B - 1, 1, 1)
            top_exp(B - 2)
            y_hi(B - 1, 0)
            y_hi(B - 1, 1)
            keep_x2(B - 1)
            top_exp(B - 1)

            def w_hi(name, parts, staged, par, n, i, used, count):
                act.wait_ge(M[f"{name}_in{par}"], 16 * (n + 1))
                act.wait_ge(M[used], count)
                act.activation(parts[0].rearrange("p k n -> p (k n)"), staged[par], ACT.Copy).then_inc(M[f"{name}_hi"], 1)

            def x_hi(i):
                for k in range(EC):
                    act.wait_ge(M["xe_ps"], EC * i + k + 1)
                    act.wait_ge(M["hid_ps"], HC * i)
                    act.activation(xe_sp[0][:, k, :], bank[k][:, :], ACT.Copy).then_inc(M["xe_hi"], 1)

            def hidden(i, par, n, c):
                act.wait_ge(M["hid_ps"], HC * i + c + 1)
                if c == 0:
                    act.wait_ge(M[f"b_in{par}"], 32 * (n + 1))
                act.wait_ge(M["gl_done"], HC * i + max(c - 1, 0))
                act.activation(gel[c % 2], bank[2 + c % HB][:, :], ACT.Gelu_apprx_tanh, bias=b1_sb[par][:, c:c + 1]).then_inc(M["gel_done"], 1)
                act.wait_ge(M["gel_done"], HC * i + c + 1)
                act.wait_ge(M["y_ps"], i)
                act.activation(g_sp[0][:, c, :], gel[c % 2], ACT.Copy).then_inc(M["gh_done"], 1)

            def blockrow(i, par, n, last):
                for c in range(HC):
                    hidden(i, par, n, c)
                    if c == 1:
                        w_hi("w2", w2_sp, w2_f, par, n, i, "y_ps", i)
                if not last:
                    nn = n + (1 if par else 0)
                    x_hi(i + 1)
                    w_hi("w1", w1_sp, w1_f, 1 - par, nn, i + 1, "hid_ps", HC * (i + 1))

            x_hi(0)
            w_hi("w1", w1_sp, w1_f, 0, 0, 0, "wo_ps", B)
            def two_blocks(q):
                blockrow(2 * q, 0, q, False)
                blockrow(2 * q + 1, 1, q, False)

            two_blocks(0)
            with act.Fori(1, (NT - 1) // 2) as q:
                two_blocks(q)
            blockrow(NT - 1, 0, (NT - 1) // 2, True)

        @block.tensor
        def _(pe):
            pe.wait_ge(M["wt_lo"], 2)
            pe.wait_ge(M["c_in"], 64)

            def tokens(n, free, count):
                if free:
                    pe.wait_ge(M[free], count)
                pe.wait_ge(M["xt_lo"], 2 * (n + 1))
                for s in range(NS):
                    for k in range(KT + 1):
                        rows = P if k < KT else KREM
                        for j, (wp, xp) in enumerate(three(wt_sp, xt_sp)):
                            mm = pe.matmul(bank[7][:, s * E:(s + 1) * E], xp[0:rows, k, s * P:(s + 1) * P], wp[0:rows, k, :],
                                           start=(s == 0 and k == 0 and j == 0), stop=(k == KT and j == 2), skip_group_check=True)
                mm.then_inc(M["tok_ps"], 1)

            def turn(n, free, count):
                pe.wait_ge(M[free], count)
                pe.wait_ge(M["s1_xn"], NS * (n + 1))
                for k in range(EC):
                    for s in range(NS):
                        mm = pe.transpose(bank[7][:, k * S + s * P:k * S + (s + 1) * P], xn1[:, s, k * P:(k + 1) * P], ident[:, :])
                mm.then_inc(M["s1_tps"], 1)

            def logits(n):
                pe.wait_ge(M["s1_xnT"], n + 1)
                for s in range(NS):
                    for k in range(EC):
                        mm = pe.matmul(bank[7][:, s * H:(s + 1) * H], xs[:, k * S + s * P:k * S + (s + 1) * P], wa_sb[:, k, :],
                                       start=(k == 0), stop=(k == EC - 1))
                mm.then_inc(M["s1_aps"], 1)

            tokens(0, None, 0)
            turn(0, "s1_u", NS)
            logits(0)

            def cum(b):
                if not isinstance(b, int) or b > 1:
                    pe.wait_ge(M["h2_done"], b - 1)
                pe.wait_ge(M["sp_la"], b + 1)
                pe.matmul(bank[7][:, 0:H], upper[:, :], la[:, 0, :], start=True, stop=True)
                pe.matmul(bank[7][:, H:2 * H], ones[:, :], la[:, 0, :], start=True, stop=False)
                pe.matmul(bank[7][:, H:2 * H], upper[:, :], la[:, 1, :], start=False, stop=True).then_inc(M["cum_ps"], 1)

            def cum_rows(b):
                pe.wait_ge(M["ncum_done"], b + 1)
                for s in range(NS):
                    mm = pe.transpose(bank[7][0:2 * H, s * P:(s + 1) * P], ccs[:, s, :], ident[:, :])
                mm.then_inc(M["ct_ps"], 1)

            def values(b, s):
                pe.wait_ge(M["xl_done"], b + 1)
                for n in range(2):
                    i = 2 * s + n
                    pe.wait_ge(M["exp_done"] if s == 0 else M["mult_done"], H * b)
                    for k in range(EC):
                        for j, (wp, xp) in enumerate(three(wsp[2], xn_sp)):
                            mm = pe.matmul(bank[2 + i][:, :], xp[:, k, s * P:(s + 1) * P], wp[:, k, n * 512:(n + 1) * 512],
                                           start=(k == 0 and j == 0), stop=(k == EC - 1 and j == 2))
                    mm.then_inc(M["v_ps"], 1)

            def project(dst, w, c, m):
                for k in range(EC):
                    for j, (wp, xp) in enumerate(three(wsp[w], xn_sp)):
                        mm = pe.matmul(dst, wp[:, k, c * P:(c + 1) * P], xp[:, k, :],
                                       start=(k == 0 and j == 0), stop=(k == EC - 1 and j == 2))
                if m is not None:
                    mm.then_inc(M[m], 1)

            def qkg(b, c):
                pe.wait_ge(M["silu_done"], NP * b + c)
                project(bank[0][:, 0:S], 0, c, None)
                project(bank[0][:, S:2 * S], 1, c, "qk_ps")
                pe.wait_ge(M["tg_done"], NP * b + c)
                project(bank[1][:, 0:S], 3, c, "g_ps")

            def decays(b, h):
                if h < 2:
                    pe.wait_ge(M["v_act"], 2 * b + h + 1)
                pe.wait_ge(M["exp_done"], H * b + max(h - 1, 0))
                if h == 0:
                    pe.wait_ge(M["ct_copied"], b + 1)
                dst = bank[2 + h % 2]
                pe.matmul(dst[:, 0:LW], sel_r[:, h:h + 1].broadcast_to([2 * H, P]), cumR[:, :], start=True, stop=False)
                pe.matmul(dst[:, :].rearrange("p (a n) -> p a n", n=P)[:, 0:3:2, :], identb[:, :],
                          maskb[:, :].rearrange("p (a n) -> p a n", n=P), start=False, stop=True).then_inc(M["d_ps"], 1)

            def scores(b, c, h):
                if c == 0:
                    pe.wait_ge(M["v_dve"], 2 * b + h % 2 + 1)
                pe.wait_ge(M["mult_done"], H * b + max(h - 1, 0))
                pe.wait_ge(M["silu_done"], NP * b + c + 1)
                r = slice(D * (h % 2), D * (h % 2) + D)
                q, k = qk_s[c % 2][r, 0:S], qk_s[c % 2][r, S:2 * S]
                dst = bank[4 + h % 2]
                pe.matmul(dst[:, 0:S], k[:, 0:P], q, start=True, stop=True)
                pe.matmul(dst[:, S:LW], k[:, P:S], q[:, P:S], start=True, stop=True).then_inc(M["s_ps"], 1)

            def weighted(b, c):
                pe.wait_ge(M["o_done"], NP * b + c)
                for hh in range(2):
                    h = 2 * c + hh
                    pe.wait_ge(M["mult_done"], H * b + h + 1)
                    dst = bank[6][D * hh:D * hh + D, :]
                    pe.matmul(dst[:, 0:S], v_sb[:, 0, h * D:(h + 1) * D], att[hh][:, 0:S], start=True, stop=False)
                    mm = pe.matmul(dst[:, P:S], v_sb[:, 1, h * D:(h + 1) * D], att[hh][:, S:LW], start=False, stop=True)
                mm.then_inc(M["o_ps"], 1)

            def gn_mean(pb, free, count):
                pe.wait_ge(M[free], count)
                pe.wait_ge(M["gmv_done"], NP * (pb + 1))
                pe.matmul(bank[7][:, 0:NP], half[:, :], gmv[:, :, 0], start=True, stop=True).then_inc(M["gn1_ps"], 1)

            def gn_var(pb):
                pe.wait_ge(M["gt2_done"], pb + 1)
                pe.matmul(bank[7][:, 0:NP], half[:, :], gt[:, :], start=True, stop=True).then_inc(M["gn2_ps"], 1)

            def out_proj(pb, j, free, count):
                if j == 0:
                    pe.wait_ge(M[free], count)
                pe.wait_ge(M["yl_done"], 2 * pb + j + 1)
                for c in range(PQ * j, PQ * j + PQ):
                    for s in range(NS):
                        for q, (wp, yp) in enumerate(three(wo_sp, y_sp)):
                            mm = pe.matmul(bank[7][:, s * E:(s + 1) * E], yp[:, c, s * P:(s + 1) * P], wp[:, c, :],
                                           start=(c == 0 and s == 0 and q == 0), stop=(c == NP - 1 and q == 2),
                                           skip_group_check=True)
                if j == 1:
                    mm.then_inc(M["wo_ps"], 1)

            def turn2(pb, free, count):
                pe.wait_ge(M[free], count)
                pe.wait_ge(M["b_xn"], NS * (pb + 1))
                for k in range(EC):
                    for s in range(NS):
                        mm = pe.transpose(bank[7][:, k * S + s * P:k * S + (s + 1) * P], xn2[:, s, k * P:(k + 1) * P], ident[:, :])
                mm.then_inc(M["x2_ps"], 1)

            def route(pb, free, count):
                pe.wait_ge(M[free], count)
                pe.wait_ge(M["x2_done"], pb + 1)
                for s in range(NS):
                    for k in range(EC):
                        mm = pe.matmul(bank[7][:, s * X:(s + 1) * X], xn2T[:, k, s * P:(s + 1) * P], wr_sb[:, k, :],
                                       start=(k == 0), stop=(k == EC - 1))
                mm.then_inc(M["lg_ps"], 1)

            def ranks(pb, free, count):
                pe.wait_ge(M[free], count)
                pe.wait_ge(M["both_done"], pb + 1)
                pe.matmul(bank[7][:, 0:X], strict[:, :], both[:, 0, :], start=True, stop=True)
                pe.matmul(bank[7][:, X:2 * X], ones[:, :], both[:, 0, :], start=True, stop=False)
                pe.matmul(bank[7][:, X:2 * X], strict[:, :], both[:, 1, :], start=False, stop=True)
                pe.matmul(bank[7][:, 2 * X:3 * X], ones[:, :], both[:, 0, :], start=True, stop=False)
                pe.matmul(bank[7][:, 2 * X:3 * X], ones[:, :], both[:, 1, :], start=False, stop=True).then_inc(M["rk_ps"], 1)

            pe.wait_ge(M["g_in"], 16 * 11)
            pe.wait_ge(M["ws_lo"], 5)
            pe.wait_ge(M["c_selr"], 3)

            def image(b, post, post2, nxt):
                values(b, 0)
                cum(b)
                qkg(b, 0)
                cum_rows(b)
                values(b, 1)
                for c in range(NP):
                    decays(b, 2 * c)
                    decays(b, 2 * c + 1)
                    if post2 and c == 0:
                        turn2(b - 2, "ct_copied", b + 1)
                    if post and c == 1:
                        gn_var(b - 1)
                    if nxt and c == 6:
                        logits(b + 1)
                    scores(b, c, 2 * c)
                    scores(b, c, 2 * c + 1)
                    if c + 1 < NP:
                        qkg(b, c + 1)
                    if post and c == 0:
                        gn_mean(b - 1, *(("x2_done", b - 1) if post2 else ("ct_copied", b + 1)))
                    if nxt and c == 1:
                        tokens(b + 1, *(("gv_done", b) if post else ("ct_copied", b + 1)))
                    if post2 and c == 3:
                        route(b - 2, *(("s1_u", NS * (b + 2)) if nxt else ("gv_done", b)))
                    if nxt and c == 5:
                        turn(b + 1, *(("lg_done", b - 1) if post2 else ("s1_u", NS * (b + 2))))
                    if post2 and c == 6:
                        ranks(b - 2, *(("s1_z", b + 2) if nxt else ("lg_done", b - 1)))
                    if post and c == 7:
                        out_proj(b - 1, 0, *(("taken_done", b - 1) if post2 else ("s1_z", b + 2)))
                        out_proj(b - 1, 1, None, 0)
                    weighted(b, c)

            image(0, False, False, True)
            image(1, True, False, True)
            image(2, True, True, True)
            image(3, True, True, True)
            with pe.Fori(2, B // 2 - 1) as p:
                image(2 * p, True, True, True)
                image(2 * p + 1, True, True, True)
            image(B - 2, True, True, True)
            image(B - 1, True, True, False)
            turn2(B - 2, "h2_done", B - 1)
            gn_mean(B - 1, "x2_done", B - 1)
            gn_var(B - 1)
            route(B - 2, "gv_done", B)
            ranks(B - 2, "lg_done", B - 1)
            out_proj(B - 1, 0, "taken_done", B - 1)
            out_proj(B - 1, 1, None, 0)
            turn2(B - 1, "h2_done", B)
            route(B - 1, "x2_done", B)
            ranks(B - 1, "lg_done", B)

            def turn_rows(i, par, n):
                pe.wait_ge(M[f"row_in{par}"], 16 * (n + 1))
                pe.wait_ge(M["xe_lo"], EC * i)
                for k in range(EC):
                    for s in range(BS):
                        mm = pe.transpose(bank[k][:, s * P:(s + 1) * P], rows_f[par][:, s, k * P:(k + 1) * P], ident[:, :])
                    mm.then_inc(M["xe_ps"], 1)

            def layer1(i):
                pe.wait_ge(M["xe_lo"], EC * (i + 1))
                pe.wait_ge(M["w1_lo"], i + 1)
                for c in range(HC):
                    pe.wait_ge(M["gel_done"], HC * i + max(c - HB + 1, 0))
                    for k in range(EC):
                        for j, (wp, xp) in enumerate(three(w1_sp, xe_sp)):
                            mm = pe.matmul(bank[2 + c % HB][:, :], wp[:, k, c * P:(c + 1) * P], xp[:, k, :],
                                           start=(k == 0 and j == 0), stop=(k == EC - 1 and j == 2))
                    mm.then_inc(M["hid_ps"], 1)

            def layer2(i):
                pe.wait_ge(M["w2_lo"], i + 1)
                pe.wait_ge(M["y_done"], 2 * i)
                for c in range(HC):
                    pe.wait_ge(M["gl_done"], HC * i + c + 1)
                    for s in range(BS):
                        for j, (wp, gp) in enumerate(three(w2_sp, g_sp)):
                            mm = pe.matmul(bank[6 + s // 2][:, (s % 2) * E:(s % 2 + 1) * E], gp[:, c, s * P:(s + 1) * P], wp[:, c, :],
                                           start=(c == 0 and s % 2 == 0 and j == 0), stop=(c == HC - 1 and j == 2),
                                           skip_group_check=True)
                mm.then_inc(M["y_ps"], 1)

            turn_rows(0, 0, 0)
            def two_blocks(q):
                for par in range(2):
                    layer1(2 * q + par)
                    turn_rows(2 * q + par + 1, 1 - par, q + par)
                    layer2(2 * q + par)

            two_blocks(0)
            with pe.Fori(1, (NT - 1) // 2) as q:
                two_blocks(q)
            layer1(NT - 1)
            layer2(NT - 1)

        @block.vector
        def _(dve):
            dve.wait_ge(M["wt_hi"], 2)
            dve.wait_ge(M["wt_in"], 32)
            dve.tensor_tensor(wt_sp[1][:, 0:KT, :], wt_f[:, 0:KT, :], f32(wt_sp[0][:, 0:KT, :]), ALU.subtract).then_inc(M["wt_lo"], 1)
            dve.tensor_tensor(wt_sp[1][0:KREM, KT, :], wt_f[0:KREM, KT, :], f32(wt_sp[0][0:KREM, KT, :]), ALU.subtract).then_inc(M["wt_lo"], 1)
            dve.wait_ge(M["c_in"], 64)

            def patches_lo(n):
                dve.wait_ge(M["xt_hi"], 2 * (n + 1))
                dve.wait_ge(M["xt_in"], 32 * (n + 1))
                hi, lo = xt_sp
                dve.tensor_tensor(lo[:, 0:KT, :], xt_f[:, 0:KT, :], f32(hi[:, 0:KT, :]), ALU.subtract).then_inc(M["xt_lo"], 1)
                dve.tensor_tensor(lo[0:KREM, KT, :], xt_f[0:KREM, KT, :], f32(hi[0:KREM, KT, :]), ALU.subtract).then_inc(M["xt_lo"], 1)

            def moments(parts, st_, mv_, sems, n):
                for s in range(NS):
                    dve.bn_stats(st_[:, s, :], parts[s]).then_inc(M[sems[0]], 1)
                dve.wait_ge(M[sems[0]], NS * (n + 1))
                plain(dve)
                for s in range(NS):
                    dve.bn_aggr(mv_[:, s, :], st_[:, s, :]).then_inc(M[sems[1]], 1)
                dve.wait_ge(M[sems[1]], NS * (n + 1))

            def embed(n):
                dve.wait_ge(M["tok_ps"], n + 1)
                dve.wait_ge(M["h_out"], 16 * n)
                tok = [bank[7][:, s * E:(s + 1) * E] for s in range(NS)]
                moments(tok, st1, mv1, ("s1_st", "s1_mv"), n)
                for s in range(NS):
                    dve.scalar_tensor_tensor(out=h1[:, s, :], in0=tok[s], scalar=mv1[:, s, 0:1], in1=gammaB[:, :],
                                             op0=ALU.subtract, op1=ALU.mult).then_inc(M["s1_u"], 1)
                dve.tensor_scalar(rs1[:, 0, :], mv1[:, :, 1], EPS, None, ALU.add).then_inc(M["s1_v1"], 1)

            def embed_moments(n):
                dve.wait_ge(M["s1_u"], NS * (n + 1))
                moments([h1[:, s, :] for s in range(NS)], st1u, mv1u, ("s1_st2", "s1_mv2"), n)
                dve.wait_ge(M["s1_v1"], n + 1)
                dve.scalar_tensor_tensor(out=rs1[:, 1, :], in0=rs1[:, 0, :], scalar=EPS, in1=mv1u[:, :, 1],
                                         op0=ALU.mult, op1=ALU.add).then_inc(M["s1_ve"], 1)

            def embed_norm(n):
                dve.wait_ge(M["s1_rs"], n + 1)
                dve.wait_ge(M["s1_tps"], n)
                for s in range(NS):
                    dve.tensor_scalar(xn1[:, s, :], h1[:, s, :], mv1u[:, s, 0:1], rs1[:, 1, s:s + 1],
                                      ALU.subtract, ALU.mult).then_inc(M["s1_xn"], 1)

            def decay_logits(n):
                dve.wait_ge(M["s1_aps"], n + 1)
                dve.wait_ge(M["sp_abs"], n)
                dve.tensor_tensor(zb[:, :].rearrange("p (s n) -> p s n", s=NS), bank[7][:, 0:NS * H].rearrange("p (s n) -> p s n", s=NS),
                                  baB[:, :].rearrange("p (a n) -> p a n", a=1).broadcast_to([P, NS, H]), ALU.add).then_inc(M["s1_z"], 1)
                dve.wait_ge(M["s1_z"], n + 1)
                dve.tensor_scalar(zm[:, :], zb[:, :], 0.0, None, ALU.max).then_inc(M["sp_m"], 1)

            def log_decay(n):
                dve.wait_ge(M["sp_l"], n + 1)
                dve.wait_ge(M["sp_m"], n + 1)
                dve.wait_ge(M["cum_ps"], n)
                dve.scalar_tensor_tensor(out=la[:, :, :].rearrange("p t n -> p (t n)"), in0=zm[:, :], scalar=-1.0,
                                         in1=zl[:, :], op0=ALU.mult, op1=ALU.subtract).then_inc(M["sp_la"], 1)

            def xn_lo(n):
                dve.wait_ge(M["xh_done"], n + 1)
                dve.tensor_tensor(xn_sp[1][:, :, :].rearrange("p k n -> p (k n)"), xs[:, :],
                                  f32(xn_sp[0][:, :, :].rearrange("p k n -> p (k n)")), ALU.subtract).then_inc(M["xl_done"], 1)

            def weight_lo(i):
                dve.wait_ge(M["ws_hi"], i + 1)
                dve.tensor_tensor(w_parts[i][1].rearrange("p k n -> p (k n)"), stage_w[i % 2],
                                  f32(w_parts[i][0].rearrange("p k n -> p (k n)")), ALU.subtract).then_inc(M["ws_lo"], 1)

            patches_lo(0)
            embed(0)
            embed_moments(0)
            embed_norm(0)
            weight_lo(0)
            weight_lo(1)
            decay_logits(0)
            for i in range(2, 5):
                weight_lo(i)
            log_decay(0)
            xn_lo(0)
            dve.wait_ge(M["g_in"], 16 * 11)
            dve.tensor_scalar(gnwh[:, :], gnw[:, :], 0.5, None, ALU.mult).then_inc(M["gnh"], 1)
            dve.tensor_scalar(gnbh[:, :], gnb[:, :], 0.5, None, ALU.mult).then_inc(M["gnh"], 1)
            dve.memset(taken[:, :], 0.0).then_inc(M["gnh"], 1)
            dve.wait_ge(M["gnh"], 3)

            def silu(b, c):
                dve.wait_ge(M["tq_done"], NP * b + c + 1)
                dve.wait_ge(M["s_ps"], H * b + max(2 * c - 2, 0))
                dve.scalar_tensor_tensor(out=qk_s[c % 2][:, :], in0=tq[:, :], scalar=1.0, in1=bank[0][:, :],
                                         op0=ALU.add, op1=ALU.mult).then_inc(M["silu_done"], 1)

            def decayed(b, c, h):
                dve.wait_ge(M["s_ps"], H * b + h + 1)
                dve.wait_ge(M["exp_done"], H * b + h + 1)
                dve.wait_ge(M["o_ps"], NP * b + c)
                dve.tensor_tensor(att[h % 2][:, :], bank[4 + h % 2][:, 0:LW], dec[h % 2][:, :], ALU.mult).then_inc(M["mult_done"], 1)

            def head_stats(b, c, par):
                dve.wait_ge(M["o_done"], NP * b + c + 1)
                dve.wait_ge(M["gmv_done"], NP * b + c)
                dve.bn_stats(gst[:, :], osb[par][:, c, :]).then_inc(M["gst_done"], 1)
                dve.wait_ge(M["gst_done"], NP * b + c + 1)
                if c == 0 and not (isinstance(b, int) and b == 0):
                    dve.wait_ge(M["gt2_done"], b)
                plain(dve)
                dve.bn_aggr(gmv[:, c, :], gst[:, :]).then_inc(M["gmv_done"], 1)

            def spread(pb):
                dve.wait_ge(M["gn1_ps"], pb + 1)
                dve.tensor_copy(gm[:, :], bank[7][:, 0:NP]).then_inc(M["gn_step"], 1)
                dve.wait_ge(M["gn_step"], 6 * pb + 1)
                dve.wait_ge(M["gmv_done"], NP * (pb + 1))
                dve.tensor_tensor(gd[:, :], gmv[:, :, 0], gm[:, :], ALU.subtract).then_inc(M["gn_step"], 1)
                dve.wait_ge(M["gn_step"], 6 * pb + 2)
                dve.wait_ge(M["gn2_ps"], pb)
                dve.tensor_tensor(gt[:, :], gd[:, :], gd[:, :], ALU.mult).then_inc(M["gn_step"], 1)
                dve.wait_ge(M["gn_step"], 6 * pb + 3)
                dve.tensor_tensor(gt[:, :], gt[:, :], gmv[:, :, 1], ALU.add).then_inc(M["gt2_done"], 1)

            def affine(pb):
                dve.wait_ge(M["gn2_ps"], pb + 1)
                dve.tensor_scalar(gr[:, :], bank[7][:, 0:NP], 16 * EPS, None, ALU.add).then_inc(M["gv_done"], 1)

            def affine_steps(pb):
                dve.wait_ge(M["gr_done"], pb + 1)
                dve.tensor_tensor(gsc[:, :], gr[:, :], gnwh[:, :], ALU.mult).then_inc(M["gn_step"], 1)
                dve.wait_ge(M["gn_step"], 6 * pb + 4)
                dve.tensor_tensor(gd[:, :], gm[:, :], gsc[:, :], ALU.mult).then_inc(M["gn_step"], 1)
                dve.wait_ge(M["gn_step"], 6 * pb + 5)
                dve.tensor_tensor(gbi[:, :], gnbh[:, :], gd[:, :], ALU.subtract).then_inc(M["gn_step"], 1)

            def gated(pb, par, j):
                dve.wait_ge(M["yn_done"], NP * pb + PQ * (j + 1))
                dve.wait_ge(M["tg_done"], NP * (pb + 1))
                cs = slice(PQ * j, PQ * j + PQ)
                dve.scalar_tensor_tensor(out=yf[:, cs, :], in0=tg[par][:, cs, :], scalar=1.0, in1=yf[:, cs, :],
                                         op0=ALU.add, op1=ALU.mult).then_inc(M["yf_done"], 1)

            def y_lo(pb, j):
                cs = slice(PQ * j, PQ * j + PQ)
                dve.wait_ge(M["yh_done"], 2 * pb + j + 1)
                dve.tensor_tensor(y_sp[1][:, cs, :], yf[:, cs, :], f32(y_sp[0][:, cs, :]), ALU.subtract).then_inc(M["yl_done"], 1)

            def residual(pb):
                dve.wait_ge(M["wo_ps"], pb + 1)
                dve.wait_ge(M["hb_in"], 16 * (pb + 1))
                dve.wait_ge(M["h2_out"], 16 * pb)
                dve.tensor_tensor(h2[:, :, :].rearrange("p s n -> p (s n)"), bank[7][:, :], hb[:, :], ALU.add).then_inc(M["h2_done"], 1)
                dve.wait_ge(M["h2_done"], pb + 1)
                moments([h2[:, s, :] for s in range(NS)], st, mv, ("b_st", "b_mv"), pb)
                dve.tensor_scalar(rs[:, :, 0], mv[:, :, 1], EPS, None, ALU.add).then_inc(M["b_ve"], 1)

            def normed(pb):
                dve.wait_ge(M["b_rs"], pb + 1)
                dve.wait_ge(M["scat"], 16 * NS * TOPK * pb)
                for s in range(NS):
                    dve.tensor_scalar(xn2[:, s, :], h2[:, s, :], mv[:, s, 0:1], rs[:, s, :], ALU.subtract, ALU.mult).then_inc(M["b_xn"], 1)

            def keep_logits(pb):
                dve.wait_ge(M["lg_ps"], pb + 1)
                dve.tensor_copy(lg[:, :, :].rearrange("p s n -> p (s n)"), bank[7][:, 0:NS * X]).then_inc(M["lg_done"], 1)

            def choose(pb):
                dve.wait_ge(M["lg_done"], pb + 1)
                plain(dve)
                for s in range(NS):
                    dve.max(top[:, s, :], lg[:, s, :]).then_inc(M["top_done"], 1)
                dve.wait_ge(M["top_done"], NS * (pb + 1))
                dve.tensor_scalar(ntop[:, :, 0], top[:, :, 0], -1.0, None, ALU.mult).then_inc(M["ntop_done"], 1)
                for s in range(NS):
                    dve.max_index(topi[:, s, :], top[:, s, :], lg[:, s, :]).then_inc(M["topi_done"], 1)
                dve.wait_ge(M["topi_done"], NS * (pb + 1))
                dve.tensor_copy(idxf[:, :, :], topi[:, :, 0:TOPK]).then_inc(M["idxf_done"], 1)
                dve.wait_ge(M["idxf_done"], pb + 1)
                for s in range(NS):
                    for k in range(TOPK):
                        dve.tensor_scalar(pick[:, s, k, :], iota8[:, :], idxf[:, s, k:k + 1], None, ALU.is_equal).then_inc(M["pick_done"], 1)
                dve.wait_ge(M["pick_done"], NS * TOPK * (pb + 1))
                dve.tensor_tensor(both[:, :, :], pick[:, :, 0, :], pick[:, :, 1, :], ALU.add).then_inc(M["both_done"], 1)

            def weigh(pb):
                dve.wait_ge(M["tope_done"], NS * (pb + 1))
                dve.reciprocal(trec[:, :, 0], tsum[:, :, 0]).then_inc(M["trec_done"], 1)
                dve.wait_ge(M["trec_done"], pb + 1)
                wrow = w_all[:, bass.ds(pb, 1), :].rearrange("p a (s k) -> p (a s) k", s=NS)
                dve.tensor_tensor(wrow, tope[:, :, 0:TOPK], trec[:, :, :].broadcast_to([P, NS, TOPK]), ALU.mult).then_inc(M["wall_done"], 1)

            def keep_ranks(pb):
                dve.wait_ge(M["rk_ps"], pb + 1)
                dve.wait_ge(M["taken_done"], pb)
                dve.tensor_tensor(rank[:, :, :], bank[7][:, 0:NS * X].rearrange("p (s n) -> p s n", s=NS),
                                  taken[:, :].rearrange("p (a n) -> p a n", a=1).broadcast_to([P, NS, X]), ALU.add).then_inc(M["rank_done"], 1)
                dve.wait_ge(M["rank_done"], pb + 1)
                dve.tensor_tensor(taken[:, :], bank[7][:, 2 * X:3 * X], taken[:, :], ALU.add).then_inc(M["taken_done"], 1)

            def place(pb):
                for s in range(NS):
                    for k in range(TOPK):
                        j = TOPK * s + k
                        dve.wait_ge(M["rsel_done"], NS * TOPK * pb + j)
                        dve.tensor_tensor_reduce(junk[:, :], rank[:, s, :], pick[:, s, k, :], 1.0, 0.0, ALU.mult, ALU.add,
                                                 rsel[:, j:j + 1]).then_inc(M["rsel_done"], 1)
                dve.wait_ge(M["rsel_done"], NS * TOPK * (pb + 1))
                dve.wait_ge(M["scat"], 16 * NS * TOPK * pb)
                dve.scalar_tensor_tensor(out=slot[:, :], in0=idxf[:, :, :].rearrange("p s k -> p (s k)"), scalar=float(CAP), in1=rsel[:, :],
                                         op0=ALU.mult, op1=ALU.add).then_inc(M["slot_done"], 1)
                dve.wait_ge(M["slot_done"], pb + 1)
                dve.tensor_copy(slots_all[:, bass.ds(pb, 1), :].rearrange("p a n -> p (a n)"), slot[:, :])
                dve.tensor_copy(idx_all[:, bass.ds(pb, 1), :].rearrange("p a n -> p (a n)"), idxf[:, :, :].rearrange("p s k -> p (s k)")).then_inc(M["slotc_done"], 1)

            def running_sums(b):
                dve.wait_ge(M["cum_ps"], b + 1)
                dve.wait_ge(M["ct_ps"], b)
                cps = bank[7][:, 0:NS * H].rearrange("p (s n) -> p s n", s=NS)
                dve.tensor_copy(ccs[:, :, 0:H].bitcast(F32R), cps).then_inc(M["cc_hi"], 1)
                dve.wait_ge(M["cc_hi"], b + 1)
                dve.tensor_tensor(ccs[:, :, H:2 * H], cps, ccs[:, :, 0:H], ALU.subtract).then_inc(M["cc_lo"], 1)
                dve.wait_ge(M["exp_done"], H * b)
                dve.tensor_scalar(ncum[:, :, :], cps, -1.0, None, ALU.mult).then_inc(M["ncum_done"], 1)

            def image(b, par, post, post2, nxt):
                if post:
                    head_stats(b - 1, NP - 1, 1 - par)
                if post2:
                    normed(b - 2)
                running_sums(b)
                silu(b, 0)
                for i in range(2):
                    dve.wait_ge(M["v_ps"], 4 * b + 3 + i)
                    if i == 0:
                        dve.wait_ge(M["o_ps"], NP * b)
                    dve.tensor_copy(v_sb[:, 1, i * 512:(i + 1) * 512], bank[4 + i][:, :]).then_inc(M["v_dve"], 1)
                for c in range(NP):
                    if post and c == 1:
                        affine(b - 1)
                    if nxt and c == 7:
                        xn_lo(b + 1)
                    decayed(b, c, 2 * c)
                    decayed(b, c, 2 * c + 1)
                    if nxt and c == 6:
                        decay_logits(b + 1)
                    if c + 1 < NP:
                        silu(b, c + 1)
                    if c >= 1:
                        head_stats(b, c - 1, par)
                    if c == 0:
                        if post:
                            spread(b - 1)
                        if nxt:
                            patches_lo(b + 1)
                    if post and c == 1:
                        affine_steps(b - 1)
                    if nxt and c == 2:
                        embed(b + 1)
                    if c == 3:
                        if nxt:
                            embed_moments(b + 1)
                        if post:
                            gated(b - 1, 1 - par, 0)
                    if c == 4:
                        if post2:
                            keep_logits(b - 2)
                        if nxt:
                            embed_norm(b + 1)
                        if post2:
                            choose(b - 2)
                    if post and c == 5:
                        gated(b - 1, 1 - par, 1)
                        y_lo(b - 1, 0)
                    if c == 6:
                        if post:
                            y_lo(b - 1, 1)
                        if post2:
                            keep_ranks(b - 2)
                            place(b - 2)
                    if c == 7:
                        if post:
                            residual(b - 1)
                        if nxt:
                            log_decay(b + 1)
                        if post2:
                            weigh(b - 2)

            image(0, 0, False, False, True)
            image(1, 1, True, False, True)
            image(2, 0, True, True, True)
            image(3, 1, True, True, True)
            with dve.Fori(2, B // 2 - 1) as p:
                image(2 * p, 0, True, True, True)
                image(2 * p + 1, 1, True, True, True)
            image(B - 2, 0, True, True, True)
            image(B - 1, 1, True, True, False)
            normed(B - 2)
            head_stats(B - 1, NP - 1, 1)
            spread(B - 1)
            affine(B - 1)
            affine_steps(B - 1)
            keep_logits(B - 2)
            choose(B - 2)
            keep_ranks(B - 2)
            place(B - 2)
            for j in range(2):
                gated(B - 1, 1, j)
                y_lo(B - 1, j)
            weigh(B - 2)
            residual(B - 1)
            normed(B - 1)
            keep_logits(B - 1)
            choose(B - 1)
            keep_ranks(B - 1)
            place(B - 1)
            weigh(B - 1)

            tbc = [0]

            def tb(ins):
                tbc[0] += 1
                ins.then_inc(M["tb"], 1)
                dve.wait_ge(M["tb"], tbc[0])

            cnt = taken[:, :]
            dve.wait_ge(M["taken_done"], B)
            tb(dve.tensor_tensor(tmp64[:, :, :], cnt.rearrange("p (n a) -> p n a", a=1).broadcast_to([P, X, NBLK]),
                                 iob[:, :].rearrange("p (n a) -> p n a", a=NBLK), ALU.is_gt))
            tb(dve.tensor_reduce(nb[:, :], tmp64[:, :, :], AX.X, ALU.add))
            tb(dve.tensor_tensor(tmp64[:, :, :], nb[:, :].rearrange("p (a n) -> p a n", a=1).broadcast_to([P, X, X]),
                                 tri8[:, :].rearrange("p (a n) -> p a n", a=X), ALU.mult))
            tb(dve.tensor_reduce(cb[:, :], tmp64[:, :, :], AX.X, ALU.add))
            tb(dve.tensor_tensor(cmp[:, :, :], cb[:, :].rearrange("p (a n) -> p a n", a=1).broadcast_to([P, NT, X]),
                                 til[:, :].rearrange("p (a n) -> p a n", a=NT), ALU.is_le))
            tb(dve.tensor_tensor(cmn[:, :, :], cmp[:, :, :], nb[:, :].rearrange("p (a n) -> p a n", a=1).broadcast_to([P, NT, X]), ALU.mult))
            tb(dve.tensor_reduce(te[:, :], cmp[:, :, :], AX.X, ALU.add))
            tb(dve.tensor_reduce(tst[:, :], cmn[:, :, :], AX.X, ALU.add))
            tiles = til[:, :].rearrange("p (a n) -> p a n", a=NT)[:, :, 0]
            tb(dve.tensor_scalar(tva[:, :], te[:, :], float(X), None, ALU.is_lt))
            tb(dve.tensor_tensor(te[:, :], te[:, :], tva[:, :], ALU.mult))
            tb(dve.tensor_tensor(tr0[:, :], tiles, tst[:, :], ALU.subtract))
            tb(dve.tensor_tensor(tr0[:, :], tr0[:, :], tva[:, :], ALU.mult))
            tb(dve.tensor_scalar(tr0[:, :], tr0[:, :], float(BLK), None, ALU.mult))
            tb(dve.scalar_tensor_tensor(out=tr0[:, :], in0=te[:, :], scalar=float(CAP), in1=tr0[:, :], op0=ALU.mult, op1=ALU.add))
            tb(dve.tensor_tensor(dlt[:, :], cb[:, :], nb[:, :], ALU.subtract))
            tb(dve.tensor_scalar(dlt[:, :], dlt[:, :], float(BLK), None, ALU.mult))
            tb(dve.scalar_tensor_tensor(out=dlt[:, :], in0=iota8[:, :], scalar=-float(CAP), in1=dlt[:, :], op0=ALU.mult, op1=ALU.add))
            dve.tensor_copy(tab[:, 0:NT], te[:, :])
            dve.tensor_copy(tab[:, NT:2 * NT], tr0[:, :])
            tb(dve.scalar_tensor_tensor(out=padf[:, :], in0=iota8[:, :], scalar=float(CAP), in1=cnt, op0=ALU.mult, op1=ALU.add))
            tb(dve.tensor_copy(padi[:, :], padf[:, :]))

            nch = B * NS * TOPK
            dve.wait_ge(M["slotc_done"], B)
            idf = idx_all[:, :, :].rearrange("p b (j a) -> p (b j) a", a=1).broadcast_to([P, nch, X])
            tb(dve.tensor_tensor(onx[:, :, :], idf, iota8[:, :].rearrange("p (a n) -> p a n", a=1).broadcast_to([P, nch, X]), ALU.is_equal))
            tb(dve.tensor_tensor(onx[:, :, :], onx[:, :, :], dlt[:, :].rearrange("p (a n) -> p a n", a=1).broadcast_to([P, nch, X]), ALU.mult))
            tb(dve.tensor_reduce(dsel[:, :], onx[:, :, :], AX.X, ALU.add))
            tb(dve.tensor_tensor(yrow[:, :], slots_all[:, :, :].rearrange("p b j -> p (b j)"), dsel[:, :], ALU.add))

            def w_lo(name, parts, staged, par, i):
                dve.wait_ge(M[f"{name}_hi"], i + 1)
                dve.tensor_tensor(parts[1].rearrange("p k n -> p (k n)"), staged[par], f32(parts[0].rearrange("p k n -> p (k n)")),
                                  ALU.subtract).then_inc(M[f"{name}_lo"], 1)

            def x_lo(i):
                for k in range(EC):
                    dve.wait_ge(M["xe_hi"], EC * i + k + 1)
                    dve.tensor_tensor(xe_sp[1][:, k, :], bank[k][:, :], f32(xe_sp[0][:, k, :]), ALU.subtract).then_inc(M["xe_lo"], 1)

            def hidden_lo(i, c):
                dve.wait_ge(M["gh_done"], HC * i + c + 1)
                dve.tensor_tensor(g_sp[1][:, c, :], gel[c % 2], f32(g_sp[0][:, c, :]), ALU.subtract).then_inc(M["gl_done"], 1)

            def keep_y(i, par, n):
                dve.wait_ge(M["y_ps"], i + 1)
                dve.wait_ge(M[f"y_out{par}"], 16 * n)
                for m in range(2):
                    dve.tensor_tensor(yo[par][:, 2 * m:2 * m + 2, :], bank[6 + m][:, :].rearrange("p (s n) -> p s n", s=2),
                                      b2_sb[par][:, :].rearrange("p (a n) -> p a n", a=1).broadcast_to([P, 2, E]), ALU.add).then_inc(M["y_done"], 1)

            def blockrow(i, par, n, last):
                for c in range(HC):
                    hidden_lo(i, c)
                    if c == 1:
                        w_lo("w2", w2_sp, w2_f, par, i)
                if not last:
                    x_lo(i + 1)
                    w_lo("w1", w1_sp, w1_f, 1 - par, i + 1)
                keep_y(i, par, n)

            x_lo(0)
            w_lo("w1", w1_sp, w1_f, 0, 0)
            def two_blocks(q):
                blockrow(2 * q, 0, q, False)
                blockrow(2 * q + 1, 1, q, False)

            two_blocks(0)
            with dve.Fori(1, (NT - 1) // 2) as q:
                two_blocks(q)
            blockrow(NT - 1, 0, (NT - 1) // 2, True)

            dve.wait_ge(M["wall_done"], B)
            for t in range(T // P):
                r = t % NG
                w = [w_all[:, t // NS, TOPK * (t % NS) + k:TOPK * (t % NS) + k + 1] for k in range(TOPK)]
                dve.wait_ge(M[f"ga_in{r}"], 32 * (t // NG + 1))
                dve.wait_ge(M[f"hf_in{r}"], 16 * (t // NG + 1))
                dve.scalar_tensor_tensor(out=f1[r], in0=ga[r], scalar=w[0], in1=hf[r], op0=ALU.mult, op1=ALU.add).then_inc(M["f1_done"], 1)
                dve.wait_ge(M["f1_done"], t + 1)
                if t >= NG:
                    dve.wait_ge(M[f"o_out{r}"], 16 * (t // NG))
                dve.scalar_tensor_tensor(out=f2[r], in0=gb[r], scalar=w[1], in1=f1[r], op0=ALU.mult, op1=ALU.add).then_inc(M["f2_done"], 1)


_INS = ['x', 'L0_tok_W', 'L0_tok_gamma', 'L0_attn_Wq', 'L0_attn_Wk', 'L0_attn_Wv', 'L0_attn_Wg', 'L0_attn_Wa',
        'L0_attn_ba', 'L0_attn_Wo', 'L0_attn_gn_w', 'L0_attn_gn_b', 'L0_ffn_w_router', 'L0_ffn_w1', 'L0_ffn_b1',
        'L0_ffn_w2', 'L0_ffn_b2']


def constants():
    i = np.arange(P)
    before = np.where(i[:, None] <= i[None, :], 0.0, -1e30)
    n = np.arange(X)
    return {
        "c_ident": np.eye(P, dtype=np.float32),
        "c_upper": (i[:, None] <= i[None, :]).astype(np.float32),
        "c_ones": np.ones((P, P), np.float32),
        "c_strict": (i[:, None] < i[None, :]).astype(np.float32),
        "c_half": ((i[:, None] // D == i[None, :] // D) / D).astype(np.float32),
        "c_sel": np.tile(np.eye(H, dtype=np.float32), (2, 1)),
        "c_mask": np.tile(before, (1, 2)).astype(np.float32),
        "c_iota": np.tile(n.astype(np.float32), (P, 1)),
        "c_blk": np.tile(np.arange(NBLK, dtype=np.float32) * BLK, (1, X)).reshape(1, X * NBLK),
        "c_tri8": (n[None, :] <= n[:, None]).astype(np.float32).reshape(1, X * X),
        "c_til": np.repeat(np.arange(NT, dtype=np.float32), X).reshape(1, NT * X),
    }


def laid_out(inputs):
    a = {n: np.asarray(inputs[n]) for n in _INS}
    side = SIDE // PATCH
    a['x'] = a['x'].reshape(B, C, side, PATCH, side, PATCH).transpose(1, 3, 5, 0, 2, 4).reshape(FEAT, T)
    a['L0_attn_gn_w'] = a['L0_attn_gn_w'].reshape(NP, P).T
    a['L0_attn_gn_b'] = a['L0_attn_gn_b'].reshape(NP, P).T
    a['L0_ffn_b1'] = a['L0_ffn_b1'].reshape(X, HC, P).transpose(0, 2, 1)
    return {n: np.ascontiguousarray(v) for n, v in a.items()}


def kernel(**inputs):
    import concourse.bacc as _bacc
    from concourse.bass_utils import run_bass_kernel_spmd as _run

    nc = _bacc.Bacc("TRN2", target_bir_lowering=False, num_devices=1)
    arrays, args = {}, []
    for name, a in {**laid_out(inputs), **constants()}.items():
        arrays[f"in_{name}"] = a
        args.append(nc.dram_tensor(f"in_{name}", a.shape, mybir.dt.from_np(a.dtype), kind="ExternalInput").ap())
    out = nc.dram_tensor("out_0", (B, S, E), F32, kind="ExternalOutput").ap()
    vit_layer(nc, *args, out)
    r = _run(nc, [arrays], core_ids=[0])
    return r.results[0]["out_0"]
```

```python
from contextlib import ExitStack

import numpy as np
import concourse.bass as bass
from concourse import mybir

F32 = mybir.dt.float32
F32R = mybir.dt.float32r
BF16 = mybir.dt.bfloat16
I32 = mybir.dt.int32
U32 = mybir.dt.uint32
ALU = mybir.AluOpType
ACT = mybir.ActivationFunctionType
AX = mybir.AxisListType

P = 128
B = 16
S = 256
NS = S // P
C, PATCH, SIDE = 5, 8, 128
FEAT = C * PATCH * PATCH
KT = FEAT // P
KREM = FEAT - KT * P
E = 256
EC = E // P
H, D = 16, 64
DI = H * D
NP = DI // P
PQ = NP // 2
X = 8
HID = 1024
HC = HID // P
TOPK = 2
T = B * S
EPS = 1e-5
BLK = 256
BS = BLK // P
CAP = T + BLK
NBLK = -(-T // BLK)
NGEL = 4
WQ = 4
YB = (BS + 1) // 2
HB = 4
NT = (T * TOPK + X * (BLK - 1)) // BLK
NUM, WT, EX = E, E + 1, E + 3
EW = E + 5
LW = S + P


def vit_layer(nc, xT, w_tok, gamma, wq, wk, wv, wg, wa, ba, wo, gn_w, gn_b,
              w_router, w1, b1, w2, b2,
              ident_d, upper_d, ones_d, strict_d, half_d, sel_d, mask_d, iota_d, blk_d, tri8_d, til_d,
              number_d, pad_d, out):
    with ExitStack() as ctx:
        def sb(name, shape, dt=F32):
            return ctx.enter_context(nc.sbuf_tensor(name, shape, dt))

        def sem(name):
            return ctx.enter_context(nc.semaphore(name))

        h_d = nc.dram_tensor("h_scratch", (B, P, NS * E), F32).ap()
        lists_d = nc.dram_tensor("expert_rows", (X * CAP + BLK, EW), F32).ap()
        out_rows = out.rearrange("b s n -> (b s) n")

        ident = sb("ident", [P, P])
        upper = sb("upper", [P, P])
        ones = sb("ones", [P, P])
        strict = sb("strict", [P, P])
        half = sb("half", [P, P])
        sel_r = sb("sel_r", [2 * H, H], F32R)
        identb = sb("identb", [P, P], BF16)
        maskb = sb("maskb", [P, 2 * P], BF16)
        iota8 = sb("iota8", [P, X])
        gammaB = sb("gammaB", [P, E])
        baB = sb("baB", [P, H])
        wa_sb = sb("wa_sb", [P, EC, H])
        wr_sb = sb("wr_sb", [P, EC, X])
        gnw = sb("gnw", [P, NP])
        gnb = sb("gnb", [P, NP])
        gnwh = sb("gnwh", [P, NP])
        gnbh = sb("gnbh", [P, NP])

        big_r = sb("big_r", [P, 20480], F32R)
        wsp = [[big_r[:, (2 * i + j) * 2048:(2 * i + j + 1) * 2048].rearrange("p (k n) -> p k n", k=EC)
                for j in range(2)] for i in range(4)]
        wo_sp = [big_r[:, 16384 + j * 2048:16384 + (j + 1) * 2048].rearrange("p (k n) -> p k n", k=NP)
                 for j in range(2)]
        def parts(first, size, chunks):
            return [big_r[:, f:f + size].rearrange("p (k n) -> p k n", k=chunks) for f in first]

        y_sp = [sb(f"y_sp{j}", [P, NP, S], F32R) for j in range(2)]
        w1_sp = [parts((0, 2048), 2048, EC), parts((10240, 14336), 2048, EC)]
        w2_sp = [parts((4096, 6144), 2048, HC), y_sp]
        g_sp = parts((8192, 12288), HC * BLK, HC)
        xe_sp = [parts((f, f + 512), EC * BLK, EC) for f in (16384, 17408)]

        xn_sp = [sb(f"xn_sp{j}", [P, EC, S], F32R) for j in range(2)]
        xt_sp = [sb(f"xt_sp{j}", [P, KT + 1, S], F32R) for j in range(2)]
        wt_sp = [sb(f"wt_sp{j}", [P, KT + 1, E], F32R) for j in range(2)]
        xt_f = sb("xt_f", [P, KT + 1, S])

        big_f = sb("big_f", [P, 8192])
        stage_w = [big_f[:, i:i + 2048] for i in (0, 2048, 6144)]
        wt_f = big_f[:, 4096:4864].rearrange("p (k n) -> p k n", k=KT + 1)
        sel_f = big_f[0:2 * H, 4864:4864 + H]
        mask_f = big_f[:, 5120:5120 + 2 * P]
        tg = [big_f[:, i * 2048:(i + 1) * 2048].rearrange("p (k n) -> p k n", k=NP) for i in range(2)]
        osb = [big_f[:, 4096 + i * 2048:4096 + (i + 1) * 2048].rearrange("p (k n) -> p k n", k=NP) for i in range(2)]
        w1_f = [big_f[:, i * 2048:(i + 1) * 2048] for i in range(2)]
        w2_f = [big_f[:, 4096 + i * 2048:4096 + (i + 1) * 2048] for i in range(2)]

        mid_f = sb("mid_f", [P, max(4096, 2 * BS * (EW + E) + NGEL * BLK)])
        v_sb = mid_f[:, 0:2048].rearrange("p (s n) -> p s n", s=NS)
        yf = mid_f[:, 2048:4096].rearrange("p (k n) -> p k n", k=NP)
        rows_f = [mid_f[:, i * BS * EW:(i + 1) * BS * EW].rearrange("p (s n) -> p s n", s=BS) for i in range(2)]
        gel = [mid_f[:, 2 * BS * EW + i * BLK:2 * BS * EW + (i + 1) * BLK] for i in range(NGEL)]
        yo = [mid_f[:, 2 * BS * EW + NGEL * BLK + i * BS * E:2 * BS * EW + NGEL * BLK + (i + 1) * BS * E].rearrange("p (s n) -> p s n", s=BS) for i in range(2)]

        qk_s = [sb(f"qk_s{i}", [P, 2 * S]) for i in range(2)]
        tq = sb("tq", [P, 2 * S])
        dec = [sb(f"dec{i}", [P, LW]) for i in range(2)]
        att = [sb(f"att{i}", [P, LW]) for i in range(2)]
        h1 = sb("h1", [P, NS, E])
        xn1 = sb("xn1", [P, NS, E])
        xs = sb("xs", [P, EC * S])
        hb = sb("hb", [P, NS * E])
        h2 = sb("h2", [P, NS, E])
        xn2 = sb("xn2", [P, NS, EW])
        xn2T = sb("xn2T", [P, EC, S])
        cumR = sb("cumR", [2 * H, LW], F32R)
        ccs = sb("ccs", [P, NS, 2 * H])
        ncum = sb("ncum", [P, NS, H])
        zb = sb("zb", [P, NS * H])
        za = sb("za", [P, NS * H])
        ze = sb("ze", [P, NS * H])
        zl = sb("zl", [P, NS * H])
        zm = sb("zm", [P, NS * H])
        la = sb("la", [P, NS, H])
        st = sb("st", [P, NS, 6])
        mv = sb("mv", [P, NS, 2])
        rs = sb("rs", [P, NS, 1])
        mhalf = sb("mhalf", [P, NP])
        st1 = sb("st1", [P, NS, 6])
        mv1 = sb("mv1", [P, NS, 2])
        st1u = sb("st1u", [P, NS, 6])
        mv1u = sb("mv1u", [P, NS, 2])
        rs1 = sb("rs1", [P, 2, NS])
        gst = sb("gst", [P, 6])
        gmv = sb("gmv", [P, NP, 2])
        gm = sb("gm", [P, NP])
        gd = sb("gd", [P, NP])
        gt = sb("gt", [P, NP])
        gr = sb("gr", [P, NP])
        gsc = sb("gsc", [P, NP])
        gbi = sb("gbi", [P, NP])
        lg = sb("lg", [P, NS, X])
        top = sb("top", [P, NS, X])
        topi = sb("topi", [P, NS, X], U32)
        tope = sb("tope", [P, NS, X])
        ntop = sb("ntop", [P, NS, 1])
        tsum = sb("tsum", [P, NS, 1])
        trec = sb("trec", [P, NS, 1])
        idxf = sb("idxf", [P, NS, TOPK])
        pick = sb("pick", [P, NS, TOPK, X])
        both = sb("both", [P, NS, X])
        rank = sb("rank", [P, NS, X])
        rsel = sb("rsel", [P, NS * TOPK])
        junk = sb("junk", [P, X])
        taken = sb("taken", [P, X])
        slot = sb("slot", [P, NS * TOPK], U32)
        number = sb("number", [P, B * NS])
        iob = sb("iob", [P, X * NBLK])
        tri8 = sb("tri8", [P, X * X])
        til = sb("til", [P, NT * X])
        tmp64 = sb("tmp64", [P, X, X])
        below = sb("below", [P, X, NBLK])
        nb = sb("nb", [P, X])
        cb = sb("cb", [P, X])
        cmp = sb("cmp", [P, NT, X])
        cmn = sb("cmn", [P, NT, X])
        te = sb("te", [P, NT])
        tst = sb("tst", [P, NT])
        tva = sb("tva", [P, NT])
        tr0 = sb("tr0", [P, NT])
        tab = sb("tab", [P, 2 * NT], I32)
        padf = sb("padf", [P, X])
        padi = sb("padi", [P, X], I32)
        ecol = [sb(f"ecol{i}", [P, 1]) for i in range(2)]
        wpart = [sb(f"wpart{i}", [P, BS]) for i in range(2 * TOPK)]
        wsel = [sb(f"wsel{i}", [P, BS]) for i in range(2)]
        tok = [sb(f"tok{i}", [P, BS], U32) for i in range(2)]
        b1_sb = [sb(f"b1_{i}", [P, HC]) for i in range(2)]
        b2_sb = [tq[:, i * E:(i + 1) * E] for i in range(2)]
        bank = [ctx.enter_context(nc.psum_tensor(f"bank{i}", [P, 512], F32)) for i in range(8)]

        names = """
        passed mh_done c_in c_sel c_selr c_maskb c_sum ws_in0 ws_in1 ws_in2 ws_hi ws_lo wt_in wt_hi wt_lo g_in
        xt_in xt_hi xt_lo tok_ps s1_st s1_mv s1_u s1_v1 s1_st2 s1_mv2 s1_ve s1_rs s1_h s1_xn
        s1_tps s1_xnT s1_aps s1_z b_ve gv_done h_out
        sp_abs sp_e sp_l sp_m sp_la gnh
        xh_done xl_done cum_ps cc_hi cc_lo ncum_done ct_ps ct_copied v_ps v_act v_dve
        qk_ps g_ps tq_done tg_done silu_done d_ps exp_done s_ps mult_done o_ps o_done gst_done gmv_done
        gn1_ps gn_step gt2_done gn2_ps gr_done yn_done yf_done yh_done yl_done
        wo_ps hb_in h2_done h2_out b_st b_mv b_rs b_xn x2_ps x2_done lg_ps lg_done top_done topi_done ntop_done
        tope_done trec_done wall_done idxf_done pick_done both_done rk_ps rank_done taken_done rsel_done
        slot_done tail_done scat
        tb pad_out
        row_in0 row_in1 w1_in0 w1_in1 w2_in0 w2_in1 b_in0 b_in1 xe_ps xe_hi xe_lo w1_hi w1_lo w2_hi w2_lo
        hid_ps gel_done gh_done gl_done y_half y_ps y_done ecol_done wk_done wsel_done y_w added
        """.split()
        M = {n: sem(n) for n in names}

        block = ctx.enter_context(nc.Block())

        def three(part_w, part_x):
            return [(part_w[0], part_x[0]), (part_w[0], part_x[1]), (part_w[1], part_x[0])]

        def f32(ap):
            return ap.bitcast(F32)

        def plain(eng):
            eng.sem_inc(M["passed"])

        W_ATT = [wv, wq, wk, wg, wo]
        w_parts = [wsp[2], wsp[0], wsp[1], wsp[3], wo_sp]

        @block.sync
        def _(sp):
            sp.dma_start(wt_f[:, 0:KT, :], w_tok[0:KT * P, :].rearrange("(k p) n -> p k n", p=P)).then_inc(M["wt_in"], 16)
            sp.dma_start(wt_f[0:KREM, KT, :], w_tok[KT * P:FEAT, :]).then_inc(M["wt_in"], 16)

            def load_patches(n):
                sp.wait_ge(M["xt_lo"], 2 * n)
                src = xT[:, bass.ds(n * S, S)]
                sp.dma_start(xt_f[:, 0:KT, :], src[0:KT * P, :].rearrange("(k p) n -> p k n", p=P)).then_inc(M["xt_in"], 16)
                sp.dma_start(xt_f[0:KREM, KT, :], src[KT * P:FEAT, :]).then_inc(M["xt_in"], 16)

            def store_h(n):
                sp.wait_ge(M["s1_h"], NS * (n + 1))
                sp.dma_start(h_d[bass.ds(n, 1), :, :].rearrange("a p n -> (a p) n"),
                             h1[:, :, :].rearrange("p s n -> p (s n)")).then_inc(M["h_out"], 16)

            def load_h(b):
                sp.wait_ge(M["h_out"], 16 * (b + 1))
                sp.wait_ge(M["h2_done"], b)
                sp.dma_start(hb[:, :], h_d[bass.ds(b, 1), :, :].rearrange("a p n -> (a p) n")).then_inc(M["hb_in"], 16)

            def store_h2(b):
                sp.wait_ge(M["h2_done"], b + 1)
                sp.dma_start(out[bass.ds(b, 1), :, :].rearrange("a (s p) n -> (a p) s n", p=P), h2[:, :, :]).then_inc(M["h2_out"], 16)

            load_patches(0)
            for dst, src in ((gammaB[:, :], gamma.rearrange("(a n) -> a n", a=1).broadcast_to([P, E])),
                             (ident[:, :], ident_d),
                             (baB[:, :], ba.rearrange("(a n) -> a n", a=1).broadcast_to([P, H])),
                             (wa_sb[:, :, :], wa.rearrange("(k p) n -> p k n", p=P))):
                sp.dma_start(dst, src).then_inc(M["c_in"], 16)
            for i, w in enumerate(W_ATT):
                if i >= 3:
                    sp.wait_ge(M["ws_lo"], i - 2)
                sp.dma_start(stage_w[i % 3].rearrange("p (k n) -> p k n", k=EC if i < 4 else NP),
                             w.rearrange("(k p) n -> p k n", p=P)).then_inc(M[f"ws_in{i % 3}"], 16)
            load_patches(1)
            store_h(0)
            load_patches(2)
            store_h(1)
            load_h(0)
            with sp.Fori(1, B - 2) as b:
                load_patches(b + 2)
                store_h(b + 1)
                store_h2(b - 1)
                load_h(b)
            store_h(B - 1)
            for b in range(B - 2, B):
                store_h2(b - 1)
                load_h(b)

            def load_w1(e, par):
                sp.dma_start(w1_f[par].rearrange("p (k n) -> p k n", k=EC),
                             w1[bass.ds(e, 1), :, :].rearrange("a (k p) n -> (a p) k n", p=P)).then_inc(M[f"w1_in{par}"], 16)

            def load_b1(e, par):
                sp.dma_start(b1_sb[par][:, :], b1[bass.ds(e, 1), :, :].rearrange("a p k -> (a p) k")).then_inc(M[f"b_in{par}"], 16)

            def load_w2(e, par):
                sp.dma_start(w2_f[par].rearrange("p (k n) -> p k n", k=HC),
                             w2[bass.ds(e, 1), :, :].rearrange("a (k p) n -> (a p) k n", p=P)).then_inc(M[f"w2_in{par}"], 16)

            def load_b2(e, par):
                sp.dma_start(b2_sb[par][:, :], b2[bass.ds(e, 1), :].broadcast_to([P, E])).then_inc(M[f"b_in{par}"], 16)

            def load_rows(r, par):
                sp.dma_start(rows_f[par], lists_d[bass.ds(r, BLK), :].rearrange("(s p) n -> p s n", p=P)).then_inc(M[f"row_in{par}"], 16)

            sp.wait_ge(M["yf_done"], 2 * (B - 1))
            load_w1(0, 0)
            load_w2(0, 0)
            load_b1(0, 0)
            sp.wait_ge(M["silu_done"], NP * B)
            load_b2(0, 0)
            store_h2(B - 1)
            sp.dma_start(lists_d[X * CAP:X * CAP + BLK, :], pad_d).then_inc(M["pad_out"], 16)
            def pad_list(e):
                first = sp.value_load(padi[0:1, e:e + 1], min_val=e * CAP, max_val=e * CAP + T)
                sp.dma_start(lists_d[bass.ds(first, BLK), :], pad_d).then_inc(M["pad_out"], 16)

            sp.wait_ge(M["tb"], 2)
            pad_list(0)
            sp.wait_ge(M["pad_out"], 16 * 2)
            sp.wait_ge(M["scat"], 16 * NS * TOPK * B)
            sp.wait_ge(M["yl_done"], 2 * B)
            load_rows(0, 0)
            sp.wait_ge(M["tb"], 18)

            def load_block(i, par):
                e = sp.value_load(tab[0:1, bass.ds(i, 1)], min_val=0, max_val=X - 1)
                r = sp.value_load(tab[0:1, bass.ds(i + NT, 1)], min_val=0, max_val=X * CAP)
                sp.wait_ge(M["w1_lo"], WQ * (i - 1))
                load_w1(e, par)
                sp.wait_ge(M["w2_lo"], WQ * (i - 1))
                load_w2(e, par)
                if isinstance(i, int) and i == 1:
                    for other in range(1, X):
                        pad_list(other)
                    sp.wait_ge(M["pad_out"], 16 * (X + 1))
                sp.wait_ge(M["xe_ps"], EC * (i - 1))
                sp.wait_ge(M["wsel_done"], i - 1)
                load_rows(r, par)
                sp.wait_ge(M["gh_done"], HC * (i - 1))
                load_b1(e, par)
                sp.wait_ge(M["y_done"], YB * (i - 1))
                load_b2(e, par)

            def two_blocks(q):
                load_block(2 * q + 1, 1)
                load_block(2 * q + 2, 0)

            two_blocks(0)
            with sp.Fori(1, (NT - 1) // 2) as q:
                two_blocks(q)
            sp.wait_ge(M["added"], 16 * BS * NT)
            sp.wait_ge(M["h2_out"], 16 * B)

        @block.gpsimd
        def _(pool):
            pool.memset(mhalf[:, :], -0.5).then_inc(M["mh_done"], 1)
            pool.dma_start(sel_f, sel_d).then_inc(M["c_sel"], 16)
            pool.dma_start(mask_f, mask_d).then_inc(M["c_maskb"], 16)
            pool.dma_start(upper[:, :], upper_d).then_inc(M["c_sum"], 16)
            pool.dma_start(ones[:, :], ones_d).then_inc(M["c_sum"], 16)
            pool.wait_ge(M["c_sel"], 16)
            pool.tensor_copy(sel_r[:, :], sel_f).then_inc(M["c_selr"], 1)
            pool.wait_ge(M["c_maskb"], 16)
            pool.tensor_copy(maskb[:, :], mask_f).then_inc(M["c_selr"], 1)
            pool.wait_ge(M["c_in"], 64)
            pool.tensor_copy(identb[:, :], ident[:, :]).then_inc(M["c_selr"], 1)
            pool.wait_ge(M["mh_done"], 1)

            def rsqrt(v, given, made, n):
                pool.wait_ge(M[given], n)
                pool.tensor_tensor(v, v, mhalf[:, 0:v.shape[1]], ALU.pow).then_inc(M[made], 1)

            def scatter(b):
                for j in range(NS * TOPK):
                    if j == 0:
                        pool.wait_ge(M["tail_done"], 2 * (b + 1))
                        pool.wait_ge(M["wall_done"], b + 1)
                        pool.wait_ge(M["slot_done"], b + 1)
                        plain(pool)
                    pool.indirect_dma_start(out=lists_d[:, :], out_offset=bass.IndirectOffsetOnAxis(ap=slot[:, j:j + 1], axis=0),
                                            in_=xn2[:, j // TOPK, :], in_offset=None).then_inc(M["scat"], 16)

            def image(b, post, post2, nxt):
                if post:
                    rsqrt(gr[:, :], "gv_done", "gr_done", b)
                if nxt:
                    rsqrt(rs1[:, :, :].rearrange("p j s -> p (j s)"), "s1_ve", "s1_rs", b + 2)
                if post2:
                    scatter(b - 2)
                if post:
                    rsqrt(rs[:, :, 0], "b_ve", "b_rs", b)

            rsqrt(rs1[:, :, :].rearrange("p j s -> p (j s)"), "s1_ve", "s1_rs", 1)
            for dst, src in ((strict, strict_d), (half, half_d), (gnw, gn_w), (gnb, gn_b),
                             (wr_sb, w_router.rearrange("(k p) n -> p k n", p=P)), (iota8, iota_d), (number, number_d),
                             (iob, blk_d.broadcast_to(iob.shape)), (tri8, tri8_d.broadcast_to(tri8.shape)),
                             (til, til_d.broadcast_to(til.shape))):
                pool.dma_start(dst[tuple(slice(None) for _ in dst.shape)], src).then_inc(M["g_in"], 16)
            image(0, False, False, True)
            image(1, True, False, True)
            image(2, True, True, True)
            with pool.Fori(3, B - 1) as b:
                image(b, True, True, True)
            image(B - 1, True, True, False)
            rsqrt(gr[:, :], "gv_done", "gr_done", B)
            scatter(B - 2)
            rsqrt(rs[:, :, 0], "b_ve", "b_rs", B)
            scatter(B - 1)

            pool.wait_ge(M["h2_out"], 16 * B)

            def add_rows(i, par):
                pool.wait_ge(M["y_done"], YB * (i + 1))
                pool.wait_ge(M["wsel_done"], i + 1)
                plain(pool)
                for s in range(BS):
                    pool.tensor_scalar(yo[par][:, s, :], yo[par][:, s, :], wsel[par][:, s:s + 1], None, ALU.mult).then_inc(M["y_w"], 1)
                if not isinstance(i, int) or i > 0:
                    pool.wait_ge(M["added"], 16 * BS * i)
                pool.wait_ge(M["y_w"], BS * (i + 1))
                plain(pool)
                for s in range(BS):
                    pool.indirect_dma_start(out=out_rows, out_offset=bass.IndirectOffsetOnAxis(ap=tok[par][:, s:s + 1], axis=0),
                                            in_=yo[par][:, s, :], in_offset=None, compute_op=ALU.add,
                                            bounds_check=T - 1, oob_is_err=False).then_inc(M["added"], 16)

            def two_blocks(q):
                add_rows(2 * q, 0)
                add_rows(2 * q + 1, 1)

            two_blocks(0)
            with pool.Fori(1, (NT - 1) // 2) as q:
                two_blocks(q)
            add_rows(NT - 1, 0)

        @block.scalar
        def _(act):
            act.wait_ge(M["wt_in"], 32)
            act.activation(wt_sp[0][:, 0:KT, :], wt_f[:, 0:KT, :], ACT.Copy).then_inc(M["wt_hi"], 1)
            act.activation(wt_sp[0][0:KREM, KT, :], wt_f[0:KREM, KT, :], ACT.Copy).then_inc(M["wt_hi"], 1)

            def patches_hi(n):
                act.wait_ge(M["xt_in"], 32 * (n + 1))
                act.wait_ge(M["tok_ps"], n)
                act.activation(xt_sp[0][:, 0:KT, :], xt_f[:, 0:KT, :], ACT.Copy).then_inc(M["xt_hi"], 1)
                act.activation(xt_sp[0][0:KREM, KT, :], xt_f[0:KREM, KT, :], ACT.Copy).then_inc(M["xt_hi"], 1)

            def keep_xnT(n):
                act.wait_ge(M["s1_tps"], n + 1)
                act.wait_ge(M["xl_done"], n)
                act.activation(xs[:, :], bank[7][:, :], ACT.Copy).then_inc(M["s1_xnT"], 1)

            def softplus(n):
                act.wait_ge(M["s1_z"], n + 1)
                act.activation(za[:, :], zb[:, :], ACT.Abs).then_inc(M["sp_abs"], 1)
                act.wait_ge(M["sp_abs"], n + 1)
                act.activation(ze[:, :], za[:, :], ACT.Exp, scale=-1.0).then_inc(M["sp_e"], 1)
                act.wait_ge(M["sp_e"], n + 1)
                act.wait_ge(M["sp_la"], n)
                act.activation(zl[:, :], ze[:, :], ACT.Ln, bias=1.0).then_inc(M["sp_l"], 1)

            def xn_hi(n):
                act.wait_ge(M["s1_xnT"], n + 1)
                act.wait_ge(M["g_ps"], NP * n)
                act.activation(xn_sp[0][:, :, :].rearrange("p k n -> p (k n)"), xs[:, :], ACT.Copy).then_inc(M["xh_done"], 1)

            def scaled_h(n):
                act.wait_ge(M["s1_rs"], n + 1)
                act.wait_ge(M["s1_xn"], NS * (n + 1))
                for s in range(NS):
                    act.activation(h1[:, s, :], h1[:, s, :], ACT.Copy, scale=rs1[:, 0, s:s + 1]).then_inc(M["s1_h"], 1)

            def weight_hi(i):
                act.wait_ge(M[f"ws_in{i % 3}"], 16 * (i // 3 + 1))
                act.activation(w_parts[i][0].rearrange("p k n -> p (k n)"), stage_w[i % 3], ACT.Copy).then_inc(M["ws_hi"], 1)

            patches_hi(0)
            for i in range(3):
                weight_hi(i)
            scaled_h(0)
            keep_xnT(0)
            xn_hi(0)
            softplus(0)
            for i in range(3, 5):
                weight_hi(i)

            def tanh_qk(b, c):
                act.wait_ge(M["qk_ps"], NP * b + c + 1)
                act.wait_ge(M["silu_done"], NP * b + c)
                act.activation(tq[:, :], bank[0][:, :], ACT.Tanh, scale=0.5).then_inc(M["tq_done"], 1)

            def tanh_g(b, c, par):
                act.wait_ge(M["g_ps"], NP * b + c + 1)
                act.activation(tg[par][:, c, :], bank[1][:, 0:S], ACT.Tanh, scale=0.5).then_inc(M["tg_done"], 1)

            def decay(b, h):
                act.wait_ge(M["d_ps"], H * b + h + 1)
                act.wait_ge(M["mult_done"], H * b + max(h - 1, 0))
                act.activation(dec[h % 2][:, 0:S], bank[2 + h % 2][:, 0:S], ACT.Exp, bias=ncum[:, 0, h:h + 1])
                act.activation(dec[h % 2][:, S:LW], bank[2 + h % 2][:, S:LW], ACT.Exp, bias=ncum[:, 1, h:h + 1]).then_inc(M["exp_done"], 1)

            def keep_o(b, c, par):
                act.wait_ge(M["o_ps"], NP * b + c + 1)
                act.activation(osb[par][:, c, :], bank[6][:, 0:S], ACT.Copy).then_inc(M["o_done"], 1)

            def affined(pb, par, j):
                act.wait_ge(M["gn_step"], 6 * pb + 6)
                act.wait_ge(M["yl_done"], 2 * pb - 1 + j) if not isinstance(pb, int) or pb > 0 else None
                for c in range(PQ * j, PQ * j + PQ):
                    act.activation(yf[:, c, :], osb[par][:, c, :], ACT.Identity, scale=gsc[:, c:c + 1], bias=gbi[:, c:c + 1]).then_inc(M["yn_done"], 1)

            def y_hi(pb, j):
                act.wait_ge(M["yf_done"], 2 * pb + j + 1)
                act.wait_ge(M["wo_ps"], pb)
                act.activation(y_sp[0][:, PQ * j:PQ * j + PQ, :], yf[:, PQ * j:PQ * j + PQ, :], ACT.Copy).then_inc(M["yh_done"], 1)

            def keep_x2(pb):
                act.wait_ge(M["x2_ps"], pb + 1)
                act.wait_ge(M["lg_ps"], pb)
                act.activation(xn2T[:, :, :].rearrange("p k n -> p (k n)"), bank[7][:, :], ACT.Copy).then_inc(M["x2_done"], 1)

            def top_exp(pb):
                act.wait_ge(M["ntop_done"], pb + 1)
                act.wait_ge(M["wall_done"], pb)
                for s in range(NS):
                    act.activation(tope[:, s, :], top[:, s, :], ACT.Exp, bias=ntop[:, s, :],
                                   accum_out=tsum[:, s, :]).then_inc(M["tope_done"], 1)

            def image(b, par, post, post2, nxt):
                for i in range(2):
                    act.wait_ge(M["v_ps"], 4 * b + i + 1)
                    if i == 0:
                        act.wait_ge(M["o_ps"], NP * b)
                    act.activation(v_sb[:, 0, i * 512:(i + 1) * 512], bank[2 + i][:, :], ACT.Copy).then_inc(M["v_act"], 1)
                tanh_qk(b, 0)
                tanh_g(b, 0, par)
                act.wait_ge(M["ct_ps"], b + 1)
                act.activation(cumR[:, 0:S], bank[7][0:2 * H, 0:S], ACT.Copy)
                act.activation(cumR[:, S:LW], bank[7][0:2 * H, P:S], ACT.Copy).then_inc(M["ct_copied"], 1)
                for c in range(NP):
                    if nxt and c == 6:
                        keep_xnT(b + 1)
                    decay(b, 2 * c)
                    decay(b, 2 * c + 1)
                    if post2 and c == 0:
                        keep_x2(b - 2)
                    if nxt and c == 0:
                        patches_hi(b + 1)
                    if post and c in (2, 3):
                        affined(b - 1, 1 - par, c - 2)
                    if post and c in (4, 6):
                        y_hi(b - 1, c // 2 - 2)
                    if c == 5:
                        if nxt:
                            scaled_h(b + 1)
                        if post2:
                            top_exp(b - 2)
                    if nxt and c == 7:
                        xn_hi(b + 1)
                        softplus(b + 1)
                    if c + 1 < NP:
                        tanh_qk(b, c + 1)
                        tanh_g(b, c + 1, par)
                    keep_o(b, c, par)

            image(0, 0, False, False, True)
            image(1, 1, True, False, True)
            image(2, 0, True, True, True)
            image(3, 1, True, True, True)
            with act.Fori(2, B // 2 - 1) as p:
                image(2 * p, 0, True, True, True)
                image(2 * p + 1, 1, True, True, True)
            image(B - 2, 0, True, True, True)
            image(B - 1, 1, True, True, False)
            keep_x2(B - 2)
            affined(B - 1, 1, 0)
            affined(B - 1, 1, 1)
            y_hi(B - 1, 0)
            top_exp(B - 2)
            y_hi(B - 1, 1)

            def w_hi(name, parts, staged, par, n, used, count, q):
                if q == 0:
                    act.wait_ge(M[f"{name}_in{par}"], 16 * (n + 1))
                    act.wait_ge(M[used], count)
                cols = slice(q * 2048 // WQ, (q + 1) * 2048 // WQ)
                act.activation(parts[0].rearrange("p k n -> p (k n)")[:, cols], staged[par][:, cols], ACT.Copy).then_inc(M[f"{name}_hi"], 1)

            def x_hi(i, par):
                for k in range(EC):
                    act.wait_ge(M["xe_ps"], EC * i + k + 1)
                    if not isinstance(i, int) or i >= 2:
                        act.wait_ge(M["hid_ps"], HC * (i - 1))
                    act.activation(xe_sp[par][0][:, k, :], bank[k][:, 0:BLK], ACT.Copy).then_inc(M["xe_hi"], 1)

            def activated(i, par, n, c):
                act.wait_ge(M["hid_ps"], HC * i + c + 1)
                if c == 0:
                    act.wait_ge(M[f"b_in{par}"], 32 * (n + 1))
                act.wait_ge(M["gl_done"], HC * i + max(c - NGEL + 1, 0))
                act.activation(gel[c % NGEL], bank[2 + c % HB][:, 0:BLK], ACT.Gelu_apprx_tanh, bias=b1_sb[par][:, c:c + 1]).then_inc(M["gel_done"], 1)

            def hidden_hi(i, c):
                act.wait_ge(M["gel_done"], HC * i + c + 1)
                act.wait_ge(M["y_half" if c < HC // 2 else "y_ps"], i)
                act.activation(g_sp[0][:, c, :], gel[c % NGEL], ACT.Copy).then_inc(M["gh_done"], 1)

            def blockrow(i, par, n, last):
                activated(i, par, n, 0)
                for c in range(HC):
                    if c + 1 < HC:
                        activated(i, par, n, c + 1)
                    hidden_hi(i, c)
                    if c < WQ and not last:
                        w_hi("w1", w1_sp[1 - par], w1_f, 1 - par, n + par, "hid_ps", HC * i, c)
                    if c >= HC - WQ and not last:
                        w_hi("w2", w2_sp[1 - par], w2_f, 1 - par, n + par, "y_ps", i, c - (HC - WQ))
                    if c == 3 and not last:
                        x_hi(i + 1, 1 - par)

            for q in range(WQ):
                w_hi("w1", w1_sp[0], w1_f, 0, 0, "g_ps", NP * B, q)
            for q in range(WQ):
                w_hi("w2", w2_sp[0], w2_f, 0, 0, "g_ps", NP * B, q)
            keep_x2(B - 1)
            top_exp(B - 1)
            act.wait_ge(M["wo_ps"], B)
            x_hi(0, 0)

            def two_blocks(q):
                blockrow(2 * q, 0, q, False)
                blockrow(2 * q + 1, 1, q, False)

            two_blocks(0)
            with act.Fori(1, (NT - 1) // 2) as q:
                two_blocks(q)
            blockrow(NT - 1, 0, (NT - 1) // 2, True)

        @block.tensor
        def _(pe):
            pe.wait_ge(M["wt_lo"], 2)

            def tokens(n, free, count):
                if free:
                    pe.wait_ge(M[free], count)
                pe.wait_ge(M["xt_lo"], 2 * (n + 1))
                for s in range(NS):
                    for k in range(KT + 1):
                        rows = P if k < KT else KREM
                        for j, (wp, xp) in enumerate(three(wt_sp, xt_sp)):
                            mm = pe.matmul(bank[7][:, s * E:(s + 1) * E], xp[0:rows, k, s * P:(s + 1) * P], wp[0:rows, k, :],
                                           start=(s == 0 and k == 0 and j == 0), stop=(k == KT and j == 2), skip_group_check=True)
                mm.then_inc(M["tok_ps"], 1)

            def turn(n, free, count):
                pe.wait_ge(M[free], count)
                pe.wait_ge(M["s1_xn"], NS * (n + 1))
                for k in range(EC):
                    for s in range(NS):
                        mm = pe.transpose(bank[7][:, k * S + s * P:k * S + (s + 1) * P], xn1[:, s, k * P:(k + 1) * P], ident[:, :])
                mm.then_inc(M["s1_tps"], 1)

            def logits(n):
                pe.wait_ge(M["s1_xnT"], n + 1)
                for s in range(NS):
                    for k in range(EC):
                        mm = pe.matmul(bank[7][:, s * H:(s + 1) * H], xs[:, k * S + s * P:k * S + (s + 1) * P], wa_sb[:, k, :],
                                       start=(k == 0), stop=(k == EC - 1))
                mm.then_inc(M["s1_aps"], 1)

            tokens(0, None, 0)
            pe.wait_ge(M["c_in"], 64)
            turn(0, "s1_u", NS)
            logits(0)

            def cum(b):
                if not isinstance(b, int) or b > 1:
                    pe.wait_ge(M["h2_done"], b - 1)
                pe.wait_ge(M["sp_la"], b + 1)
                pe.matmul(bank[7][:, 0:H], upper[:, :], la[:, 0, :], start=True, stop=True)
                pe.matmul(bank[7][:, H:2 * H], ones[:, :], la[:, 0, :], start=True, stop=False)
                pe.matmul(bank[7][:, H:2 * H], upper[:, :], la[:, 1, :], start=False, stop=True).then_inc(M["cum_ps"], 1)

            def cum_rows(b):
                pe.wait_ge(M["ncum_done"], b + 1)
                for s in range(NS):
                    mm = pe.transpose(bank[7][0:2 * H, s * P:(s + 1) * P], ccs[:, s, :], ident[:, :])
                mm.then_inc(M["ct_ps"], 1)

            def values(b, s):
                pe.wait_ge(M["xl_done"], b + 1)
                for n in range(2):
                    i = 2 * s + n
                    pe.wait_ge(M["exp_done"] if s == 0 else M["mult_done"], H * b)
                    for k in range(EC):
                        for j, (wp, xp) in enumerate(three(wsp[2], xn_sp)):
                            mm = pe.matmul(bank[2 + i][:, :], xp[:, k, s * P:(s + 1) * P], wp[:, k, n * 512:(n + 1) * 512],
                                           start=(k == 0 and j == 0), stop=(k == EC - 1 and j == 2))
                    mm.then_inc(M["v_ps"], 1)

            def project(dst, w, c, m):
                for k in range(EC):
                    for j, (wp, xp) in enumerate(three(wsp[w], xn_sp)):
                        mm = pe.matmul(dst, wp[:, k, c * P:(c + 1) * P], xp[:, k, :],
                                       start=(k == 0 and j == 0), stop=(k == EC - 1 and j == 2))
                if m is not None:
                    mm.then_inc(M[m], 1)

            def qkg(b, c):
                if isinstance(b, int) and b == 0 and c == 0:
                    pe.wait_ge(M["ws_lo"], 4)
                pe.wait_ge(M["silu_done"], NP * b + c)
                project(bank[0][:, 0:S], 0, c, None)
                project(bank[0][:, S:2 * S], 1, c, "qk_ps")
                pe.wait_ge(M["tg_done"], NP * b + c)
                project(bank[1][:, 0:S], 3, c, "g_ps")

            def decays(b, h):
                if h < 2:
                    pe.wait_ge(M["v_act"], 2 * b + h + 1)
                pe.wait_ge(M["exp_done"], H * b + max(h - 1, 0))
                if h == 0:
                    pe.wait_ge(M["ct_copied"], b + 1)
                dst = bank[2 + h % 2]
                pe.matmul(dst[:, 0:LW], sel_r[:, h:h + 1].broadcast_to([2 * H, P]), cumR[:, :], start=True, stop=False)
                pe.matmul(dst[:, :].rearrange("p (a n) -> p a n", n=P)[:, 0:3:2, :], identb[:, :],
                          maskb[:, :].rearrange("p (a n) -> p a n", n=P), start=False, stop=True).then_inc(M["d_ps"], 1)

            def scores(b, c, h):
                if c == 0:
                    pe.wait_ge(M["v_dve"], 2 * b + h % 2 + 1)
                pe.wait_ge(M["mult_done"], H * b + max(h - 1, 0))
                pe.wait_ge(M["silu_done"], NP * b + c + 1)
                r = slice(D * (h % 2), D * (h % 2) + D)
                q, k = qk_s[c % 2][r, 0:S], qk_s[c % 2][r, S:2 * S]
                dst = bank[4 + h % 2]
                pe.matmul(dst[:, 0:S], k[:, 0:P], q, start=True, stop=True)
                pe.matmul(dst[:, S:LW], k[:, P:S], q[:, P:S], start=True, stop=True).then_inc(M["s_ps"], 1)

            def weighted(b, c):
                pe.wait_ge(M["o_done"], NP * b + c)
                for hh in range(2):
                    h = 2 * c + hh
                    pe.wait_ge(M["mult_done"], H * b + h + 1)
                    dst = bank[6][D * hh:D * hh + D, :]
                    pe.matmul(dst[:, 0:S], v_sb[:, 0, h * D:(h + 1) * D], att[hh][:, 0:S], start=True, stop=False)
                    mm = pe.matmul(dst[:, P:S], v_sb[:, 1, h * D:(h + 1) * D], att[hh][:, S:LW], start=False, stop=True)
                mm.then_inc(M["o_ps"], 1)

            def gn_mean(pb, free, count):
                pe.wait_ge(M[free], count)
                pe.wait_ge(M["gmv_done"], NP * (pb + 1))
                pe.matmul(bank[7][:, 0:NP], half[:, :], gmv[:, :, 0], start=True, stop=True).then_inc(M["gn1_ps"], 1)

            def gn_var(pb):
                pe.wait_ge(M["gt2_done"], pb + 1)
                pe.matmul(bank[7][:, 0:NP], half[:, :], gt[:, :], start=True, stop=True).then_inc(M["gn2_ps"], 1)

            def out_proj(pb, j, free, count):
                if j == 0:
                    pe.wait_ge(M[free], count)
                pe.wait_ge(M["yl_done"], 2 * pb + j + 1)
                for c in range(PQ * j, PQ * j + PQ):
                    for s in range(NS):
                        for q, (wp, yp) in enumerate(three(wo_sp, y_sp)):
                            mm = pe.matmul(bank[7][:, s * E:(s + 1) * E], yp[:, c, s * P:(s + 1) * P], wp[:, c, :],
                                           start=(c == 0 and s == 0 and q == 0), stop=(c == NP - 1 and q == 2),
                                           skip_group_check=True)
                if j == 1:
                    mm.then_inc(M["wo_ps"], 1)

            def turn2(pb, free, count):
                pe.wait_ge(M[free], count)
                pe.wait_ge(M["b_xn"], NS * (pb + 1))
                for k in range(EC):
                    for s in range(NS):
                        mm = pe.transpose(bank[7][:, k * S + s * P:k * S + (s + 1) * P], xn2[:, s, k * P:(k + 1) * P], ident[:, :])
                mm.then_inc(M["x2_ps"], 1)

            def route(pb, free, count):
                pe.wait_ge(M[free], count)
                pe.wait_ge(M["x2_done"], pb + 1)
                for s in range(NS):
                    for k in range(EC):
                        mm = pe.matmul(bank[7][:, s * X:(s + 1) * X], xn2T[:, k, s * P:(s + 1) * P], wr_sb[:, k, :],
                                       start=(k == 0), stop=(k == EC - 1))
                mm.then_inc(M["lg_ps"], 1)

            def ranks(pb, free, count):
                pe.wait_ge(M[free], count)
                pe.wait_ge(M["both_done"], pb + 1)
                pe.matmul(bank[7][:, 0:X], strict[:, :], both[:, 0, :], start=True, stop=True)
                pe.matmul(bank[7][:, X:2 * X], ones[:, :], both[:, 0, :], start=True, stop=False)
                pe.matmul(bank[7][:, X:2 * X], strict[:, :], both[:, 1, :], start=False, stop=True)
                pe.matmul(bank[7][:, 2 * X:3 * X], ones[:, :], both[:, 0, :], start=True, stop=False)
                pe.matmul(bank[7][:, 2 * X:3 * X], ones[:, :], both[:, 1, :], start=False, stop=True).then_inc(M["rk_ps"], 1)

            pe.wait_ge(M["c_sum"], 32)
            pe.wait_ge(M["c_selr"], 3)
            pe.wait_ge(M["ws_lo"], 1)

            def image(b, post, post2, nxt):
                values(b, 0)
                cum(b)
                qkg(b, 0)
                cum_rows(b)
                values(b, 1)
                for c in range(NP):
                    decays(b, 2 * c)
                    decays(b, 2 * c + 1)
                    if post2 and c == 0:
                        turn2(b - 2, "ct_copied", b + 1)
                    if post and c == 1:
                        gn_var(b - 1)
                    if nxt and c == 6:
                        logits(b + 1)
                    scores(b, c, 2 * c)
                    scores(b, c, 2 * c + 1)
                    if c + 1 < NP:
                        qkg(b, c + 1)
                    if post and c == 0:
                        gn_mean(b - 1, *(("x2_done", b - 1) if post2 else ("ct_copied", b + 1)))
                    if nxt and c == 1:
                        tokens(b + 1, *(("gv_done", b) if post else ("ct_copied", b + 1)))
                    if post2 and c == 3:
                        route(b - 2, *(("s1_u", NS * (b + 2)) if nxt else ("gv_done", b)))
                    if nxt and c == 5:
                        turn(b + 1, *(("lg_done", b - 1) if post2 else ("s1_u", NS * (b + 2))))
                    if post2 and c == 6:
                        ranks(b - 2, *(("s1_z", b + 2) if nxt else ("lg_done", b - 1)))
                    if post and c == 7:
                        out_proj(b - 1, 0, *(("taken_done", b - 1) if post2 else ("s1_z", b + 2)))
                        out_proj(b - 1, 1, None, 0)
                    weighted(b, c)

            image(0, False, False, True)
            pe.wait_ge(M["ws_lo"], 5)
            pe.wait_ge(M["g_in"], 16 * 10)
            image(1, True, False, True)
            image(2, True, True, True)
            image(3, True, True, True)
            with pe.Fori(2, B // 2 - 1) as p:
                image(2 * p, True, True, True)
                image(2 * p + 1, True, True, True)
            image(B - 2, True, True, True)
            image(B - 1, True, True, False)
            gn_mean(B - 1, "h2_done", B - 1)
            gn_var(B - 1)
            turn2(B - 2, "gv_done", B)
            route(B - 2, "x2_done", B - 1)
            ranks(B - 2, "lg_done", B - 1)
            out_proj(B - 1, 0, "taken_done", B - 1)
            out_proj(B - 1, 1, None, 0)
            turn2(B - 1, "h2_done", B)
            route(B - 1, "x2_done", B)
            ranks(B - 1, "lg_done", B)

            def turn_rows(i, par, n):
                pe.wait_ge(M[f"row_in{par}"], 16 * (n + 1))
                pe.wait_ge(M["xe_lo"], EC * i)
                for k in range(EC):
                    for s in range(BS):
                        mm = pe.transpose(bank[k][:, s * P:(s + 1) * P], rows_f[par][:, s, k * P:(k + 1) * P], ident[:, :])
                    mm.then_inc(M["xe_ps"], 1)

            def layer1(i, par, chunks):
                if chunks[0] == 0:
                    pe.wait_ge(M["xe_lo"], EC * (i + 1))
                    pe.wait_ge(M["w1_lo"], WQ * (i + 1))
                for c in chunks:
                    done = HC * i + c - HB + 1
                    if not isinstance(done, int) or done > 0:
                        pe.wait_ge(M["gel_done"], done)
                    for k in range(EC):
                        for j, (wp, xp) in enumerate(three(w1_sp[par], xe_sp[par])):
                            mm = pe.matmul(bank[2 + c % HB][:, 0:BLK], wp[:, k, c * P:(c + 1) * P], xp[:, k, :],
                                           start=(k == 0 and j == 0), stop=(k == EC - 1 and j == 2))
                    mm.then_inc(M["hid_ps"], 1)

            def layer2(i, par, chunks):
                if chunks[0] == 0:
                    pe.wait_ge(M["w2_lo"], WQ * (i + 1))
                    pe.wait_ge(M["y_done"], YB * i)
                for c in chunks:
                    pe.wait_ge(M["gl_done"], HC * i + c + 1)
                    for s in range(BS):
                        for j, (wp, gp) in enumerate(three(w2_sp[par], g_sp)):
                            mm = pe.matmul(bank[6 + s // 2][:, (s % 2) * E:(s % 2 + 1) * E], gp[:, c, s * P:(s + 1) * P], wp[:, c, :],
                                           start=(c == 0 and s % 2 == 0 and j == 0), stop=(c == HC - 1 and j == 2),
                                           skip_group_check=True)
                mm.then_inc(M["y_half" if c < HC - 1 else "y_ps"], 1)

            first, second = range(HC // 2), range(HC // 2, HC)
            turn_rows(0, 0, 0)
            layer1(0, 0, first)

            def two_blocks(q):
                for par in range(2):
                    layer1(2 * q + par, par, second)
                    turn_rows(2 * q + par + 1, 1 - par, q + par)
                    layer2(2 * q + par, par, first)
                    layer1(2 * q + par + 1, 1 - par, first)
                    layer2(2 * q + par, par, second)

            two_blocks(0)
            with pe.Fori(1, (NT - 1) // 2) as q:
                two_blocks(q)
            layer1(NT - 1, 0, second)
            layer2(NT - 1, 0, first)
            layer2(NT - 1, 0, second)

        @block.vector
        def _(dve):
            dve.wait_ge(M["wt_hi"], 2)
            dve.wait_ge(M["wt_in"], 32)
            dve.tensor_tensor(wt_sp[1][:, 0:KT, :], wt_f[:, 0:KT, :], f32(wt_sp[0][:, 0:KT, :]), ALU.subtract).then_inc(M["wt_lo"], 1)
            dve.tensor_tensor(wt_sp[1][0:KREM, KT, :], wt_f[0:KREM, KT, :], f32(wt_sp[0][0:KREM, KT, :]), ALU.subtract).then_inc(M["wt_lo"], 1)

            def patches_lo(n):
                dve.wait_ge(M["xt_hi"], 2 * (n + 1))
                dve.wait_ge(M["xt_in"], 32 * (n + 1))
                hi, lo = xt_sp
                dve.tensor_tensor(lo[:, 0:KT, :], xt_f[:, 0:KT, :], f32(hi[:, 0:KT, :]), ALU.subtract).then_inc(M["xt_lo"], 1)
                dve.tensor_tensor(lo[0:KREM, KT, :], xt_f[0:KREM, KT, :], f32(hi[0:KREM, KT, :]), ALU.subtract).then_inc(M["xt_lo"], 1)

            def moments(parts, st_, mv_, sems, n):
                for s in range(NS):
                    dve.bn_stats(st_[:, s, :], parts[s]).then_inc(M[sems[0]], 1)
                dve.wait_ge(M[sems[0]], NS * (n + 1))
                plain(dve)
                for s in range(NS):
                    dve.bn_aggr(mv_[:, s, :], st_[:, s, :]).then_inc(M[sems[1]], 1)
                dve.wait_ge(M[sems[1]], NS * (n + 1))

            def embed(n):
                dve.wait_ge(M["tok_ps"], n + 1)
                dve.wait_ge(M["h_out"], 16 * n)
                tok = [bank[7][:, s * E:(s + 1) * E] for s in range(NS)]
                moments(tok, st1, mv1, ("s1_st", "s1_mv"), n)
                for s in range(NS):
                    dve.scalar_tensor_tensor(out=h1[:, s, :], in0=tok[s], scalar=mv1[:, s, 0:1], in1=gammaB[:, :],
                                             op0=ALU.subtract, op1=ALU.mult).then_inc(M["s1_u"], 1)
                dve.tensor_scalar(rs1[:, 0, :], mv1[:, :, 1], EPS, None, ALU.add).then_inc(M["s1_v1"], 1)

            def embed_moments(n):
                dve.wait_ge(M["s1_u"], NS * (n + 1))
                moments([h1[:, s, :] for s in range(NS)], st1u, mv1u, ("s1_st2", "s1_mv2"), n)
                dve.wait_ge(M["s1_v1"], n + 1)
                dve.scalar_tensor_tensor(out=rs1[:, 1, :], in0=rs1[:, 0, :], scalar=EPS, in1=mv1u[:, :, 1],
                                         op0=ALU.mult, op1=ALU.add).then_inc(M["s1_ve"], 1)

            def embed_norm(n):
                dve.wait_ge(M["s1_rs"], n + 1)
                dve.wait_ge(M["s1_tps"], n)
                for s in range(NS):
                    dve.tensor_scalar(xn1[:, s, :], h1[:, s, :], mv1u[:, s, 0:1], rs1[:, 1, s:s + 1],
                                      ALU.subtract, ALU.mult).then_inc(M["s1_xn"], 1)

            def decay_logits(n):
                dve.wait_ge(M["s1_aps"], n + 1)
                dve.wait_ge(M["sp_abs"], n)
                dve.tensor_tensor(zb[:, :].rearrange("p (s n) -> p s n", s=NS), bank[7][:, 0:NS * H].rearrange("p (s n) -> p s n", s=NS),
                                  baB[:, :].rearrange("p (a n) -> p a n", a=1).broadcast_to([P, NS, H]), ALU.add).then_inc(M["s1_z"], 1)
                dve.wait_ge(M["s1_z"], n + 1)
                dve.tensor_scalar(zm[:, :], zb[:, :], 0.0, None, ALU.max).then_inc(M["sp_m"], 1)

            def log_decay(n):
                dve.wait_ge(M["sp_l"], n + 1)
                dve.wait_ge(M["sp_m"], n + 1)
                dve.wait_ge(M["cum_ps"], n)
                dve.scalar_tensor_tensor(out=la[:, :, :].rearrange("p t n -> p (t n)"), in0=zm[:, :], scalar=-1.0,
                                         in1=zl[:, :], op0=ALU.mult, op1=ALU.subtract).then_inc(M["sp_la"], 1)

            def xn_lo(n):
                dve.wait_ge(M["xh_done"], n + 1)
                dve.tensor_tensor(xn_sp[1][:, :, :].rearrange("p k n -> p (k n)"), xs[:, :],
                                  f32(xn_sp[0][:, :, :].rearrange("p k n -> p (k n)")), ALU.subtract).then_inc(M["xl_done"], 1)

            def weight_lo(i):
                dve.wait_ge(M["ws_hi"], i + 1)
                dve.tensor_tensor(w_parts[i][1].rearrange("p k n -> p (k n)"), stage_w[i % 3],
                                  f32(w_parts[i][0].rearrange("p k n -> p (k n)")), ALU.subtract).then_inc(M["ws_lo"], 1)

            patches_lo(0)
            dve.wait_ge(M["c_in"], 64)
            embed(0)
            embed_moments(0)
            weight_lo(0)
            embed_norm(0)
            weight_lo(1)
            decay_logits(0)
            xn_lo(0)
            weight_lo(2)
            log_decay(0)
            for i in range(3, 5):
                weight_lo(i)

            def silu(b, c):
                dve.wait_ge(M["tq_done"], NP * b + c + 1)
                dve.wait_ge(M["s_ps"], H * b + max(2 * c - 2, 0))
                dve.scalar_tensor_tensor(out=qk_s[c % 2][:, :], in0=tq[:, :], scalar=1.0, in1=bank[0][:, :],
                                         op0=ALU.add, op1=ALU.mult).then_inc(M["silu_done"], 1)

            def decayed(b, c, h):
                dve.wait_ge(M["s_ps"], H * b + h + 1)
                dve.wait_ge(M["exp_done"], H * b + h + 1)
                dve.wait_ge(M["o_ps"], NP * b + c)
                dve.tensor_tensor(att[h % 2][:, :], bank[4 + h % 2][:, 0:LW], dec[h % 2][:, :], ALU.mult).then_inc(M["mult_done"], 1)

            def head_stats(b, c, par):
                dve.wait_ge(M["o_done"], NP * b + c + 1)
                dve.wait_ge(M["gmv_done"], NP * b + c)
                dve.bn_stats(gst[:, :], osb[par][:, c, :]).then_inc(M["gst_done"], 1)
                dve.wait_ge(M["gst_done"], NP * b + c + 1)
                if c == 0 and not (isinstance(b, int) and b == 0):
                    dve.wait_ge(M["gt2_done"], b)
                plain(dve)
                dve.bn_aggr(gmv[:, c, :], gst[:, :]).then_inc(M["gmv_done"], 1)

            def spread(pb):
                dve.wait_ge(M["gn1_ps"], pb + 1)
                dve.tensor_copy(gm[:, :], bank[7][:, 0:NP]).then_inc(M["gn_step"], 1)
                dve.wait_ge(M["gn_step"], 6 * pb + 1)
                dve.wait_ge(M["gmv_done"], NP * (pb + 1))
                dve.tensor_tensor(gd[:, :], gmv[:, :, 0], gm[:, :], ALU.subtract).then_inc(M["gn_step"], 1)
                dve.wait_ge(M["gn_step"], 6 * pb + 2)
                dve.wait_ge(M["gn2_ps"], pb)
                dve.tensor_tensor(gt[:, :], gd[:, :], gd[:, :], ALU.mult).then_inc(M["gn_step"], 1)
                dve.wait_ge(M["gn_step"], 6 * pb + 3)
                dve.tensor_tensor(gt[:, :], gt[:, :], gmv[:, :, 1], ALU.add).then_inc(M["gt2_done"], 1)

            def affine(pb):
                dve.wait_ge(M["gn2_ps"], pb + 1)
                dve.tensor_scalar(gr[:, :], bank[7][:, 0:NP], 16 * EPS, None, ALU.add).then_inc(M["gv_done"], 1)

            def affine_steps(pb):
                dve.wait_ge(M["gr_done"], pb + 1)
                dve.tensor_tensor(gsc[:, :], gr[:, :], gnwh[:, :], ALU.mult).then_inc(M["gn_step"], 1)
                dve.wait_ge(M["gn_step"], 6 * pb + 4)
                dve.tensor_tensor(gd[:, :], gm[:, :], gsc[:, :], ALU.mult).then_inc(M["gn_step"], 1)
                dve.wait_ge(M["gn_step"], 6 * pb + 5)
                dve.tensor_tensor(gbi[:, :], gnbh[:, :], gd[:, :], ALU.subtract).then_inc(M["gn_step"], 1)

            def gated(pb, par, j):
                dve.wait_ge(M["yn_done"], NP * pb + PQ * (j + 1))
                dve.wait_ge(M["tg_done"], NP * (pb + 1))
                cs = slice(PQ * j, PQ * j + PQ)
                dve.scalar_tensor_tensor(out=yf[:, cs, :], in0=tg[par][:, cs, :], scalar=1.0, in1=yf[:, cs, :],
                                         op0=ALU.add, op1=ALU.mult).then_inc(M["yf_done"], 1)

            def y_lo(pb, j):
                cs = slice(PQ * j, PQ * j + PQ)
                dve.wait_ge(M["yh_done"], 2 * pb + j + 1)
                dve.tensor_tensor(y_sp[1][:, cs, :], yf[:, cs, :], f32(y_sp[0][:, cs, :]), ALU.subtract).then_inc(M["yl_done"], 1)

            def residual(pb):
                dve.wait_ge(M["wo_ps"], pb + 1)
                dve.wait_ge(M["hb_in"], 16 * (pb + 1))
                dve.wait_ge(M["h2_out"], 16 * pb)
                dve.tensor_tensor(h2[:, :, :].rearrange("p s n -> p (s n)"), bank[7][:, :], hb[:, :], ALU.add).then_inc(M["h2_done"], 1)
                dve.wait_ge(M["h2_done"], pb + 1)
                moments([h2[:, s, :] for s in range(NS)], st, mv, ("b_st", "b_mv"), pb)
                dve.tensor_scalar(rs[:, :, 0], mv[:, :, 1], EPS, None, ALU.add).then_inc(M["b_ve"], 1)

            def normed(pb):
                dve.wait_ge(M["b_rs"], pb + 1)
                dve.wait_ge(M["scat"], 16 * NS * TOPK * pb)
                for s in range(NS):
                    dve.tensor_scalar(xn2[:, s, 0:E], h2[:, s, :], mv[:, s, 0:1], rs[:, s, :], ALU.subtract, ALU.mult).then_inc(M["b_xn"], 1)

            def keep_logits(pb):
                dve.wait_ge(M["lg_ps"], pb + 1)
                dve.tensor_copy(lg[:, :, :].rearrange("p s n -> p (s n)"), bank[7][:, 0:NS * X]).then_inc(M["lg_done"], 1)

            def choose(pb):
                dve.wait_ge(M["lg_done"], pb + 1)
                plain(dve)
                for s in range(NS):
                    dve.max(top[:, s, :], lg[:, s, :]).then_inc(M["top_done"], 1)
                dve.wait_ge(M["top_done"], NS * (pb + 1))
                dve.tensor_scalar(ntop[:, :, 0], top[:, :, 0], -1.0, None, ALU.mult).then_inc(M["ntop_done"], 1)
                for s in range(NS):
                    dve.max_index(topi[:, s, :], top[:, s, :], lg[:, s, :]).then_inc(M["topi_done"], 1)
                dve.wait_ge(M["topi_done"], NS * (pb + 1))
                dve.tensor_copy(idxf[:, :, :], topi[:, :, 0:TOPK]).then_inc(M["idxf_done"], 1)
                dve.tensor_copy(xn2[:, :, EX:EX + TOPK], topi[:, :, 0:TOPK]).then_inc(M["tail_done"], 1)
                dve.tensor_copy(xn2[:, :, NUM], number[:, bass.ds(NS * pb, NS)]).then_inc(M["tail_done"], 1)
                dve.wait_ge(M["idxf_done"], pb + 1)
                for s in range(NS):
                    for k in range(TOPK):
                        dve.tensor_scalar(pick[:, s, k, :], iota8[:, :], idxf[:, s, k:k + 1], None, ALU.is_equal).then_inc(M["pick_done"], 1)
                dve.wait_ge(M["pick_done"], NS * TOPK * (pb + 1))
                dve.tensor_tensor(both[:, :, :], pick[:, :, 0, :], pick[:, :, 1, :], ALU.add).then_inc(M["both_done"], 1)

            def weigh(pb):
                dve.wait_ge(M["tope_done"], NS * (pb + 1))
                dve.reciprocal(trec[:, :, 0], tsum[:, :, 0]).then_inc(M["trec_done"], 1)
                dve.wait_ge(M["trec_done"], pb + 1)
                dve.tensor_tensor(xn2[:, :, WT:WT + TOPK], tope[:, :, 0:TOPK], trec[:, :, :].broadcast_to([P, NS, TOPK]), ALU.mult).then_inc(M["wall_done"], 1)

            def keep_ranks(pb):
                dve.wait_ge(M["rk_ps"], pb + 1)
                dve.wait_ge(M["taken_done"], pb)
                dve.tensor_tensor(rank[:, :, :], bank[7][:, 0:NS * X].rearrange("p (s n) -> p s n", s=NS),
                                  taken[:, :].rearrange("p (a n) -> p a n", a=1).broadcast_to([P, NS, X]), ALU.add).then_inc(M["rank_done"], 1)
                dve.wait_ge(M["rank_done"], pb + 1)
                dve.tensor_tensor(taken[:, :], bank[7][:, 2 * X:3 * X], taken[:, :], ALU.add).then_inc(M["taken_done"], 1)

            def place(pb):
                for s in range(NS):
                    for k in range(TOPK):
                        j = TOPK * s + k
                        dve.wait_ge(M["rsel_done"], NS * TOPK * pb + j)
                        dve.tensor_tensor_reduce(junk[:, :], rank[:, s, :], pick[:, s, k, :], 1.0, 0.0, ALU.mult, ALU.add,
                                                 rsel[:, j:j + 1]).then_inc(M["rsel_done"], 1)
                dve.wait_ge(M["rsel_done"], NS * TOPK * (pb + 1))
                dve.wait_ge(M["scat"], 16 * NS * TOPK * pb)
                dve.scalar_tensor_tensor(out=slot[:, :], in0=idxf[:, :, :].rearrange("p s k -> p (s k)"), scalar=float(CAP), in1=rsel[:, :],
                                         op0=ALU.mult, op1=ALU.add).then_inc(M["slot_done"], 1)

            def running_sums(b):
                dve.wait_ge(M["cum_ps"], b + 1)
                dve.wait_ge(M["ct_ps"], b)
                cps = bank[7][:, 0:NS * H].rearrange("p (s n) -> p s n", s=NS)
                dve.tensor_copy(ccs[:, :, 0:H].bitcast(F32R), cps).then_inc(M["cc_hi"], 1)
                dve.wait_ge(M["cc_hi"], b + 1)
                dve.tensor_tensor(ccs[:, :, H:2 * H], cps, ccs[:, :, 0:H], ALU.subtract).then_inc(M["cc_lo"], 1)
                dve.wait_ge(M["exp_done"], H * b)
                dve.tensor_scalar(ncum[:, :, :], cps, -1.0, None, ALU.mult).then_inc(M["ncum_done"], 1)

            def w_lo(name, parts, staged, par, i, q):
                dve.wait_ge(M[f"{name}_hi"], WQ * i + q + 1)
                cols = slice(q * 2048 // WQ, (q + 1) * 2048 // WQ)
                hi, lo = (part.rearrange("p k n -> p (k n)")[:, cols] for part in parts)
                dve.tensor_tensor(lo, staged[par][:, cols], f32(hi), ALU.subtract).then_inc(M[f"{name}_lo"], 1)

            def image(b, par, post, post2, nxt):
                if post:
                    head_stats(b - 1, NP - 1, 1 - par)
                if post2:
                    normed(b - 2)
                running_sums(b)
                silu(b, 0)
                for i in range(2):
                    dve.wait_ge(M["v_ps"], 4 * b + 3 + i)
                    if i == 0:
                        dve.wait_ge(M["o_ps"], NP * b)
                    dve.tensor_copy(v_sb[:, 1, i * 512:(i + 1) * 512], bank[4 + i][:, :]).then_inc(M["v_dve"], 1)
                for c in range(NP):
                    if post and c == 1:
                        affine(b - 1)
                    if nxt and c == 7:
                        xn_lo(b + 1)
                    decayed(b, c, 2 * c)
                    decayed(b, c, 2 * c + 1)
                    if nxt and c == 6:
                        decay_logits(b + 1)
                    if c + 1 < NP:
                        silu(b, c + 1)
                    if c >= 1:
                        head_stats(b, c - 1, par)
                    if c == 0:
                        if post:
                            spread(b - 1)
                        if nxt:
                            patches_lo(b + 1)
                    if post and c == 1:
                        affine_steps(b - 1)
                    if nxt and c == 2:
                        embed(b + 1)
                    if c == 3:
                        if nxt:
                            embed_moments(b + 1)
                        if post:
                            gated(b - 1, 1 - par, 0)
                    if c == 4:
                        if post2:
                            keep_logits(b - 2)
                        if nxt:
                            embed_norm(b + 1)
                        if post2:
                            choose(b - 2)
                    if post and c == 5:
                        gated(b - 1, 1 - par, 1)
                        y_lo(b - 1, 0)
                    if c == 6:
                        if post:
                            y_lo(b - 1, 1)
                        if post2:
                            weigh(b - 2)
                            keep_ranks(b - 2)
                            place(b - 2)
                    if c == 7:
                        if post:
                            residual(b - 1)
                        if nxt:
                            log_decay(b + 1)

            dve.memset(taken[:, :], 0.0).then_inc(M["gnh"], 1)
            image(0, 0, False, False, True)
            dve.wait_ge(M["g_in"], 16 * 10)
            dve.tensor_scalar(gnwh[:, :], gnw[:, :], 0.5, None, ALU.mult).then_inc(M["gnh"], 1)
            dve.tensor_scalar(gnbh[:, :], gnb[:, :], 0.5, None, ALU.mult).then_inc(M["gnh"], 1)
            dve.wait_ge(M["gnh"], 3)
            image(1, 1, True, False, True)
            image(2, 0, True, True, True)
            image(3, 1, True, True, True)
            with dve.Fori(2, B // 2 - 1) as p:
                image(2 * p, 0, True, True, True)
                image(2 * p + 1, 1, True, True, True)
            image(B - 2, 0, True, True, True)
            image(B - 1, 1, True, True, False)
            head_stats(B - 1, NP - 1, 1)
            spread(B - 1)
            normed(B - 2)
            affine(B - 1)
            affine_steps(B - 1)
            keep_logits(B - 2)
            gated(B - 1, 1, 0)
            choose(B - 2)
            gated(B - 1, 1, 1)
            y_lo(B - 1, 0)
            keep_ranks(B - 2)
            y_lo(B - 1, 1)
            weigh(B - 2)
            place(B - 2)
            residual(B - 1)
            normed(B - 1)
            for q in range(WQ):
                w_lo("w1", w1_sp[0], w1_f, 0, 0, q)
            keep_logits(B - 1)
            choose(B - 1)
            keep_ranks(B - 1)
            weigh(B - 1)
            place(B - 1)

            tbc = [0]

            def tb(ins):
                tbc[0] += 1
                ins.then_inc(M["tb"], 1)
                dve.wait_ge(M["tb"], tbc[0])

            cnt = taken[:, :]
            dve.wait_ge(M["taken_done"], B)
            tb(dve.scalar_tensor_tensor(out=padf[:, :], in0=iota8[:, :], scalar=float(CAP), in1=cnt, op0=ALU.mult, op1=ALU.add))
            tb(dve.tensor_copy(padi[:, :], padf[:, :]))
            tb(dve.tensor_tensor(below[:, :, :], cnt.rearrange("p (n a) -> p n a", a=1).broadcast_to([P, X, NBLK]),
                                 iob[:, :].rearrange("p (n a) -> p n a", a=NBLK), ALU.is_gt))
            tb(dve.tensor_reduce(nb[:, :], below[:, :, :], AX.X, ALU.add))
            tb(dve.tensor_tensor(tmp64[:, :, :], nb[:, :].rearrange("p (a n) -> p a n", a=1).broadcast_to([P, X, X]),
                                 tri8[:, :].rearrange("p (a n) -> p a n", a=X), ALU.mult))
            tb(dve.tensor_reduce(cb[:, :], tmp64[:, :, :], AX.X, ALU.add))
            tb(dve.tensor_tensor(cmp[:, :, :], cb[:, :].rearrange("p (a n) -> p a n", a=1).broadcast_to([P, NT, X]),
                                 til[:, :].rearrange("p (a n) -> p a n", a=NT), ALU.is_le))
            tb(dve.tensor_tensor(cmn[:, :, :], cmp[:, :, :], nb[:, :].rearrange("p (a n) -> p a n", a=1).broadcast_to([P, NT, X]), ALU.mult))
            tb(dve.tensor_reduce(te[:, :], cmp[:, :, :], AX.X, ALU.add))
            tb(dve.tensor_reduce(tst[:, :], cmn[:, :, :], AX.X, ALU.add))
            tiles = til[:, :].rearrange("p (a n) -> p a n", a=NT)[:, :, 0]
            tb(dve.tensor_scalar(tva[:, :], te[:, :], float(X), None, ALU.is_lt))
            tb(dve.tensor_tensor(tr0[:, :], tiles, tst[:, :], ALU.subtract))
            tb(dve.tensor_tensor(tr0[:, :], tr0[:, :], tva[:, :], ALU.mult))
            tb(dve.tensor_scalar(tr0[:, :], tr0[:, :], float(BLK), None, ALU.mult))
            tb(dve.scalar_tensor_tensor(out=tr0[:, :], in0=te[:, :], scalar=float(CAP), in1=tr0[:, :], op0=ALU.mult, op1=ALU.add))
            tb(dve.tensor_tensor(te[:, :], te[:, :], tva[:, :], ALU.mult))
            tb(dve.tensor_copy(tab[:, 0:NT], te[:, :]))
            tb(dve.tensor_copy(tab[:, NT:2 * NT], tr0[:, :]))

            def x_lo(i, par):
                for k in range(EC):
                    dve.wait_ge(M["xe_hi"], EC * i + k + 1)
                    dve.tensor_tensor(xe_sp[par][1][:, k, :], bank[k][:, 0:BLK], f32(xe_sp[par][0][:, k, :]), ALU.subtract).then_inc(M["xe_lo"], 1)

            def row_tails(i, par, n):
                dve.wait_ge(M[f"row_in{par}"], 16 * (n + 1))
                if not isinstance(i, int) or i >= 2:
                    dve.wait_ge(M["added"], 16 * BS * (i - 1))
                dve.tensor_copy(ecol[par][:, :], te[:, bass.ds(i, 1)]).then_inc(M["ecol_done"], 1)
                dve.tensor_copy(tok[par][:, :], rows_f[par][:, :, NUM]).then_inc(M["ecol_done"], 1)
                dve.wait_ge(M["ecol_done"], 2 * (i + 1))
                for k in range(TOPK):
                    dve.scalar_tensor_tensor(out=wpart[TOPK * par + k][:, :], in0=rows_f[par][:, :, EX + k], scalar=ecol[par][:, :],
                                             in1=rows_f[par][:, :, WT + k], op0=ALU.is_equal, op1=ALU.mult).then_inc(M["wk_done"], 1)
                dve.wait_ge(M["wk_done"], TOPK * (i + 1))
                dve.tensor_tensor(wsel[par][:, :], wpart[TOPK * par][:, :], wpart[TOPK * par + 1][:, :], ALU.add).then_inc(M["wsel_done"], 1)

            def hidden_lo(i, c):
                dve.wait_ge(M["gh_done"], HC * i + c + 1)
                dve.tensor_tensor(g_sp[1][:, c, :], gel[c % NGEL], f32(g_sp[0][:, c, :]), ALU.subtract).then_inc(M["gl_done"], 1)

            def keep_y(i, par):
                dve.wait_ge(M["y_ps"], i + 1)
                if not isinstance(i, int) or i >= 2:
                    dve.wait_ge(M["added"], 16 * BS * (i - 1))
                for m in range(YB):
                    n = min(2, BS - 2 * m)
                    dve.tensor_tensor(yo[par][:, 2 * m:2 * m + n, :], bank[6 + m][:, 0:n * E].rearrange("p (s n) -> p s n", s=n),
                                      b2_sb[par][:, :].rearrange("p (a n) -> p a n", a=1).broadcast_to([P, n, E]), ALU.add).then_inc(M["y_done"], 1)

            def blockrow(i, par, n, last):
                for c in range(HC):
                    hidden_lo(i, c)
                    if c < WQ and not last:
                        w_lo("w1", w1_sp[1 - par], w1_f, 1 - par, i + 1, c)
                    if c >= HC - WQ and not last:
                        w_lo("w2", w2_sp[1 - par], w2_f, 1 - par, i + 1, c - (HC - WQ))
                    if c == 2 and not (isinstance(i, int) and i == 0):
                        keep_y(i - 1, 1 - par)
                    if c == 3 and not last:
                        x_lo(i + 1, 1 - par)
                    if c == 4:
                        row_tails(i, par, n)

            for q in range(WQ):
                w_lo("w2", w2_sp[0], w2_f, 0, 0, q)
            x_lo(0, 0)

            def two_blocks(q):
                blockrow(2 * q, 0, q, False)
                blockrow(2 * q + 1, 1, q, False)

            two_blocks(0)
            two_blocks(1)
            with dve.Fori(2, (NT - 1) // 2) as q:
                two_blocks(q)
            blockrow(NT - 1, 0, (NT - 1) // 2, True)
            keep_y(NT - 1, 0)


_INS = ['x', 'L0_tok_W', 'L0_tok_gamma', 'L0_attn_Wq', 'L0_attn_Wk', 'L0_attn_Wv', 'L0_attn_Wg', 'L0_attn_Wa',
        'L0_attn_ba', 'L0_attn_Wo', 'L0_attn_gn_w', 'L0_attn_gn_b', 'L0_ffn_w_router', 'L0_ffn_w1', 'L0_ffn_b1',
        'L0_ffn_w2', 'L0_ffn_b2']


def constants():
    i = np.arange(P)
    before = np.where(i[:, None] <= i[None, :], 0.0, -1e30)
    n = np.arange(X)
    return {
        "c_ident": np.eye(P, dtype=np.float32),
        "c_upper": (i[:, None] <= i[None, :]).astype(np.float32),
        "c_ones": np.ones((P, P), np.float32),
        "c_strict": (i[:, None] < i[None, :]).astype(np.float32),
        "c_half": ((i[:, None] // D == i[None, :] // D) / D).astype(np.float32),
        "c_sel": np.tile(np.eye(H, dtype=np.float32), (2, 1)),
        "c_mask": np.tile(before, (1, 2)).astype(np.float32),
        "c_iota": np.tile(n.astype(np.float32), (P, 1)),
        "c_blk": np.tile(np.where(np.arange(NBLK) > 0, np.arange(NBLK) * BLK, -1).astype(np.float32), (1, X)).reshape(1, X * NBLK),
        "c_tri8": (n[None, :] <= n[:, None]).astype(np.float32).reshape(1, X * X),
        "c_til": np.repeat(np.arange(NT, dtype=np.float32), X).reshape(1, NT * X),
        "c_number": (i[:, None] + P * np.arange(B * NS)[None, :]).astype(np.float32),
        "c_pad": np.where(np.arange(EW)[None, :] == NUM, T, 0).astype(np.float32).repeat(BLK, 0),
    }


def laid_out(inputs):
    a = {n: np.asarray(inputs[n]) for n in _INS}
    side = SIDE // PATCH
    a['x'] = a['x'].reshape(B, C, side, PATCH, side, PATCH).transpose(1, 3, 5, 0, 2, 4).reshape(FEAT, T)
    a['L0_attn_gn_w'] = a['L0_attn_gn_w'].reshape(NP, P).T
    a['L0_attn_gn_b'] = a['L0_attn_gn_b'].reshape(NP, P).T
    a['L0_ffn_b1'] = a['L0_ffn_b1'].reshape(X, HC, P).transpose(0, 2, 1)
    return {n: np.ascontiguousarray(v) for n, v in a.items()}


def kernel(**inputs):
    import concourse.bacc as _bacc
    from concourse.bass_utils import run_bass_kernel_spmd as _run

    nc = _bacc.Bacc("TRN2", target_bir_lowering=False, num_devices=1)
    arrays, args = {}, []
    for name, a in {**laid_out(inputs), **constants()}.items():
        arrays[f"in_{name}"] = a
        args.append(nc.dram_tensor(f"in_{name}", a.shape, mybir.dt.from_np(a.dtype), kind="ExternalInput").ap())
    out = nc.dram_tensor("out_0", (B, S, E), F32, kind="ExternalOutput").ap()
    vit_layer(nc, *args, out)
    r = _run(nc, [arrays], core_ids=[0])
    return r.results[0]["out_0"]
```
